# Optimizing a Trainium2 kernel written in Bass

```python
import numpy as np
import jax
import jax.numpy as jnp

def _softmax(x, axis=-1):
    return jax.nn.softmax(x, axis=axis)

def _gelu(x):
    return jax.nn.gelu(x, approximate=True)

def _silu(x):
    return jax.nn.silu(x)

def _sigmoid(x):
    return jax.nn.sigmoid(x)

def _layernorm(x, axis=-1, eps=1e-05):
    m = jnp.mean(x, axis=axis, keepdims=True)
    v = jnp.var(x, axis=axis, keepdims=True)
    return (x - m) / jnp.sqrt(v + eps)

def _scatter_add(tgt, idx, src, axis=0):
    return tgt.at[idx].add(src)

def _segment_sum(src, seg, n):
    return jax.ops.segment_sum(src, seg, n)
kernel_name = 'mk_decoder_postln_d1_seqx_r8_d06e15'

def setup_inputs(seed: int=0):
    np.random.seed(seed)
    _w = jnp.asarray

    def _rec_inputs():
        import jax
        import jax.numpy as jnp
        _rk = jax.random.key(seed)
        x = 0.002226 + 0.9996 * jax.random.normal(jax.random.fold_in(_rk, 1), (4, 512, 128), jnp.float32)
        _lenS = 512 - jax.random.randint(jax.random.fold_in(_rk, 7), (4,), 0, max(1, 512 // 4) + 1, jnp.int32)
        _lenS2 = 154 - jax.random.randint(jax.random.fold_in(_rk, 8), (4,), 0, max(1, 154 // 4) + 1, jnp.int32)
        _ctx_1024P = jax.random.normal(jax.random.fold_in(_rk, 11), (4, 16, 128), jnp.float32)
        _ctx_1024c = jax.random.dirichlet(jax.random.fold_in(_rk, 511), 0.3 * jnp.ones((16,), jnp.float32), (4, 154))
        _ctx_1024t = jnp.einsum('bsk,bkd->bsd', _ctx_1024c, _ctx_1024P)
        _ctx_1024t = _ctx_1024t * jax.lax.rsqrt(jnp.mean(jnp.square(_ctx_1024t)) + 1e-12) * 0.953939
        ctx_1024 = -0.000125008 + 0.999885 * (_ctx_1024t + 0.3 * jax.random.normal(jax.random.fold_in(_rk, 611), (4, 154, 128), jnp.float32))
        return (x, ctx_1024)
    x, ctx_1024 = _rec_inputs()

    def _L0_attn_setup():
        import jax, jax.numpy as jnp
        import numpy as np
        D_MODEL, N_HEADS, N_KV, HEAD_DIM, D_LAT = (128, 8, 2, 128, 32)
        N_REP = N_HEADS // N_KV
        B, T = (2, 256)
        key = jax.random.key(seed)
        ks = jax.random.split(key, 8)
        s = lambda fan_in: 1.0 / np.sqrt(fan_in)
        return {'x': jax.random.normal(ks[0], (B, T, D_MODEL), jnp.float32), 'wq': jax.random.normal(ks[1], (D_MODEL, N_HEADS * HEAD_DIM), jnp.float32) * s(D_MODEL), 'wk_down': jax.random.normal(ks[2], (D_MODEL, N_KV * D_LAT), jnp.float32) * s(D_MODEL), 'wv_down': jax.random.normal(ks[3], (D_MODEL, N_KV * D_LAT), jnp.float32) * s(D_MODEL), 'wk_up': jax.random.normal(ks[4], (D_LAT, HEAD_DIM), jnp.float32) * s(D_LAT), 'wv_up': jax.random.normal(ks[5], (D_LAT, HEAD_DIM), jnp.float32) * s(D_LAT), 'wo': jax.random.normal(ks[6], (N_HEADS * HEAD_DIM, D_MODEL), jnp.float32) * s(N_HEADS * HEAD_DIM)}
    _L0_attn_all = _L0_attn_setup()
    _L0_attn_in = {k: v for k, v in _L0_attn_all.items() if k in ('wq', 'wk_down', 'wv_down', 'wk_up', 'wv_up', 'wo')}
    del _L0_attn_all

    def _L0_xattn_setup():
        import jax, jax.numpy as jnp
        import numpy as np
        EPS = 1e-05

        def layer_norm(x, g, b):
            mu = jnp.mean(x, axis=-1, keepdims=True)
            var = jnp.var(x, axis=-1, keepdims=True)
            return (x - mu) * jax.lax.rsqrt(var + EPS) * g + b
        key = jax.random.key(seed)
        ks = jax.random.split(key, 8)
        dim, heads, dim_head = (128, 16, 64)
        inner = heads * dim_head
        b, n, m = (8, 512, 64)
        s = dim ** (-0.5)
        return {'x': jax.random.normal(ks[0], (b, n, dim), jnp.float32), 'latents': jax.random.normal(ks[1], (b, m, dim), jnp.float32), 'ln_m_g': jnp.ones((dim,), jnp.float32), 'ln_m_b': jnp.zeros((dim,), jnp.float32), 'ln_l_g': jnp.ones((dim,), jnp.float32), 'ln_l_b': jnp.zeros((dim,), jnp.float32), 'Wq': jax.random.normal(ks[2], (dim, inner), jnp.float32) * s, 'Wkv': jax.random.normal(ks[3], (dim, 2 * inner), jnp.float32) * s, 'Wout': jax.random.normal(ks[4], (inner, dim), jnp.float32) * s}
    _L0_xattn_all = _L0_xattn_setup()
    _L0_xattn_in = {k: v for k, v in _L0_xattn_all.items() if k in ('ln_m_g', 'ln_m_b', 'ln_l_g', 'ln_l_b', 'Wq', 'Wkv', 'Wout')}
    del _L0_xattn_all

    def _L0_ffn_setup():
        import jax, jax.numpy as jnp
        import numpy as np
        import math
        N_EXP = 8
        TOP_K = 2
        CAPACITY_FACTOR = 1.25

        def _capacity(num_tokens):
            cap = math.floor(TOP_K * CAPACITY_FACTOR * num_tokens / N_EXP)
            cap += cap % 2
            return int(cap)
        key = jax.random.key(seed)
        k1, k2, k3, k4 = jax.random.split(key, 4)
        B, C, d = (4, 128, 128)
        x = jax.random.normal(k1, (B, C, d), dtype=jnp.float32)
        w_g = jax.random.normal(k2, (d, N_EXP), dtype=jnp.float32) * 0.02
        c_fc = jax.random.normal(k3, (N_EXP, d, 4 * d), dtype=jnp.float32) * 0.02
        c_proj = jax.random.normal(k4, (N_EXP, 4 * d, d), dtype=jnp.float32) * 0.02
        return {'x': x, 'w_g': w_g, 'c_fc': c_fc, 'c_proj': c_proj}
    _L0_ffn_all = _L0_ffn_setup()
    _L0_ffn_in = {k: v for k, v in _L0_ffn_all.items() if k in ('w_g', 'c_fc', 'c_proj')}
    del _L0_ffn_all
    return {'x': x, 'ctx_1024': ctx_1024, 'L0_attn_wq': _L0_attn_in['wq'], 'L0_attn_wk_down': _L0_attn_in['wk_down'], 'L0_attn_wv_down': _L0_attn_in['wv_down'], 'L0_attn_wk_up': _L0_attn_in['wk_up'], 'L0_attn_wv_up': _L0_attn_in['wv_up'], 'L0_attn_wo': _L0_attn_in['wo'], 'L0_xattn_ln_m_g': _L0_xattn_in['ln_m_g'], 'L0_xattn_ln_m_b': _L0_xattn_in['ln_m_b'], 'L0_xattn_ln_l_g': _L0_xattn_in['ln_l_g'], 'L0_xattn_ln_l_b': _L0_xattn_in['ln_l_b'], 'L0_xattn_Wq': _L0_xattn_in['Wq'], 'L0_xattn_Wkv': _L0_xattn_in['Wkv'], 'L0_xattn_Wout': _L0_xattn_in['Wout'], 'L0_ffn_w_g': _L0_ffn_in['w_g'], 'L0_ffn_c_fc': _L0_ffn_in['c_fc'], 'L0_ffn_c_proj': _L0_ffn_in['c_proj']}

def reference(x, ctx_1024, L0_attn_wq, L0_attn_wk_down, L0_attn_wv_down, L0_attn_wk_up, L0_attn_wv_up, L0_attn_wo, L0_xattn_ln_m_g, L0_xattn_ln_m_b, L0_xattn_ln_l_g, L0_xattn_ln_l_b, L0_xattn_Wq, L0_xattn_Wkv, L0_xattn_Wout, L0_ffn_w_g, L0_ffn_c_fc, L0_ffn_c_proj):
    import jax
    import jax.numpy as jnp

    def _L0_attn_ref(x, wq, wk_down, wv_down, wk_up, wv_up, wo):
        import jax, jax.numpy as jnp
        import numpy as np
        D_MODEL, N_HEADS, N_KV, HEAD_DIM, D_LAT = (128, 8, 2, 128, 32)
        N_REP = N_HEADS // N_KV
        B, T = (2, 256)
        Bq, Tq, _ = x.shape
        scale = HEAD_DIM ** (-0.5)
        q = (x @ wq).reshape(Bq, Tq, N_KV, N_REP, HEAD_DIM)
        k_lat = (x @ wk_down).reshape(Bq, Tq, N_KV, D_LAT)
        v_lat = (x @ wv_down).reshape(Bq, Tq, N_KV, D_LAT)
        k = jnp.einsum('bkhl,ld->bkhd', k_lat, wk_up)
        v = jnp.einsum('bkhl,ld->bkhd', v_lat, wv_up)
        scores = jnp.einsum('bqhrd,bkhd->bhrqk', q, k) * scale
        causal = jnp.tril(jnp.ones((Tq, Tq), dtype=bool))
        scores = jnp.where(causal, scores, jnp.finfo(scores.dtype).min)
        probs = jax.nn.softmax(scores, axis=-1)
        y = jnp.einsum('bhrqk,bkhd->bqhrd', probs, v)
        y = y.reshape(Bq, Tq, N_HEADS * HEAD_DIM)
        return y @ wo

    def _L0_xattn_ref(x, latents, ln_m_g, ln_m_b, ln_l_g, ln_l_b, Wq, Wkv, Wout):
        import jax, jax.numpy as jnp
        import numpy as np
        EPS = 1e-05

        def layer_norm(x, g, b):
            mu = jnp.mean(x, axis=-1, keepdims=True)
            var = jnp.var(x, axis=-1, keepdims=True)
            return (x - mu) * jax.lax.rsqrt(var + EPS) * g + b
        heads, dim_head = (16, 64)
        scale = dim_head ** (-0.5)
        x = layer_norm(x, ln_m_g, ln_m_b)
        lat = layer_norm(latents, ln_l_g, ln_l_b)
        b, m, _ = lat.shape
        q = lat @ Wq
        kv_input = jnp.concatenate([x, lat], axis=1)
        kv = kv_input @ Wkv
        k, v = jnp.split(kv, 2, axis=-1)

        def split_heads(t):
            return t.reshape(t.shape[0], t.shape[1], heads, dim_head).transpose(0, 2, 1, 3)
        q, k, v = (split_heads(q), split_heads(k), split_heads(v))
        dots = jnp.einsum('bhid,bhjd->bhij', q, k) * scale
        attn = jax.nn.softmax(dots, axis=-1)
        out = jnp.einsum('bhij,bhjd->bhid', attn, v)
        out = out.transpose(0, 2, 1, 3).reshape(b, m, heads * dim_head)
        return out @ Wout

    def _L0_ffn_ref(x, w_g, c_fc, c_proj):
        import jax, jax.numpy as jnp
        import numpy as np
        import math
        N_EXP = 8
        TOP_K = 2
        CAPACITY_FACTOR = 1.25

        def _capacity(num_tokens):
            cap = math.floor(TOP_K * CAPACITY_FACTOR * num_tokens / N_EXP)
            cap += cap % 2
            return int(cap)
        B, C, d = x.shape
        T = B * C
        cap = _capacity(T)
        xt = x.reshape(T, d)
        logits = xt @ w_g
        top_v, top_i = jax.lax.top_k(logits, TOP_K)
        full = jnp.full_like(logits, -jnp.inf)
        full = full.at[jnp.arange(T)[:, None], top_i].set(top_v)
        probs = jax.nn.softmax(full, axis=-1)
        exp_mask = jax.nn.one_hot(top_i, N_EXP, dtype=jnp.int32)
        exp_mask = jnp.transpose(exp_mask, (1, 0, 2))
        exp_rank = jnp.cumsum(exp_mask.reshape(TOP_K * T, N_EXP), axis=0) - 1
        exp_rank = exp_rank.reshape(TOP_K, T, N_EXP)
        exp_mask = exp_mask * (exp_rank < cap).astype(jnp.int32)
        exp_rank = jnp.sum(exp_mask * exp_rank, axis=-1)
        exp_weights = exp_mask.astype(x.dtype) * probs[None]
        rank_oh = jax.nn.one_hot(exp_rank, cap, dtype=x.dtype)
        cb_weight = jnp.einsum('kte,ktc->tec', exp_weights, rank_oh)
        sec_mask = (cb_weight != 0).astype(x.dtype)
        exp_batches = jnp.einsum('tec,td->ecd', sec_mask, xt)
        h = jax.nn.gelu(jnp.einsum('ecd,edf->ecf', exp_batches, c_fc), approximate=False)
        exp_out = jnp.einsum('ecf,efd->ecd', h, c_proj)
        out = cb_weight.reshape(T, N_EXP * cap) @ exp_out.reshape(N_EXP * cap, d)
        return out.reshape(B, C, d)
    x = _layernorm(x + _L0_attn_ref(x, L0_attn_wq, L0_attn_wk_down, L0_attn_wv_down, L0_attn_wk_up, L0_attn_wv_up, L0_attn_wo), axis=-1)
    x = _layernorm(x + _L0_xattn_ref(ctx_1024, x, L0_xattn_ln_m_g, L0_xattn_ln_m_b, L0_xattn_ln_l_g, L0_xattn_ln_l_b, L0_xattn_Wq, L0_xattn_Wkv, L0_xattn_Wout), axis=-1)
    x = _layernorm(x + _L0_ffn_ref(x, L0_ffn_w_g, L0_ffn_c_fc, L0_ffn_c_proj), axis=-1)
    return x

_drawn_inputs = setup_inputs


def setup_inputs(seed=0):
    import zlib

    import numpy as np

    out = dict(_drawn_inputs(seed))
    spreads = {'L0_xattn_ln_m_g': (1.0, 0.2),
     'L0_xattn_ln_m_b': (0.0, 0.1),
     'L0_xattn_ln_l_g': (1.0, 0.2),
     'L0_xattn_ln_l_b': (0.0, 0.1)}
    factors = {}
    for name, (base, spread) in spreads.items():
        noise = np.random.default_rng([zlib.crc32(name.encode()), seed]).standard_normal(out[name].shape)
        drawn = base * np.exp(spread * noise) if base else spread * noise
        out[name] = jnp.asarray(drawn.astype(out[name].dtype))
    for name, factor in factors.items():
        out[name] = (out[name] * factor).astype(out[name].dtype)
    return out
```

```python
from contextlib import ExitStack

import concourse.bass as bass
from concourse import mybir

ALU = mybir.AluOpType
ACT = mybir.ActivationFunctionType
AX_X = mybir.AxisListType.X
F32 = mybir.dt.float32
F32R = mybir.dt.float32r
BF16 = mybir.dt.bfloat16
U32 = mybir.dt.uint32

P = 128
B = 4
T = 512
D = 128
NT = T // P
TILES = B * NT
EPS = 1e-5

HS, KVS, REP, DL = 8, 2, 4, 32
SELF_SCALE = float(D) ** -0.5
SHIFT_ROW = 3 * DL
SELF_N = [T - P * j for j in range(NT)]
SELF_AT = [sum(SELF_N[:j]) for j in range(NT)]
SELF_W = sum(SELF_N)
MASKED = -1.0e30

HX, DH = 16, 64
CROSS_SCALE = float(DH) ** -0.5
CTX = 154
CTX_TAIL = CTX - P
KEYS = T + CTX
KEYS_E = KEYS + 2
HALF = KEYS_E // 2
KC = (KEYS + P - 1) // P
KPAD = KC * P
TAIL = KEYS - (KC - 1) * P
PAIRS = HX // 2
STEPS = B * PAIRS

E, FF = 8, 512
FC = FF // P
CAP = 640
SLOTS = E * CAP
ST = CAP // P
DROPPED = 8192.0

RING = 6
STEPS_SELF = 50
STEPS_CLOSE = 25
STEPS_COMBINE = 23


class Names:

    def __init__(self, names):
        self.names = names
        self.at = {n: k for k, n in enumerate(names)}
        self.n = len(names)

    def bank(self, name):
        return self.at[name] % RING

    def turn(self, name):
        return self.at[name] // RING

    def turns(self, bank):
        return (self.n - bank + RING - 1) // RING


def f(ap):
    return ap.bitcast(F32)


class Mem:

    def __init__(self, nc, ctx):
        self.nc, self.ctx = nc, ctx

    def sb(self, name, shape, dt=F32):
        return self.ctx.enter_context(self.nc.sbuf_tensor(name, shape, dt))

    def pb(self, name, shape):
        return self.ctx.enter_context(self.nc.psum_tensor(name, shape, F32))

    def sem(self, name):
        return self.ctx.enter_context(self.nc.semaphore(name))

    def split(self, name, shape):
        return self.sb(name + "_hi", shape, F32R), self.sb(name + "_lo", shape, F32R)


def setup_stage(nc, I, C):
    with ExitStack() as ctx:
        m = Mem(nc, ctx)
        wq = m.sb("wq", [P, HS * D])
        wkd = m.sb("wkd", [P, KVS * DL])
        wku = m.sb("wku", [DL, D])
        wvu = m.sb("wvu", [DL, D])
        wo = m.sb("wo", [P, HS, D])
        cq = m.sb("cq", [P, HX * DH])
        ckv = m.sb("ckv", [P, 2 * HX * DH])
        wqT = m.sb("wqT", [P, HS, P])
        upT = m.sb("upT", [P, 2, DL])
        stage_hi, stage_lo = m.split("stage", [P, 2, HX, DH])
        zero = m.sb("zero", [P, 8, P])
        pq = [m.pb(f"pq{k}", [P, 4, P]) for k in range(2)]
        pu = m.pb("pu", [P, 2, DL])
        pa = m.pb("pa", [P, HS, DL])
        pv = m.pb("pv", [P, KVS, D])
        loaded = m.sem("loaded")
        loaded_self = m.sem("loaded_self")
        consts = m.sem("consts")
        turned = m.sem("turned")
        copied = m.sem("copied")
        high = m.sem("high")
        low = m.sem("low")
        combined = m.sem("combined")
        stored = m.sem("stored")
        block = ctx.enter_context(nc.Block())

        @block.sync
        def _(sp):
            sp.dma_start(wq[:], I["wq"]).then_inc(loaded_self, 16)
            sp.dma_start(wku[:], I["wk_up"]).then_inc(loaded_self, 16)
            sp.dma_start(wvu[:], I["wv_up"]).then_inc(loaded_self, 16)
            sp.dma_start(wo[:], I["wo"].rearrange("(h p) n -> p h n", p=P)).then_inc(loaded_self, 16)
            sp.dma_start(wkd[:], I["wk_down"]).then_inc(loaded_self, 16)
            sp.dma_start(C["wvd"][:], I["wv_down"]).then_inc(loaded_self, 16)
            sp.dma_start(cq[:], I["Wq"]).then_inc(loaded, 16)
            sp.dma_start(ckv[:], I["Wkv"]).then_inc(loaded, 16)
            sp.dma_start(C["xall"][:], I["x"].rearrange("b (n p) d -> p (b n) d", p=P)).then_inc(loaded, 16)
            sp.dma_start(C["gb"][:, 0:1], I["ln_l_g"].rearrange("(p a) -> p a", a=1)).then_inc(loaded, 16)
            sp.dma_start(C["gb"][:, 1:2], I["ln_l_b"].rearrange("(p a) -> p a", a=1)).then_inc(loaded, 16)
            sp.dma_start(C["gb"][:, 2:3], I["ln_m_g"].rearrange("(p a) -> p a", a=1)).then_inc(loaded, 16)
            sp.dma_start(C["gb"][:, 3:4], I["ln_m_b"].rearrange("(p a) -> p a", a=1)).then_inc(loaded, 16)
            sp.dma_start(C["wg"][:], I["w_g"]).then_inc(loaded, 16)
            sp.wait_ge(consts, 1)
            for e in range(E):
                sp.dma_start(C["xslots"][e * CAP:(e + 1) * CAP, :].rearrange("(n p) d -> p n d", p=P),
                             zero[:, 0:ST, :]).then_inc(stored, 16)
            for b in range(B):
                sp.dma_start(C["vals"][b, :, TAIL:P, KC - 1, :].rearrange("s p c -> p s c"),
                             zero[0:P - TAIL, 0:PAIRS, :]).then_inc(stored, 16)
            sp.wait_ge(high, 2)
            sp.wait_ge(low, 2)
            for part, src in enumerate((stage_hi, stage_lo)):
                for kind in range(2):
                    for h in range(2):
                        for twice in range(2):
                            sp.dma_start(
                                f(C["wpair"][:, :, part, kind, h, twice, :]).rearrange("s p c -> p s c"),
                                f(src[:, kind, :, :]).rearrange("p (s h) c -> p s h c", h=2)[:, :, h, :],
                            ).then_inc(stored, 16)
            sp.wait_ge(loaded, 16 * 8)
            sp.wait_ge(stored, 16 * (E + B + 16))

        @block.gpsimd
        def _(pool):
            pool.memset(zero[:], 0.0).then_inc(consts, 1)
            pool.memset(C["ident"][:], 0.0).then_inc(consts, 1)
            pool.memset(C["mask"][:], 0.0).then_inc(consts, 1)
            pool.memset(C["maskT"][:], 0.0).then_inc(consts, 1)
            pool.memset(C["ones"][:], 1.0).then_inc(consts, 1)
            pool.memset(C["upper"][:], 0.0).then_inc(consts, 1)
            pool.memset(C["aq_hi"][:].bitcast(F32), 0.0).then_inc(consts, 1)
            pool.memset(C["aq_lo"][:].bitcast(F32), 0.0).then_inc(consts, 1)
            pool.memset(C["wk_hi"][:].bitcast(F32), 0.0).then_inc(consts, 1)
            pool.memset(C["wk_lo"][:].bitcast(F32), 0.0).then_inc(consts, 1)
            pool.wait_ge(consts, 10)
            pool.affine_select(out=C["ident"][:], in_=C["ident"][:], compare_op=ALU.not_equal, fill=1.0, base=0,
                               pattern=[[-1, P]], channel_multiplier=1).then_inc(consts, 1)
            pool.affine_select(out=C["mask"][:], in_=C["mask"][:], compare_op=ALU.is_ge, fill=MASKED, base=0,
                               pattern=[[-1, P]], channel_multiplier=1).then_inc(consts, 1)
            pool.affine_select(out=C["maskT"][:], in_=C["maskT"][:], compare_op=ALU.is_ge, fill=MASKED, base=0,
                               pattern=[[1, P]], channel_multiplier=-1).then_inc(consts, 1)
            pool.affine_select(out=C["upper"][:], in_=C["upper"][:], compare_op=ALU.is_ge, fill=1.0, base=0,
                               pattern=[[-1, P]], channel_multiplier=1).then_inc(consts, 1)
            pool.wait_ge(consts, 14)
            pool.tensor_copy(C["ident_b"][:], C["ident"][:]).then_inc(consts, 1)

        @block.tensor
        def _(pe):
            pe.wait_ge(consts, 14)
            pe.wait_ge(loaded_self, 16 * 6)
            for h in range(HS):
                t = pe.transpose(pq[h // 4][:, h % 4, :], wq[:, h * D:(h + 1) * D], C["ident"][:])
                if h % 4 == 3:
                    t.then_inc(turned, 1)
            pe.transpose(pu[:, 0, :], wku[:], C["ident"][0:DL, 0:DL])
            pe.transpose(pu[:, 1, :], wvu[:], C["ident"][0:DL, 0:DL]).then_inc(turned, 1)
            pe.wait_ge(copied, 3)
            for h in range(HS):
                t = pe.matmul(pa[:, h, :], wqT[:, h, :], upT[:, 0, :], start=True, stop=True)
            t.then_inc(combined, 1)
            for h in range(HS):
                t = pe.matmul(pv[DL * (h % REP):DL * (h % REP) + DL, h // REP, :], upT[:, 1, :], wo[:, h, :],
                              start=True, stop=True)
            t.then_inc(combined, 1)

        @block.vector
        def _(dve):
            for k in range(2):
                dve.wait_ge(turned, k + 1)
                dve.tensor_copy(wqT[:, 4 * k:4 * k + 4, :], pq[k][:]).then_inc(copied, 1)
            dve.wait_ge(turned, 3)
            dve.tensor_copy(upT[:], pu[:]).then_inc(copied, 1)
            dve.wait_ge(loaded, 16 * 8)
            for kind, src in enumerate((cq[:], ckv[:, 0:HX * DH])):
                dve.wait_ge(high, kind + 1)
                dve.tensor_tensor(stage_lo[:, kind, :, :], src.rearrange("p (h c) -> p h c", c=DH),
                                  f(stage_hi[:, kind, :, :]), ALU.subtract).then_inc(low, 1)
            dve.wait_ge(high, 3)
            dve.tensor_tensor(C["wv_lo"][:], ckv[:, HX * DH:], f(C["wv_hi"][:]), ALU.subtract).then_inc(low, 1)
            dve.wait_ge(combined, 1)
            dve.wait_ge(consts, 10)
            for c in range(3):
                dve.wait_ge(high, 6)
                dve.tensor_tensor(C["aq_lo"][:, :, c * DL:(c + 1) * DL], pa[:], f(C["aq_hi"][:, :, c * DL:(c + 1) * DL]),
                                  ALU.subtract).then_inc(low, 1)
            for c in range(3):
                dve.wait_ge(high, 7 + c)
                dve.tensor_tensor(C["wk_lo"][:, :, c * DL:(c + 1) * DL], wkd[:].rearrange("p (g l) -> p g l", l=DL),
                                  f(C["wk_hi"][:, :, c * DL:(c + 1) * DL]), ALU.subtract).then_inc(low, 1)
            dve.wait_ge(combined, 2)
            dve.tensor_copy(C["bo"][:], pv[:]).then_inc(low, 1)

        @block.scalar
        def _(act):
            act.wait_ge(loaded, 16 * 8)
            for kind, src in enumerate((cq[:], ckv[:, 0:HX * DH])):
                act.activation(stage_hi[:, kind, :, :], src.rearrange("p (h c) -> p h c", c=DH),
                               ACT.Copy).then_inc(high, 1)
            act.activation(C["wv_hi"][:], ckv[:, HX * DH:], ACT.Copy).then_inc(high, 1)
            act.wait_ge(combined, 1)
            act.wait_ge(consts, 10)
            for c in range(3):
                act.activation(C["aq_hi"][:, :, c * DL:(c + 1) * DL], pa[:], ACT.Copy).then_inc(high, 1)
            act.wait_ge(loaded_self, 16 * 6)
            for c in range(3):
                act.activation(C["wk_hi"][:, :, c * DL:(c + 1) * DL],
                               wkd[:].rearrange("p (g l) -> p g l", l=DL), ACT.Copy).then_inc(high, 1)


SELF_UNITS = Names(
    ["xT", "k0", "k1", "v", "q0", "q1", "ma0", "mb0", "mc0"]
    + [u for h in range(HS)
       for u in ([f"q{h + 2}"] if h + 2 < HS else []) + ([f"m{c}{h + 1}" for c in "abc"] if h + 1 < HS else [])
       + [f"t{h}"] + [f"s{h}_{j}" for j in range(NT)]]
    + ["y", "lT", "cT"] + [f"V{c}_{k}" for c in range(KC) for k in range(2)])


class Count:

    def __init__(self, sem, per, ahead=1):
        self.sem, self.per, self.ahead, self.n = sem, per, ahead, 0

    def credit(self, eng):
        eng.sem_inc(self.sem, self.per * self.ahead)

    def now(self, eng, i, k):
        eng.wait_ge(self.sem, (i + self.ahead) * self.per + k)

    def before(self, eng, i, k, turns=1):
        eng.wait_ge(self.sem, (i + self.ahead - turns) * self.per + k)

    def done(self, ins):
        self.n += 1
        ins.then_inc(self.sem, 1)

    def own(self, eng, i, at=None):
        eng.wait_ge(self.sem, (i + self.ahead) * self.per + self.n)
        if at is not None:
            eng.sem_inc(at, 1)


def norm_stats(dve, i, st, held, tiles, stats, mv, ve):
    for k, t in enumerate(tiles):
        st.done(dve.bn_stats(stats[0:t.shape[0], k, :], t))
    st.own(dve, i, held)
    for k, t in enumerate(tiles):
        st.done(dve.bn_aggr(mv[0:t.shape[0], k, :], stats[0:t.shape[0], k, :]))
    st.own(dve, i)
    return dve.tensor_scalar(ve, mv[:, 0:len(tiles), 1], EPS, None, ALU.add)


def norm_root(act, i, root, k, ve, r0):
    act.activation(r0, ve, ACT.Ln).then_inc(root.sem, 1)
    root.now(act, i, 2 * k + 1)
    act.activation(r0, r0, ACT.Exp, scale=-0.5).then_inc(root.sem, 1)


def norm_apply(dve, i, st, tiles, outs, mv, ve, r0, r1):
    st.done(dve.tensor_tensor(r1, r0, r0, ALU.mult))
    st.own(dve, i)
    st.done(dve.tensor_tensor(r1, r1, ve, ALU.mult))
    st.own(dve, i)
    st.done(dve.tensor_scalar(r1, r1, -0.5, 1.5, ALU.mult, ALU.add))
    st.own(dve, i)
    st.done(dve.tensor_tensor(r1, r1, r0, ALU.mult))
    st.own(dve, i)
    last = None
    for k, (t, o) in enumerate(zip(tiles, outs)):
        if last is not None:
            st.done(last)
        n = t.shape[0]
        last = dve.tensor_scalar(o, t, mv[0:n, k, 0:1], r1[0:n, k:k + 1], ALU.subtract, ALU.mult)
    return last


def self_stage(nc, I, C):
    U = SELF_UNITS
    with ExitStack() as ctx:
        m = Mem(nc, ctx)
        xs = m.sb("xs", [P, NT, D])
        cs = m.sb("cs", [P, 2, D])
        xT = m.sb("xT", [P, T])
        xT_hi, xT_lo = m.split("xTs", [P, T])
        kop = m.sb("kop", [P, KVS, T], F32R)
        qop = m.sb("qop", [P, 4, T], F32R)
        vlat = m.sb("vlat", [P, NT, KVS * DL])
        nmax = m.sb("nmax", [P, 2, NT, P])
        probs = m.sb("probs", [P, HS, SELF_W])
        rden = m.sb("rden", [P, T])
        oT = m.sb("oT", [P, KVS, T])
        y = m.sb("y", [P, NT, D])
        x1 = m.sb("x1", [P, NT, D])
        lat = m.sb("lat", [P, NT, D])
        cn = m.sb("cn", [P, 2, D])
        stats = m.sb("stats", [P, 3, NT, 6])
        mv = m.sb("mv", [P, 3, NT, 2])
        ve = m.sb("ve", [P, 3, NT])
        r0 = m.sb("r0", [P, 3, NT])
        r1 = m.sb("r1", [P, 3, NT])
        kvf = m.sb("kvf", [P, KEYS_E])
        kvT_hi, kvT_lo = m.split("kvT", [P, KPAD])
        vout = m.sb("vout", [P, 2, HX * DH])
        ring = [m.pb(f"ring{k}", [P, T]) for k in range(RING)]
        o_ps = m.pb("o_ps", [P, T])
        den_ps = m.pb("den_ps", [P, T])

        x_in = m.sem("x_in")
        c_in = m.sem("c_in")
        zeroed = m.sem("zeroed")
        unit = Count(m.sem("unit"), U.n)
        high = Count(m.sem("high"), 3 + HS)
        low = Count(m.sem("low"), 3 + HS)
        xT_done = Count(m.sem("xT_done"), 1)
        vlat_done = Count(m.sem("vlat_done"), 1)
        max_done = Count(m.sem("max_done"), 3 * HS)
        row_done = Count(m.sem("row_done"), HS)
        probs_done = Count(m.sem("probs_done"), NT * HS)
        o_done = Count(m.sem("o_done"), KVS)
        oT_done = Count(m.sem("oT_done"), KVS)
        y_done = Count(m.sem("y_done"), 1)
        var_done = Count(m.sem("var_done"), 3)
        root_done = Count(m.sem("root_done"), 6)
        step = Count(m.sem("step"), STEPS_SELF)
        held = m.sem("held")
        x1_done = Count(m.sem("x1_done"), 1)
        x1_kept = Count(m.sem("x1_kept"), 16)
        lat_done = Count(m.sem("lat_done"), 1)
        cn_done = Count(m.sem("cn_done"), 1)
        kv_full = Count(m.sem("kv_full"), 2)
        kv_high = Count(m.sem("kv_high"), 2)
        kv_low = Count(m.sem("kv_low"), 2)
        kv_kept = Count(m.sem("kv_kept"), 32)
        v_act = Count(m.sem("v_act"), KC)
        v_dve = Count(m.sem("v_dve"), KC)
        v_kept = [Count(m.sem(f"v_kept{k}"), 8 * KC) for k in range(2)]
        block = ctx.enter_context(nc.Block())

        readers = {"xT": (xT_done, 1), "k0": (low, 2), "k1": (low, 3), "v": (vlat_done, 1), "y": (y_done, 1),
                   "lT": (kv_full, 1), "cT": (kv_full, 2)}
        for h in range(HS):
            readers[f"q{h}"] = (low, 4 + h)
            readers[f"t{h}"] = (row_done, 1 + h)
            for k, c in enumerate("abc"):
                readers[f"m{c}{h}"] = (max_done, 3 * h + k + 1)
            for j in range(NT):
                readers[f"s{h}_{j}"] = (probs_done, NT * h + j + 1)
        for c in range(KC):
            readers[f"V{c}_0"] = (v_act, c + 1)
            readers[f"V{c}_1"] = (v_dve, c + 1)

        def at_unit(eng, i, name):
            unit.now(eng, i, U.at[name] + 1)

        def ps(name):
            return ring[U.bank(name)]

        def vout_free(eng, i, c):
            kept = v_kept[c % 2]
            kept.now(eng, i, 16 * (c // 2)) if c >= 2 else kept.before(eng, i, 8 * KC)

        @block.gpsimd
        def _(pool):
            pool.memset(mv[:], 0.0).then_inc(zeroed, 1)
            pool.memset(nmax[:], 0.0).then_inc(zeroed, 1)
            pool.wait_ge(zeroed, 2)
            pool.memset(f(kop[SHIFT_ROW:P, :, :]), 0.0).then_inc(zeroed, 1)
            pool.wait_ge(zeroed, 3)
            pool.memset(f(kvT_hi[:, KEYS_E:KPAD]), 0.0).then_inc(zeroed, 1)
            pool.memset(f(kvT_lo[:, KEYS_E:KPAD]), 0.0).then_inc(zeroed, 1)
            pool.wait_ge(zeroed, 5)
            pool.memset(f(kop[SHIFT_ROW:SHIFT_ROW + 1, :, :]), 1.0).then_inc(zeroed, 1)

        @block.sync
        def _(sp):
            for c in (x1_kept, kv_kept, *v_kept):
                c.credit(sp)
            with sp.Fori(0, B) as i:
                unit.before(sp, i, U.at["xT"] + 1)
                sp.dma_start(xs[:], I["x"][bass.ds(i, 1), :, :].rearrange("b (n p) d -> p (b n) d", p=P)).then_inc(x_in, 16)
                cn_done.before(sp, i, 1)
                sp.dma_start(cs[:, 0, :], I["ctx"][bass.ds(i, 1), 0:P, :].rearrange("b p d -> p (b d)")).then_inc(c_in, 16)
                sp.dma_start(cs[0:CTX_TAIL, 1, :],
                             I["ctx"][bass.ds(i, 1), P:CTX, :].rearrange("b p d -> p (b d)")).then_inc(c_in, 16)
                x1_done.now(sp, i, 1)
                sp.dma_start(C["x1all"][:, bass.ds(i, 1), :, :], x1[:, None, :, :]).then_inc(x1_kept.sem, 16)
                kv_high.now(sp, i, 2)
                kv_low.now(sp, i, 2)
                sp.dma_start(f(C["kv_hi"][:, bass.ds(i, 1), :]), f(kvT_hi[:, None, 0:KEYS_E])).then_inc(kv_kept.sem, 16)
                sp.dma_start(f(C["kv_lo"][:, bass.ds(i, 1), :]), f(kvT_lo[:, None, 0:KEYS_E])).then_inc(kv_kept.sem, 16)
                for c in range(KC):
                    n = P if c < KC - 1 else TAIL
                    v_act.now(sp, i, c + 1)
                    v_dve.now(sp, i, c + 1)
                    sp.dma_start(C["vals"][bass.ds(i, 1), :, 0:n, c, :].rearrange("b s p c -> p (b s) c"),
                                 vout[0:n, c % 2, :].rearrange("p (s c) -> p s c", s=PAIRS)).then_inc(v_kept[c % 2].sem, 16)
            sp.wait_ge(x1_kept.sem, 16 * (B + 1))
            sp.wait_ge(kv_kept.sem, 32 * (B + 1))
            for c in v_kept:
                sp.wait_ge(c.sem, 8 * KC * (B + 1))

        @block.tensor
        def _(pe):
            for c in (unit, o_done):
                c.credit(pe)
            pe.wait_ge(zeroed, 6)
            with pe.Fori(0, B) as i:

                def begin(name):
                    k = U.at[name]
                    if k >= RING:
                        count, n = readers[U.names[k - RING]]
                        count.now(pe, i, n)
                    else:
                        last = max(x for x in range(U.n) if x % RING == k)
                        count, n = readers[U.names[last]]
                        count.before(pe, i, n)
                    return ps(name)

                def three(out, hi, lo, mhi, mlo):
                    pe.matmul(out, hi, mhi, start=True, stop=False)
                    pe.matmul(out, hi, mlo, start=False, stop=False)
                    return pe.matmul(out, lo, mhi, start=False, stop=True)

                def query(h):
                    unit.done(three(begin(f"q{h}")[:], C["aq_hi"][:, h, :], C["aq_lo"][:, h, :], xT_hi[:], xT_lo[:]))

                def max_scores(h):
                    g = h // REP
                    low.now(pe, i, 4 + h)
                    for name, tiles in (("ma", (0, 1)), ("mb", (2,)), ("mc", (3,))):
                        o = begin(f"{name}{h}")
                        for t in tiles:
                            n = max(256, P * (t + 1))
                            o0 = 256 * t if t < 2 else 0
                            pe.matmul(o[:, o0:o0 + n], qop[0:SHIFT_ROW, h % 4, t * P:(t + 1) * P],
                                      kop[0:SHIFT_ROW, g, 0:n], start=True, stop=False)
                            last = pe.matmul(o[:, o0 + t * P:o0 + (t + 1) * P], C["ident_b"][:], C["mask"][:],
                                             start=False, stop=True)
                        unit.done(last)

                def max_row(h):
                    max_done.now(pe, i, 3 * h + 3)
                    o = begin(f"t{h}")
                    for t in range(NT):
                        last = pe.transpose(o[:, t * P:(t + 1) * P], nmax[:, h % 2, t, :], C["ident"][:])
                    unit.done(last)

                def scores(h):
                    g = h // REP
                    row_done.now(pe, i, h + 1)
                    for j in range(NT):
                        o = begin(f"s{h}_{j}")
                        pe.matmul(o[:, 0:SELF_N[j]], kop[:, g, j * P:(j + 1) * P], qop[:, h % 4, j * P:T],
                                  start=True, stop=False)
                        unit.done(pe.matmul(o[:, 0:P], C["ident_b"][:], C["maskT"][:], start=False, stop=True))

                def values(g):
                    probs_done.now(pe, i, NT * REP * (g + 1))
                    vlat_done.now(pe, i, 1)
                    oT_done.now(pe, i, g) if g else oT_done.before(pe, i, KVS)
                    for o, first in ((o_ps, None), (den_ps, C["ones"][:, 0:DL])):
                        for j in range(NT):
                            for r in range(REP):
                                p = probs[:, REP * g + r, SELF_AT[j]:SELF_AT[j] + SELF_N[j]]
                                w = vlat[:, j, g * DL:(g + 1) * DL] if first is None else first
                                last = pe.matmul(o[DL * r:DL * r + DL, j * P:T], w, p, start=(j == 0),
                                                 stop=(j == NT - 1))
                    o_done.done(last)

                pe.wait_ge(x_in, 16 * i + 16)
                o = begin("xT")
                for t in range(NT):
                    last = pe.transpose(o[:, t * P:(t + 1) * P], xs[:, t, :], C["ident"][:])
                unit.done(last)
                low.now(pe, i, 1)
                for g in range(KVS):
                    unit.done(three(begin(f"k{g}")[:], C["wk_hi"][:, g, :], C["wk_lo"][:, g, :], xT_hi[:], xT_lo[:]))
                o = begin("v")
                xT_done.now(pe, i, 1)
                for t in range(NT):
                    last = pe.matmul(o[:, t * KVS * DL:(t + 1) * KVS * DL], xT[:, t * P:(t + 1) * P], C["wvd"][:],
                                     start=True, stop=True)
                unit.done(last)
                query(0)
                query(1)
                max_scores(0)
                for h in range(HS):
                    if h + 2 < HS:
                        query(h + 2)
                    if h + 1 < HS:
                        max_scores(h + 1)
                    max_row(h)
                    scores(h)
                    if h == REP:
                        values(0)
                values(1)
                oT_done.now(pe, i, KVS)
                o = begin("y")
                for t in range(NT):
                    for g in range(KVS):
                        last = pe.matmul(o[:, t * P:(t + 1) * P], oT[:, g, t * P:(t + 1) * P], C["bo"][:, g, :],
                                         start=(g == 0), stop=(g == KVS - 1))
                unit.done(last)
                lat_done.now(pe, i, 1)
                o = begin("lT")
                for t in range(NT):
                    last = pe.transpose(o[:, t * P:(t + 1) * P], lat[:, t, :], C["ident"][:])
                unit.done(last)
                cn_done.now(pe, i, 1)
                o = begin("cT")
                pe.transpose(o[:, 0:P], cn[:, 0, :], C["ident"][:])
                unit.done(pe.transpose(o[:, P:CTX], cn[0:CTX_TAIL, 1, :], C["ident"][0:CTX_TAIL, 0:CTX_TAIL]))
                kv_high.now(pe, i, 2)
                kv_low.now(pe, i, 2)
                for c in range(KC):
                    for k in range(2):
                        cols = slice(k * T, (k + 1) * T)
                        unit.done(three(begin(f"V{c}_{k}")[:], kvT_hi[:, c * P:(c + 1) * P], kvT_lo[:, c * P:(c + 1) * P],
                                        C["wv_hi"][:, cols], C["wv_lo"][:, cols]))
                assert unit.n == U.n and o_done.n == KVS

        @block.scalar
        def _(act):
            for c in (high, row_done, probs_done, root_done, kv_high, v_act):
                c.credit(act)
            with act.Fori(0, B) as i:

                def high_part(name, out, rows):
                    at_unit(act, i, name)
                    high.done(act.activation(out, ps(name)[0:rows, :], ACT.Copy))

                def row_and_probs(h):
                    at_unit(act, i, f"t{h}")
                    row_done.done(act.activation(qop[SHIFT_ROW:P, h % 4, :], ps(f"t{h}")[SHIFT_ROW:P, :], ACT.Copy))
                    for j in range(NT):
                        at_unit(act, i, f"s{h}_{j}")
                        probs_done.done(act.activation(probs[:, h, SELF_AT[j]:SELF_AT[j] + SELF_N[j]],
                                                       ps(f"s{h}_{j}")[:, 0:SELF_N[j]], ACT.Exp, scale=SELF_SCALE))

                high_part("xT", xT_hi[:], P)
                for g in range(KVS):
                    high_part(f"k{g}", kop[0:SHIFT_ROW, g, :], SHIFT_ROW)
                high_part("q0", qop[0:SHIFT_ROW, 0, :], SHIFT_ROW)
                high_part("q1", qop[0:SHIFT_ROW, 1, :], SHIFT_ROW)
                for h in range(HS):
                    if h + 2 < HS:
                        high_part(f"q{h + 2}", qop[0:SHIFT_ROW, (h + 2) % 4, :], SHIFT_ROW)
                    row_and_probs(h)
                    if h == 0:
                        var_done.now(act, i, 1)
                        norm_root(act, i, root_done, 0, ve[:, 0, 0:2], r0[:, 0, 0:2])
                for k in (1, 2):
                    var_done.now(act, i, 1 + k)
                    norm_root(act, i, root_done, k, ve[:, k, :], r0[:, k, :])
                for k, (a, b) in enumerate(((0, T), (T, KEYS_E))):
                    kv_full.now(act, i, k + 1)
                    if k == 0:
                        kv_kept.before(act, i, 32)
                    kv_high.done(act.activation(kvT_hi[:, a:b], kvf[:, a:b], ACT.Copy))
                for c in range(KC):
                    n = P if c < KC - 1 else TAIL
                    at_unit(act, i, f"V{c}_0")
                    vout_free(act, i, c)
                    v_act.done(act.activation(vout[0:n, c % 2, 0:T], ps(f"V{c}_0")[0:n, :], ACT.Copy))

        @block.vector
        def _(dve):
            for c in (low, xT_done, vlat_done, max_done, oT_done, y_done, var_done, step, x1_done, lat_done, cn_done,
                      kv_full, kv_low, v_dve):
                c.credit(dve)
            dve.wait_ge(zeroed, 6)
            with dve.Fori(0, B) as i:

                def low_part(name, out, ins):
                    high.now(dve, i, {"xT": 1, "k0": 2, "k1": 3}.get(name) or 4 + int(name[1:]))
                    low.done(dve.tensor_tensor(out, ins, f(out), ALU.subtract))

                def low_of(name):
                    if name[0] == "k":
                        o, r = kop[:, int(name[1:]), :], slice(2 * DL, 3 * DL)
                    else:
                        o, r = qop[:, int(name[1:]) % 4, :], slice(DL, 2 * DL)
                    low_part(name, o[r, :], ps(name)[r, :])

                def maxima(h):
                    for name, tiles in (("ma", (0, 1)), ("mb", (2,)), ("mc", (3,))):
                        at_unit(dve, i, f"{name}{h}")
                        for t in tiles:
                            o0 = 256 * t if t < 2 else 0
                            last = dve.tensor_reduce(nmax[:, h % 2, t, SHIFT_ROW:SHIFT_ROW + 1],
                                                     ps(f"{name}{h}")[:, o0:o0 + P * (t + 1)], AX_X, ALU.max, negate=True)
                            if t == 0:
                                step.done(last)
                        max_done.done(last)

                def outputs(g):
                    o_done.now(dve, i, g + 1)
                    step.own(dve, i)
                    step.done(dve.reciprocal(rden[:], den_ps[:]))
                    step.own(dve, i)
                    oT_done.done(dve.tensor_tensor(oT[:, g, :], o_ps[:], rden[:], ALU.mult))

                high.now(dve, i, 1)
                low.done(dve.tensor_tensor(xT_lo[:], ps("xT")[:], f(xT_hi[:]), ALU.subtract))
                xT_done.done(dve.tensor_copy(xT[:], ps("xT")[:]))
                low_of("k0")
                low_of("k1")
                at_unit(dve, i, "v")
                vlat_done.done(dve.tensor_copy(vlat[:], ps("v")[:, 0:NT * KVS * DL].rearrange("p (t l) -> p t l", t=NT)))
                low_of("q0")
                low_of("q1")
                maxima(0)
                dve.wait_ge(c_in, 32 * i + 32)
                ctiles = [cs[:, 0, :], cs[0:CTX_TAIL, 1, :]]
                var_done.done(norm_stats(dve, i, step, held, ctiles, stats[:, 0], mv[:, 0], ve[:, 0, 0:2]))
                for h in range(HS):
                    if h + 2 < HS:
                        low_of(f"q{h + 2}")
                    if h + 1 < HS:
                        maxima(h + 1)
                    if h == 1:
                        root_done.now(dve, i, 2)
                        var_done.now(dve, i, 1)
                        cn_done.done(norm_apply(dve, i, step, ctiles, [cn[:, 0, :], cn[0:CTX_TAIL, 1, :]], mv[:, 0],
                                                ve[:, 0, 0:2], r0[:, 0, 0:2], r1[:, 0, 0:2]))
                    if h == REP:
                        outputs(0)
                outputs(1)
                at_unit(dve, i, "y")
                y_done.done(dve.tensor_tensor(y[:].rearrange("p n d -> p (n d)"), ps("y")[:],
                                              C["xall"][:, bass.ds(i * NT, NT), :].rearrange("p n d -> p (n d)"), ALU.add))
                y_done.now(dve, i, 1)
                yt = [y[:, t, :] for t in range(NT)]
                var_done.done(norm_stats(dve, i, step, held, yt, stats[:, 1], mv[:, 1], ve[:, 1]))
                root_done.now(dve, i, 4)
                var_done.now(dve, i, 2)
                x1_kept.before(dve, i, 16)
                xt = [x1[:, t, :] for t in range(NT)]
                x1_done.done(norm_apply(dve, i, step, yt, xt, mv[:, 1], ve[:, 1], r0[:, 1], r1[:, 1]))
                x1_done.now(dve, i, 1)
                var_done.done(norm_stats(dve, i, step, held, xt, stats[:, 2], mv[:, 2], ve[:, 2]))
                root_done.now(dve, i, 6)
                var_done.now(dve, i, 3)
                lat_done.done(norm_apply(dve, i, step, xt, [lat[:, t, :] for t in range(NT)], mv[:, 2], ve[:, 2],
                                         r0[:, 2], r1[:, 2]))
                for k, (name, a, b, g) in enumerate((("lT", 0, T, 0), ("cT", T, KEYS, 2))):
                    at_unit(dve, i, name)
                    gain, bias = C["gb"][:, g:g + 1], C["gb"][:, g + 1:g + 2]
                    if k:
                        step.done(dve.tensor_scalar(kvf[:, KEYS:KEYS_E], ps(name)[:, CTX - 2:CTX], gain, bias, ALU.mult, ALU.add))
                    kv_full.done(dve.tensor_scalar(kvf[:, a:b], ps(name)[:, 0:b - a], gain, bias, ALU.mult, ALU.add))
                for k, (a, b) in enumerate(((0, T), (T, KEYS_E))):
                    kv_high.now(dve, i, k + 1)
                    kv_full.now(dve, i, k + 1)
                    kv_low.done(dve.tensor_tensor(kvT_lo[:, a:b], kvf[:, a:b], f(kvT_hi[:, a:b]), ALU.subtract))
                for c in range(KC):
                    n = P if c < KC - 1 else TAIL
                    at_unit(dve, i, f"V{c}_1")
                    vout_free(dve, i, c)
                    v_dve.done(dve.tensor_copy(vout[0:n, c % 2, T:], ps(f"V{c}_1")[0:n, :]))
                assert step.n == STEPS_SELF, step.n


FRONT = ["q", "k0", "k1", "m0_0", "m0_1", "m0_2", "m0_3", "m1_0", "m1_1", "t0", "m1_2", "m1_3", "t1"]


def cross_stage(nc, I, C):
    F_AT = {n: k for k, n in enumerate(FRONT)}
    NF = len(FRONT)
    with ExitStack() as ctx:
        m = Mem(nc, ctx)
        w = [m.sb(f"w{s}", [P, 2, 2, 2, 2, DH], F32R) for s in range(2)]
        v = [m.sb(f"v{s}", [P, KC, P]) for s in range(2)]
        qa = [m.sb(f"qa{s}", [P, 2, T], F32R) for s in range(2)]
        qb = [m.sb(f"qb{s}", [P, 2, T], F32R) for s in range(2)]
        ka = [m.sb(f"ka{s}", [P, 2, KPAD], F32R) for s in range(2)]
        kb = [m.sb(f"kb{s}", [P, 2, KPAD], F32R) for s in range(2)]
        nmax = m.sb("nmaxx", [P, 2, NT, P])
        probs = m.sb("probsx", [P, 2, KC, T])
        psum = [m.sb(f"psum{s}", [P, 2, T]) for s in range(2)]
        oraw = [m.sb(f"oraw{s}", [P, T]) for s in range(2)]
        rden = m.sb("rdenx", [P, T])
        front = [m.pb(f"front{k}", [P, 2, T]) for k in range(2)]
        sc = [m.pb(f"sc{k}", [P, T]) for k in range(2)]
        o_ps = m.pb("o_psx", [P, T])
        den_ps = m.pb("den_psx", [P, T])

        w_in = [m.sem(f"w_in{s}") for s in range(2)]
        v_in = [m.sem(f"v_in{s}") for s in range(2)]
        zeroed = m.sem("zeroedx")
        unit = Count(m.sem("unitx"), NF, 2)
        score = Count(m.sem("score"), 2 * KC, 2)
        qa_high = Count(m.sem("qa_high"), 1, 2)
        qb_high = Count(m.sem("qb_high"), 1, 2)
        ka_high = Count(m.sem("ka_high"), 2, 2)
        qa_low = Count(m.sem("qa_low"), 1, 2)
        kb_low = Count(m.sem("kb_low"), 2, 2)
        maxed = Count(m.sem("maxed"), 2 * NT, 2)
        row_in = Count(m.sem("row_in"), 2, 2)
        expd = Count(m.sem("expd"), 2 * KC, 2)
        summed = Count(m.sem("summed"), 2 * (KC - 1), 2)
        o_done = Count(m.sem("o_donex"), 1, 2)
        den_done = Count(m.sem("den_done"), 1, 2)
        o_out = Count(m.sem("o_out"), 1, 2)
        recip = Count(m.sem("recip"), 1, 2)
        norm = Count(m.sem("norm"), 1, 2)
        block = ctx.enter_context(nc.Block())

        readers = {"q": (qa_low, 1), "k0": (kb_low, 1), "k1": (kb_low, 2), "t0": (row_in, 1), "t1": (row_in, 2)}
        for h in range(2):
            for t in range(NT):
                readers[f"m{h}_{t}"] = (maxed, NT * h + t + 1)

        def front_of(s, name):
            return front[(s * NF + F_AT[name]) % 2]

        def turns(eng, body):
            body(0, 0, 0, first=True)
            body(1, 1, 0)
            with eng.Fori(1, STEPS // 2 - 1) as i:
                body(2 * i, 0, i)
                body(2 * i + 1, 1, i)
            body(STEPS - 2, 0, STEPS // 2 - 1)
            body(STEPS - 1, 1, STEPS // 2 - 1, last=True)

        def after(s, u):
            return 1 - s, u + s

        @block.sync
        def _(sp):
            def load(j, s, u, first=False, last=False):
                unit.before(sp, j, F_AT["k1"] + 1, 2)
                sp.dma_start(f(w[s][:]).rearrange("p a b c d e -> p (a b c d e)"),
                             f(C["wpair"][bass.ds(j % PAIRS, 1)]).rearrange("s p a b c d e -> p (s a b c d e)")).then_inc(w_in[s], 16)
                o_done.before(sp, j, 1, 2)
                sp.dma_start(v[s][:].rearrange("p k c -> p (k c)"),
                             C["vals"].rearrange("b s p k c -> (b s) p (k c)")[bass.ds(j, 1)].rearrange("s p c -> p (s c)")
                             ).then_inc(v_in[s], 16)

            turns(sp, load)

        @block.gpsimd
        def _(pool):
            summed.credit(pool)
            for s in range(2):
                pool.memset(f(kb[s][:]), 0.0).then_inc(zeroed, 1)
                pool.memset(f(ka[s][:, :, KEYS_E:KPAD]), 0.0).then_inc(zeroed, 1)
            pool.memset(probs[:, :, KC - 1, :], 0.0).then_inc(zeroed, 1)
            pool.memset(nmax[:], 0.0).then_inc(zeroed, 1)
            pool.wait_ge(zeroed, 6)
            for s in range(2):
                pool.memset(f(kb[s][DH:DH + 1, :, :]), 1.0).then_inc(zeroed, 1)

            def sums(j, s, u, first=False, last=False):
                den_done.before(pool, j, 1, 2)
                for c in range(1, KC):
                    expd.now(pool, j, 2 * c + 2)
                    for h in range(2):
                        n = P if c < KC - 1 else TAIL
                        if c > 1:
                            summed.now(pool, j, 2 * (c - 2) + h + 1)
                        summed.done(pool.tensor_tensor(psum[s][0:n, h, :], probs[0:n, h, 0, :] if c == 1 else psum[s][0:n, h, :],
                                                       probs[0:n, h, c, :], ALU.add))

            turns(pool, sums)

        @block.tensor
        def _(pe):
            for c in (unit, score, o_done, den_done):
                c.credit(pe)
            pe.wait_ge(zeroed, 8)

            def begin(j, s, name):
                k = F_AT[name]
                count, n = readers[FRONT[(k - 2) % NF]]
                count.now(pe, j, n) if k >= 2 else count.before(pe, j, n)
                return front_of(s, name)

            def project(j, s, kind, h, out, cols):
                hi, lo = w[s][:, 0, kind, h, :, :].rearrange("p a c -> p (a c)"), w[s][:, 1, kind, h, :, :].rearrange("p a c -> p (a c)")
                khi = C["kv_hi"][:, bass.ds(j // PAIRS, 1), cols].rearrange("p b n -> p (b n)")
                klo = C["kv_lo"][:, bass.ds(j // PAIRS, 1), cols].rearrange("p b n -> p (b n)")
                pe.matmul(out, hi, khi, start=True, stop=False)
                pe.matmul(out, hi, klo, start=False, stop=False)
                return pe.matmul(out, lo, khi, start=False, stop=True)

            def queries(j, s, u):
                pe.wait_ge(w_in[s], 16 * (u + 1))
                o = begin(j, s, "q")
                for h in range(2):
                    last = project(j, s, 0, h, o[:, h, :], slice(0, T))
                unit.done(last)

            def keys(j, s, u, h):
                o = begin(j, s, f"k{h}")
                for k in range(2):
                    last = project(j, s, 1, h, o[:, k, 0:HALF], slice(k * HALF, (k + 1) * HALF))
                unit.done(last)

            def max_scores(j, s, h, t):
                if t == 0:
                    qa_low.now(pe, j, 1)
                    ka_high.now(pe, j, h + 1)
                o = begin(j, s, f"m{h}_{t}")
                for k in range(2):
                    last = pe.matmul(o[:, k, 0:HALF], qa[s][:, h, t * P:(t + 1) * P],
                                     ka[s][:, h, k * HALF:(k + 1) * HALF], start=True, stop=True)
                unit.done(last)

            def max_row(j, s, h):
                maxed.now(pe, j, NT * (h + 1))
                o = begin(j, s, f"t{h}")
                for t in range(NT):
                    last = pe.transpose(o[:, 0, t * P:(t + 1) * P], nmax[:, h, t, :], C["ident"][:])
                unit.done(last)

            def score_tile(j, s, c, h):
                k = 2 * c + h
                expd.now(pe, j, k - 1) if k >= 2 else expd.before(pe, j, 2 * KC - 1 + k)
                if c == 0:
                    row_in.now(pe, j, h + 1)
                    kb_low.now(pe, j, h + 1)
                pe.matmul(sc[h][:], ka[s][:, h, c * P:(c + 1) * P], qa[s][:, h, :], start=True, stop=False)
                score.done(pe.matmul(sc[h][:], kb[s][:, h, c * P:(c + 1) * P], qb[s][:, h, :], start=False, stop=True))

            def scores(j, s, c):
                score_tile(j, s, c, 0)
                score_tile(j, s, c, 1)

            def values(j, s, u, c):
                if c == 0:
                    pe.wait_ge(v_in[s], 16 * (u + 1))
                    o_out.before(pe, j, 1)
                expd.now(pe, j, 2 * c + 2)
                for h in range(2):
                    last = pe.matmul(o_ps[h * DH:(h + 1) * DH, :], v[s][:, c, h * DH:(h + 1) * DH], probs[:, h, c, :],
                                     start=(c == 0), stop=(c == KC - 1))
                if c == KC - 1:
                    o_done.done(last)

            def denominators(j, s):
                summed.now(pe, j, 2 * (KC - 1))
                recip.before(pe, j, 1)
                for h in range(2):
                    last = pe.matmul(den_ps[h * DH:(h + 1) * DH, :], C["ones"][:, 0:DH], psum[s][:, h, :], start=True, stop=True)
                den_done.done(last)

            def maxima(j, s, k, last):
                if not last:
                    max_scores(j, s, k // NT, k % NT)

            def step(j, s, u, first=False, last=False):
                n, (ns, nu) = j + 1, after(s, u)
                scores(j, s, 0)
                if not last:
                    queries(n, ns, nu)
                scores(j, s, 1)
                if not first:
                    denominators(j - 1, 1 - s)
                if not last:
                    keys(n, ns, nu, 0)
                values(j, s, u, 0)
                if not last:
                    keys(n, ns, nu, 1)
                scores(j, s, 2)
                maxima(n, ns, 0, last)
                values(j, s, u, 1)
                maxima(n, ns, 1, last)
                scores(j, s, 3)
                maxima(n, ns, 2, last)
                values(j, s, u, 2)
                maxima(n, ns, 3, last)
                scores(j, s, 4)
                maxima(n, ns, 4, last)
                values(j, s, u, 3)
                maxima(n, ns, 5, last)
                score_tile(j, s, 5, 0)
                if not last:
                    max_row(n, ns, 0)
                maxima(n, ns, 6, last)
                score_tile(j, s, 5, 1)
                maxima(n, ns, 7, last)
                values(j, s, u, 4)
                if not last:
                    max_row(n, ns, 1)
                values(j, s, u, 5)

            queries(0, 0, 0)
            keys(0, 0, 0, 0)
            keys(0, 0, 0, 1)
            for k in range(2 * NT):
                maxima(0, 0, k, False)
                if k == 5:
                    max_row(0, 0, 0)
            max_row(0, 0, 1)
            turns(pe, step)
            denominators(STEPS - 1, 1)

        @block.scalar
        def _(act):
            for c in (qa_high, qb_high, ka_high, row_in, expd):
                c.credit(act)

            def q_high(j, s):
                unit.now(act, j, F_AT["q"] + 1)
                qa_high.done(act.activation(qa[s][:], front_of(s, "q")[:], ACT.Copy))

            def q_again(j, s):
                qa_high.now(act, j, 1)
                qb_high.done(act.activation(qb[s][0:DH, :, :], f(qa[s][0:DH, :, :]), ACT.Copy))

            def k_high(j, s, h):
                unit.now(act, j, F_AT[f"k{h}"] + 1)
                ka_high.done(act.activation(ka[s][:, h, 0:KEYS_E].rearrange("p (a n) -> p a n", a=2),
                                            front_of(s, f"k{h}")[:, :, 0:HALF], ACT.Copy))

            def row(j, s, h):
                unit.now(act, j, F_AT[f"t{h}"] + 1)
                row_in.done(act.activation(qb[s][DH:P, h, :], front_of(s, f"t{h}")[DH:P, 0, :], ACT.Copy))

            def exponential(j, c, h):
                score.now(act, j, 2 * c + h + 1)
                summed.before(act, j, 2 * (max(c, 1) - 1) + h + 1)
                rows = P if c < KC - 1 else TAIL
                expd.done(act.activation(probs[0:rows, h, c, :], sc[h][0:rows, :], ACT.Exp, scale=CROSS_SCALE))

            def step(j, s, u, first=False, last=False):
                n, (ns, nu) = j + 1, after(s, u)
                for c in range(KC):
                    exponential(j, c, 0)
                    if c == KC - 1 and not last:
                        row(n, ns, 0)
                    exponential(j, c, 1)
                    if last:
                        continue
                    if c == 0:
                        q_high(n, ns)
                    elif c == 1:
                        k_high(n, ns, 0)
                        k_high(n, ns, 1)
                    elif c == 2:
                        q_again(n, ns)
                if not last:
                    row(n, ns, 1)

            q_high(0, 0)
            q_again(0, 0)
            k_high(0, 0, 0)
            k_high(0, 0, 1)
            row(0, 0, 0)
            row(0, 0, 1)
            turns(act, step)

        @block.vector
        def _(dve):
            for c in (qa_low, kb_low, maxed, o_out, recip, norm):
                c.credit(dve)

            def q_low(j, s):
                qa_high.now(dve, j, 1)
                o = qa[s][DH:P, :, :]
                qa_low.done(dve.tensor_tensor(o, front_of(s, "q")[DH:P, :, :], f(o), ALU.subtract))

            def k_low(j, s, h):
                ka_high.now(dve, j, h + 1)
                view = lambda x: x[s][0:DH, h, 0:KEYS_E].rearrange("p (a n) -> p a n", a=2)
                kb_low.done(dve.tensor_tensor(view(kb), front_of(s, f"k{h}")[0:DH, :, 0:HALF], f(view(ka)), ALU.subtract))

            def maxima(j, s, h):
                for t in range(NT):
                    unit.now(dve, j, F_AT[f"m{h}_{t}"] + 1)
                    maxed.done(dve.tensor_reduce(nmax[:, h, t, DH:DH + 1], front_of(s, f"m{h}_{t}")[:, :, 0:HALF],
                                                 mybir.AxisListType.XY, ALU.max, negate=True))

            def reciprocals(j):
                den_done.now(dve, j, 1)
                norm.before(dve, j, 1)
                recip.done(dve.reciprocal(rden[:], den_ps[:]))

            def outputs(j, s):
                o_done.now(dve, j, 1)
                norm.before(dve, j, 1, 2)
                o_out.done(dve.tensor_copy(oraw[s][:], o_ps[:]))

            def normalise(j, s):
                recip.now(dve, j, 1)
                o_out.now(dve, j, 1)
                out = C["oall"][:, bass.ds(j, 1), :].rearrange("p a n -> p (a n)")
                norm.done(dve.tensor_tensor(out, oraw[s][:], rden[:], ALU.mult))

            def step(j, s, u, first=False, last=False):
                n, (ns, nu) = j + 1, after(s, u)
                if not last:
                    q_low(n, ns)
                    k_low(n, ns, 0)
                    k_low(n, ns, 1)
                    maxima(n, ns, 0)
                    maxima(n, ns, 1)
                if not first:
                    reciprocals(j - 1)
                outputs(j, s)
                if not first:
                    normalise(j - 1, 1 - s)

            dve.wait_ge(zeroed, 8)
            q_low(0, 0)
            k_low(0, 0, 0)
            k_low(0, 0, 1)
            maxima(0, 0, 0)
            maxima(0, 0, 1)
            turns(dve, step)
            reciprocals(STEPS - 1)
            normalise(STEPS - 1, 1)


def close_stage(nc, I, C):
    names = ["out", "back", "turn", "logit"]
    with ExitStack() as ctx:
        m = Mem(nc, ctx)
        wout = m.sb("wout", [P, PAIRS, D])
        t1 = m.sb("t1", [P, T])
        y = m.sb("yc", [P, NT, D])
        x2 = m.sb("x2", [P, NT, D])
        x2T = m.sb("x2T", [P, T])
        stats = m.sb("statsc", [P, NT, 6])
        mv = m.sb("mvc", [P, NT, 2])
        ve = m.sb("vec", [P, NT])
        r0 = m.sb("r0c", [P, NT])
        r1 = m.sb("r1c", [P, NT])
        lg = m.sb("lg", [P, NT, E])
        top = m.sb("top", [P, NT, E])
        idx = m.sb("idx", [P, NT, E], U32)
        ps = [m.pb(f"cps{k}", [P, T]) for k in range(4)]
        w_in = m.sem("wout_in")
        unit = Count(m.sem("cunit"), 4)
        t1_done = Count(m.sem("t1_done"), 1)
        y_done = Count(m.sem("y_donec"), 1)
        var_done = Count(m.sem("var_donec"), 1)
        root_done = Count(m.sem("root_donec"), 2)
        step = Count(m.sem("stepc"), STEPS_CLOSE)
        held = m.sem("heldc")
        x2_done = Count(m.sem("x2_done"), 1)
        x2_kept = Count(m.sem("x2_kept"), 16)
        x2T_done = Count(m.sem("x2T_done"), 1)
        lg_done = Count(m.sem("lg_done"), 1)
        block = ctx.enter_context(nc.Block())

        @block.sync
        def _(sp):
            x2_kept.credit(sp)
            sp.dma_start(wout[:], I["Wout"].rearrange("(s p) n -> p s n", p=P)).then_inc(w_in, 16)
            with sp.Fori(0, B) as i:
                x2_done.now(sp, i, 1)
                sp.dma_start(C["x2all"][:, bass.ds(i * NT, NT), :], x2[:]).then_inc(x2_kept.sem, 16)
            sp.wait_ge(x2_kept.sem, 16 * (B + 1))

        @block.tensor
        def _(pe):
            unit.credit(pe)
            pe.wait_ge(w_in, 16)
            with pe.Fori(0, B) as i:
                t1_done.before(pe, i, 1)
                for s in range(PAIRS):
                    last = pe.matmul(ps[0][:], wout[:, s, :], C["oall"][:, bass.ds(i * PAIRS + s, 1), :].rearrange("p a n -> p (a n)"),
                                     start=(s == 0), stop=(s == PAIRS - 1))
                unit.done(last)
                t1_done.now(pe, i, 1)
                y_done.before(pe, i, 1)
                for t in range(NT):
                    last = pe.transpose(ps[1][:, t * P:(t + 1) * P], t1[:, t * P:(t + 1) * P], C["ident"][:])
                unit.done(last)
                x2_done.now(pe, i, 1)
                x2T_done.before(pe, i, 1)
                for t in range(NT):
                    last = pe.transpose(ps[2][:, t * P:(t + 1) * P], x2[:, t, :], C["ident"][:])
                unit.done(last)
                x2T_done.now(pe, i, 1)
                lg_done.before(pe, i, 1)
                for t in range(NT):
                    last = pe.matmul(ps[3][:, t * E:(t + 1) * E], x2T[:, t * P:(t + 1) * P], C["wg"][:], start=True, stop=True)
                unit.done(last)

        @block.scalar
        def _(act):
            for c in (root_done, x2T_done):
                c.credit(act)
            with act.Fori(0, B) as i:
                var_done.now(act, i, 1)
                norm_root(act, i, root_done, 0, ve[:], r0[:])
                unit.now(act, i, 3)
                x2T_done.done(act.activation(x2T[:], ps[2][:], ACT.Copy))

        @block.vector
        def _(dve):
            for c in (t1_done, y_done, var_done, step, x2_done, lg_done):
                c.credit(dve)
            with dve.Fori(0, B) as i:
                unit.now(dve, i, 1)
                t1_done.done(dve.tensor_copy(t1[:], ps[0][:]))
                unit.now(dve, i, 2)
                y_done.done(dve.tensor_tensor(y[:], ps[1][:].rearrange("p (n d) -> p n d", n=NT),
                                              C["x1all"][:, bass.ds(i, 1), :, :].rearrange("p b n d -> p (b n) d"), ALU.add))
                y_done.now(dve, i, 1)
                yt = [y[:, t, :] for t in range(NT)]
                var_done.done(norm_stats(dve, i, step, held, yt, stats, mv, ve[:]))
                root_done.now(dve, i, 2)
                var_done.now(dve, i, 1)
                x2_kept.before(dve, i, 16)
                x2_done.done(norm_apply(dve, i, step, yt, [x2[:, t, :] for t in range(NT)], mv, ve[:], r0[:], r1[:]))
                unit.now(dve, i, 4)
                lg_done.done(dve.tensor_copy(lg[:], ps[3][:, 0:NT * E].rearrange("p (n e) -> p n e", n=NT)))
                lg_done.now(dve, i, 1)
                dve.sem_inc(held, 1)
                for t in range(NT):
                    step.done(dve.max(top[:, t, :], lg[:, t, :]))
                step.own(dve, i, held)
                for t in range(NT):
                    step.done(dve.max_index(idx[:, t, :], top[:, t, :], lg[:, t, :]))
                step.own(dve, i)
                step.done(dve.tensor_copy(C["topv"][:, :, bass.ds(i * NT, NT)], top[:, :, 0:2].rearrange("p n k -> p k n")))
                step.done(dve.tensor_copy(C["topi"][:, :, bass.ds(i * NT, NT)], idx[:, :, 0:2].rearrange("p n k -> p k n")))
                assert step.n == STEPS_CLOSE, step.n


def route_stage(nc, I, C):
    K2 = 2 * TILES
    with ExitStack() as ctx:
        m = Mem(nc, ctx)
        eio = m.sb("eio", [P, E], U32)
        ef = m.sb("ef", [P, E])
        oh = m.sb("oh", [P, K2, E])
        tot = m.sb("tot", [P, K2, E])
        run = [m.sb(f"run{k}", [P, K2, E]) for k in range(2)]
        rank = m.sb("rank", [P, K2])
        over = m.sb("over", [P, K2])
        slotf = m.sb("slotf", [P, K2])
        e2 = m.sb("e2", [P, TILES])
        den = m.sb("denr", [P, TILES])
        ps_u = m.pb("ps_u", [P, K2, E])
        ps_t = m.pb("ps_t", [P, K2, E])
        pool_done = m.sem("pool_done")
        step = m.sem("stepr")
        oh_done = m.sem("oh_done")
        counted = m.sem("counted")
        diff_done = m.sem("diff_done")
        exp_done = m.sem("exp_done")
        slot_done = m.sem("slot_done")
        scattered = m.sem("scattered")
        block = ctx.enter_context(nc.Block())

        @block.gpsimd
        def _(pool):
            pool.iota(eio[:], pattern=[[1, E]], base=0, channel_multiplier=0).then_inc(pool_done, 1)
            pool.memset(C["yg"][:], 0.0).then_inc(pool_done, 1)
            pool.wait_ge(slot_done, 1)
            for k in range(2):
                for t in range(TILES):
                    n = k * TILES + t
                    pool.indirect_dma_start(C["xslots"], bass.IndirectOffsetOnAxis(ap=C["slot"][:, n:n + 1], axis=0),
                                            C["x2all"][:, t, :], None, bounds_check=SLOTS - 1,
                                            oob_is_err=False).then_inc(scattered, 16)
            pool.wait_ge(scattered, 16 * K2)

        @block.scalar
        def _(act):
            act.wait_ge(diff_done, 1)
            act.activation(e2[:], e2[:], ACT.Exp).then_inc(exp_done, 1)

        @block.tensor
        def _(pe):
            pe.wait_ge(oh_done, 1)
            flat = oh[:].rearrange("p n e -> p (n e)")
            pe.matmul(ps_u[:].rearrange("p n e -> p (n e)"), C["upper"][:], flat, start=True, stop=True)
            pe.matmul(ps_t[:].rearrange("p n e -> p (n e)"), C["ones"][:], flat, start=True, stop=True).then_inc(counted, 1)

        @block.vector
        def _(dve):
            n = [0]

            def then(ins):
                n[0] += 1
                ins.then_inc(step, 1)
                dve.wait_ge(step, n[0])

            topi = C["topi"][:].rearrange("p k n -> p (k n)")
            dve.tensor_tensor(e2[:], C["topv"][:, 1, :], C["topv"][:, 0, :], ALU.subtract).then_inc(diff_done, 1)
            dve.wait_ge(pool_done, 1)
            then(dve.tensor_copy(ef[:], eio[:]))
            dve.tensor_tensor(oh[:], topi.unsqueeze(2).broadcast_to([P, K2, E]), ef[:].unsqueeze(1).broadcast_to([P, K2, E]),
                              ALU.is_equal).then_inc(oh_done, 1)
            dve.wait_ge(counted, 1)
            then(dve.tensor_copy(tot[:], ps_t[:]))
            src, k, d = tot, 0, 1
            while d < K2:
                then(dve.tensor_copy(run[k][:, 0:d, :], src[:, 0:d, :]))
                then(dve.tensor_tensor(run[k][:, d:K2, :], src[:, d:K2, :], src[:, 0:K2 - d, :], ALU.add))
                src, k, d = run[k], 1 - k, 2 * d
            free = run[k]
            then(dve.tensor_tensor(src[:], src[:], tot[:], ALU.subtract))
            then(dve.tensor_tensor(free[:], ps_u[:], src[:], ALU.add))
            dve.wait_ge(oh_done, 1)
            then(dve.tensor_tensor(free[:], free[:], oh[:], ALU.mult))
            then(dve.tensor_reduce(rank[:], free[:], AX_X, ALU.add))
            then(dve.tensor_scalar(over[:], rank[:], float(CAP), None, ALU.is_ge))
            then(dve.scalar_tensor_tensor(out=slotf[:], in0=topi, scalar=float(CAP), in1=rank[:], op0=ALU.mult, op1=ALU.add))
            then(dve.scalar_tensor_tensor(out=slotf[:], in0=over[:], scalar=DROPPED, in1=slotf[:], op0=ALU.mult, op1=ALU.add))
            dve.tensor_copy(C["slot"][:], slotf[:]).then_inc(slot_done, 1)
            dve.wait_ge(exp_done, 1)
            then(dve.tensor_scalar(den[:], e2[:], 1.0, None, ALU.add))
            then(dve.reciprocal(C["wt"][:, 0:TILES], den[:]))
            then(dve.tensor_tensor(C["wt"][:, TILES:K2], C["wt"][:, 0:TILES], e2[:], ALU.mult))
            then(dve.tensor_scalar(over[:], over[:], -1.0, 1.0, ALU.mult, ALU.add))
            then(dve.tensor_tensor(C["wt"][:], C["wt"][:], over[:], ALU.mult))


def expert_stage(nc, I, C):
    N2 = CAP // 2
    with ExitStack() as ctx:
        m = Mem(nc, ctx)
        xe = [m.sb(f"xe{s}", [P, ST, D]) for s in range(2)]
        wf = [m.sb(f"wf{s}", [P, FF]) for s in range(2)]
        wp = [m.sb(f"wp{s}", [P, FC, D]) for s in range(2)]
        xeT = [m.sb(f"xeT{s}", [P, CAP]) for s in range(2)]
        hT = m.sb("hT", [P, FC, CAP])
        ye = [m.sb(f"ye{s}", [P, ST, D]) for s in range(2)]
        ps_x = m.pb("ps_x", [P, 2, T])
        ps_h = [m.pb(f"ps_h{k}", [P, 2, T]) for k in range(2)]
        ps_y = m.pb("ps_y", [P, 2, T])
        x_in = [m.sem(f"xe_in{s}") for s in range(2)]
        w_in = [m.sem(f"we_in{s}") for s in range(2)]
        turned = Count(m.sem("turned_e"), 1, 2)
        xeT_done = Count(m.sem("xeT_done"), 2, 2)
        h_done = Count(m.sem("h_done"), FC, 2)
        act_done = Count(m.sem("act_done"), FC, 2)
        y_done = Count(m.sem("y_done_e"), 1, 2)
        y_out = Count(m.sem("y_out"), 2, 2)
        y_kept = [Count(m.sem(f"y_kept{s}"), 16, 1) for s in range(2)]
        block = ctx.enter_context(nc.Block())

        def turns(eng, body):
            with eng.Fori(0, E // 2) as i:
                body(2 * i, 0, i)
                body(2 * i + 1, 1, i)

        @block.sync
        def _(sp):
            def load(e, s, i):
                turned.before(sp, e, 1, 2)
                sp.dma_start(xe[s][:], C["xslots"].rearrange("(e n p) d -> e p n d", p=P, n=ST)[bass.ds(e, 1)]
                             .rearrange("e p n d -> p (e n) d")).then_inc(x_in[s], 16)
                y_done.before(sp, e, 1, 2)
                sp.dma_start(wf[s][:], I["c_fc"][bass.ds(e, 1)].rearrange("e p n -> p (e n)")).then_inc(w_in[s], 16)
                sp.dma_start(wp[s][:], I["c_proj"][bass.ds(e, 1)].rearrange("e (c p) d -> p (e c) d", p=P)).then_inc(w_in[s], 16)

            turns(sp, load)

        @block.gpsimd
        def _(pool):
            for c in y_kept:
                c.credit(pool)

        @block.tensor
        def _(pe):
            for c in (turned, h_done, y_done):
                c.credit(pe)

            def expert(e, s, i):
                pe.wait_ge(x_in[s], 16 * (i + 1))
                xeT_done.before(pe, e, 2)
                for t in range(ST):
                    last = pe.transpose(ps_x[:, t // NT, (t % NT) * P:(t % NT) * P + P], xe[s][:, t, :], C["ident"][:])
                turned.done(last)
                pe.wait_ge(w_in[s], 32 * (i + 1))
                xeT_done.now(pe, e, 2)
                for c in range(FC):
                    act_done.now(pe, e, c - 1) if c >= 2 else act_done.before(pe, e, FC - 1 + c)
                    for k in range(2):
                        last = pe.matmul(ps_h[c % 2][:, k, 0:N2], wf[s][:, c * P:(c + 1) * P], xeT[s][:, k * N2:(k + 1) * N2],
                                         start=True, stop=True)
                    h_done.done(last)
                act_done.now(pe, e, FC)
                y_out.before(pe, e, 2)
                for t in range(ST):
                    for c in range(FC):
                        last = pe.matmul(ps_y[:, t // NT, (t % NT) * P:(t % NT) * P + P], hT[:, c, t * P:(t + 1) * P],
                                         wp[s][:, c, :], start=(c == 0), stop=(c == FC - 1))
                y_done.done(last)

            turns(pe, expert)

        @block.scalar
        def _(act):
            for c in (act_done,):
                c.credit(act)

            def expert(e, s, i):
                for c in range(FC):
                    h_done.now(act, e, c + 1)
                    if c == 0:
                        y_done.before(act, e, 1)
                    act_done.done(act.activation(hT[:, c, :].rearrange("p (k n) -> p k n", k=2), ps_h[c % 2][:, :, 0:N2], ACT.Gelu))
                y_out.now(act, e, 2)
                act.dma_start(C["yslots"].rearrange("(e n p) d -> e p n d", p=P, n=ST)[bass.ds(e, 1)]
                              .rearrange("e p n d -> p (e n) d"), ye[s][:]).then_inc(y_kept[s].sem, 16)

            turns(act, expert)
            for c in y_kept:
                act.wait_ge(c.sem, 16 * (E // 2 + 1))

        @block.vector
        def _(dve):
            for c in (xeT_done, y_out):
                c.credit(dve)

            def expert(e, s, i):
                turned.now(dve, e, 1)
                xeT_done.done(dve.tensor_copy(xeT[s][:, 0:T], ps_x[:, 0, :]))
                xeT_done.done(dve.tensor_copy(xeT[s][:, T:CAP], ps_x[:, 1, 0:CAP - T]))
                y_done.now(dve, e, 1)
                y_kept[s].before(dve, i, 16)
                y_out.done(dve.tensor_copy(ye[s][:, 0:NT, :], ps_y[:, 0, :].rearrange("p (n d) -> p n d", n=NT)))
                y_out.done(dve.tensor_copy(ye[s][:, NT:ST, :], ps_y[:, 1:2, 0:D]))

            turns(dve, expert)


def combine_stage(nc, I, C, out):
    with ExitStack() as ctx:
        m = Mem(nc, ctx)
        y = m.sb("yf", [P, TILES, D])
        z = m.sb("zf", [P, TILES, D])
        stats = m.sb("statsf", [P, TILES, 6])
        mv = m.sb("mvf", [P, TILES, 2])
        ve = m.sb("vef", [P, TILES])
        r0 = m.sb("r0f", [P, TILES])
        r1 = m.sb("r1f", [P, TILES])
        got = [m.sem(f"got{b}") for b in range(B)]
        var_done = Count(m.sem("var_donef"), 1)
        root_done = Count(m.sem("root_donef"), 2)
        step = Count(m.sem("stepf"), STEPS_COMBINE)
        held = m.sem("heldf")
        z_done = Count(m.sem("z_done"), 1)
        stored = m.sem("storedf")
        block = ctx.enter_context(nc.Block())

        @block.gpsimd
        def _(pool):
            for b in range(B):
                for k in range(2):
                    for t in range(b * NT, (b + 1) * NT):
                        n = k * TILES + t
                        pool.indirect_dma_start(C["yg"][:, n, :], None, C["yslots"],
                                                bass.IndirectOffsetOnAxis(ap=C["slot"][:, n:n + 1], axis=0),
                                                bounds_check=SLOTS - 1, oob_is_err=False).then_inc(got[b], 16)

        @block.scalar
        def _(act):
            root_done.credit(act)
            for b in range(B):
                var_done.now(act, b, 1)
                norm_root(act, b, root_done, 0, ve[:, b * NT:(b + 1) * NT], r0[:, b * NT:(b + 1) * NT])

        @block.sync
        def _(sp):
            for b in range(B):
                z_done.now(sp, b, 1)
                sp.dma_start(out[b].rearrange("(n p) d -> p n d", p=P), z[:, b * NT:(b + 1) * NT, :]).then_inc(stored, 16)
            sp.wait_ge(stored, 16 * B)

        @block.vector
        def _(dve):
            for c in (var_done, step, z_done):
                c.credit(dve)
            for b in range(B):
                step.n = 0
                dve.wait_ge(got[b], 16 * 2 * NT)
                r = slice(b * NT, (b + 1) * NT)
                for k in range(2):
                    for t in range(b * NT, (b + 1) * NT):
                        n = k * TILES + t
                        step.done(dve.scalar_tensor_tensor(out=y[:, t, :], in0=C["yg"][:, n, :], scalar=C["wt"][:, n:n + 1],
                                                           in1=C["x2all"][:, t, :] if k == 0 else y[:, t, :],
                                                           op0=ALU.mult, op1=ALU.add))
                    step.own(dve, b)
                yt = [y[:, t, :] for t in range(b * NT, (b + 1) * NT)]
                var_done.done(norm_stats(dve, b, step, held, yt, stats[:, r], mv[:, r], ve[:, r]))
                root_done.now(dve, b, 2)
                var_done.now(dve, b, 1)
                z_done.done(norm_apply(dve, b, step, yt, [z[:, t, :] for t in range(b * NT, (b + 1) * NT)], mv[:, r],
                                       ve[:, r], r0[:, r], r1[:, r]))
                assert step.n == STEPS_COMBINE, step.n


def common(m):
    C = {}
    C["ident"] = m.sb("ident", [P, P])
    C["ident_b"] = m.sb("ident_b", [P, P], BF16)
    C["mask"] = m.sb("mask", [P, P], BF16)
    C["maskT"] = m.sb("maskT", [P, P], BF16)
    C["ones"] = m.sb("ones", [P, P])
    C["upper"] = m.sb("upper", [P, P])
    C["gb"] = m.sb("gb", [P, 4])
    C["wg"] = m.sb("wg", [P, E])
    C["x1all"] = m.sb("x1all", [P, B, NT, D])
    C["kv_hi"], C["kv_lo"] = m.split("kvall", [P, B, KEYS_E])
    return C


def self_common(m, C):
    C["aq_hi"], C["aq_lo"] = m.split("aq", [P, HS, P])
    C["wk_hi"], C["wk_lo"] = m.split("wk", [P, KVS, P])
    C["wv_hi"], C["wv_lo"] = m.split("wv", [P, HX * DH])
    C["wvd"] = m.sb("wvd", [P, KVS * DL])
    C["bo"] = m.sb("bo", [P, KVS, D])
    C["xall"] = m.sb("xall", [P, TILES, D])


def decoder(nc, I, out):
    with ExitStack() as ctx:
        m = Mem(nc, ctx)
        C = common(m)
        late_common(m, C)
        dram = lambda name, shape, dt=F32: nc.dram_tensor(name, shape, dt, kind="Internal").ap()
        C["xslots"] = dram("xslots", (SLOTS, D))
        C["yslots"] = dram("yslots", (SLOTS, D))
        C["wpair"] = dram("wpair", (PAIRS, P, 2, 2, 2, 2, DH), F32R)
        C["vals"] = dram("vals", (B, PAIRS, P, KC, P))
        with ExitStack() as early:
            self_common(Mem(nc, early), C)
            setup_stage(nc, I, C)
            self_stage(nc, I, C)
        with ExitStack() as mid:
            C["oall"] = Mem(nc, mid).sb("oall", [P, STEPS, T])
            cross_stage(nc, I, C)
            close_stage(nc, I, C)
        C["yg"] = m.sb("yg", [P, 2 * TILES, D])
        route_stage(nc, I, C)
        expert_stage(nc, I, C)
        combine_stage(nc, I, C, out)


def late_common(m, C):
    C["x2all"] = m.sb("x2all", [P, TILES, D])
    C["topv"] = m.sb("topv", [P, 2, TILES])
    C["topi"] = m.sb("topi", [P, 2, TILES])
    C["slot"] = m.sb("slot", [P, 2 * TILES], U32)
    C["wt"] = m.sb("wt", [P, 2 * TILES])


INPUTS = {"x": "x", "ctx_1024": "ctx", "L0_attn_wq": "wq", "L0_attn_wk_down": "wk_down", "L0_attn_wv_down": "wv_down",
          "L0_attn_wk_up": "wk_up", "L0_attn_wv_up": "wv_up", "L0_attn_wo": "wo", "L0_xattn_ln_m_g": "ln_m_g",
          "L0_xattn_ln_m_b": "ln_m_b", "L0_xattn_ln_l_g": "ln_l_g", "L0_xattn_ln_l_b": "ln_l_b", "L0_xattn_Wq": "Wq",
          "L0_xattn_Wkv": "Wkv", "L0_xattn_Wout": "Wout", "L0_ffn_w_g": "w_g", "L0_ffn_c_fc": "c_fc",
          "L0_ffn_c_proj": "c_proj"}


def kernel(**inputs):
    import numpy as np
    import concourse.bacc as bacc
    from concourse import mybir as mb
    from concourse.bass_utils import run_bass_kernel_spmd

    nc = bacc.Bacc("TRN2", target_bir_lowering=False, num_devices=1)
    arrays, I = {}, {}
    for name, short in INPUTS.items():
        a = np.ascontiguousarray(inputs[name])
        arrays[f"in_{name}"] = a
        I[short] = nc.dram_tensor(f"in_{name}", a.shape, mb.dt.from_np(a.dtype), kind="ExternalInput").ap()
    out = nc.dram_tensor("out_0", (B, T, D), F32, kind="ExternalOutput").ap()
    decoder(nc, I, out)
    return run_bass_kernel_spmd(nc, [arrays], core_ids=[0]).results[0]["out_0"]
```

```python
from contextlib import ExitStack

import concourse.bass as bass
from concourse import mybir

ALU = mybir.AluOpType
ACT = mybir.ActivationFunctionType
AX_X = mybir.AxisListType.X
F32 = mybir.dt.float32
F32R = mybir.dt.float32r
BF16 = mybir.dt.bfloat16
U32 = mybir.dt.uint32
I32 = mybir.dt.int32

P = 128
B = 4
T = 512
D = 128
NT = T // P
TILES = B * NT
EPS = 1e-5
VOUTS = 3

HS, KVS, REP, DL = 8, 2, 4, 32
SELF_SCALE = float(D) ** -0.5
SHIFT_ROW = 3 * DL
SELF_N = [T - P * j for j in range(NT)]
SELF_AT = [sum(SELF_N[:j]) for j in range(NT)]
SELF_W = sum(SELF_N)
MASKED = -1.0e30

HX, DH = 16, 64
CROSS_SCALE = float(DH) ** -0.5
CTX = 154
CTX_TAIL = CTX - P
KEYS = T + CTX
KEYS_E = KEYS + 2
HALF = KEYS_E // 2
KC = (KEYS + P - 1) // P
KPAD = KC * P
TAIL = KEYS - (KC - 1) * P
PAIRS = HX // 2
STEPS = B * PAIRS

E, FF = 8, 512
FC = FF // P
CAP = 640
SLOTS = E * CAP
ST = CAP // P
SETUP_STORES = E + B + 4
DROPPED = 8192.0

RING = 4
TAIL_RING = 2
ROOT_MAGIC = float(0x5F3759DF - (1 << 22) - (1 << 31))


def norm_steps(tiles):
    return 2 * tiles + 11


class Names:

    def __init__(self, names, ring):
        self.names = names
        self.at = {n: k for k, n in enumerate(names)}
        self.n = len(names)
        self.ring = ring

    def bank(self, name):
        return self.at[name] % self.ring

    def before(self, name):
        k = self.at[name]
        if k >= self.ring:
            return self.names[k - self.ring], False
        return self.names[max(x for x in range(self.n) if x % self.ring == k)], True


def f(ap):
    return ap.bitcast(F32)


class Mem:

    def __init__(self, nc, ctx):
        self.nc, self.ctx = nc, ctx

    def sb(self, name, shape, dt=F32):
        return self.ctx.enter_context(self.nc.sbuf_tensor(name, shape, dt))

    def pb(self, name, shape):
        return self.ctx.enter_context(self.nc.psum_tensor(name, shape, F32))

    def sem(self, name):
        return self.ctx.enter_context(self.nc.semaphore(name))

    def split(self, name, shape):
        return self.sb(name + "_hi", shape, F32R), self.sb(name + "_lo", shape, F32R)


def setup_stage(nc, I, C):
    with ExitStack() as ctx:
        m = Mem(nc, ctx)
        wq = m.sb("wq", [P, HS * D])
        wkd = m.sb("wkd", [P, KVS * DL])
        wku = m.sb("wku", [DL, D])
        wvu = m.sb("wvu", [DL, D])
        wo = m.sb("wo", [P, HS, D])
        cq = m.sb("cq", [P, HX * DH])
        ckv = m.sb("ckv", [P, 2 * HX * DH])
        wqT = m.sb("wqT", [P, HS, P])
        upT = m.sb("upT", [P, 2, DL])
        stage_hi, stage_lo, zero, stored = C["stage_hi"], C["stage_lo"], C["zero"], C["stored"]
        pq = [m.pb(f"pq{k}", [P, 4, P]) for k in range(2)]
        pu = m.pb("pu", [P, 2, DL])
        pa = m.pb("pa", [P, HS, DL])
        pv = m.pb("pv", [P, KVS, D])
        loaded = m.sem("loaded")
        loaded_self = m.sem("loaded_self")
        consts = m.sem("consts")
        turned = m.sem("turned")
        copied = m.sem("copied")
        high = m.sem("high")
        low = m.sem("low")
        combined = m.sem("combined")
        block = ctx.enter_context(nc.Block())

        @block.sync
        def _(sp):
            sp.dma_start(wq[:], I["wq"]).then_inc(loaded_self, 16)
            sp.dma_start(wku[:], I["wk_up"]).then_inc(loaded_self, 16)
            sp.dma_start(wvu[:], I["wv_up"]).then_inc(loaded_self, 16)
            sp.dma_start(wo[:], I["wo"].rearrange("(h p) n -> p h n", p=P)).then_inc(loaded_self, 16)
            sp.dma_start(wkd[:], I["wk_down"]).then_inc(loaded_self, 16)
            sp.dma_start(C["wvd"][:], I["wv_down"]).then_inc(loaded_self, 16)
            sp.dma_start(cq[:], I["Wq"]).then_inc(loaded, 16)
            sp.dma_start(ckv[:], I["Wkv"]).then_inc(loaded, 16)
            sp.dma_start(C["xall"][:], I["x"].rearrange("b (n p) d -> p (b n) d", p=P)).then_inc(loaded, 16)
            sp.dma_start(C["gb"][:, 0:1], I["ln_l_g"].rearrange("(p a) -> p a", a=1)).then_inc(loaded, 16)
            sp.dma_start(C["gb"][:, 1:2], I["ln_l_b"].rearrange("(p a) -> p a", a=1)).then_inc(loaded, 16)
            sp.dma_start(C["gb"][:, 2:3], I["ln_m_g"].rearrange("(p a) -> p a", a=1)).then_inc(loaded, 16)
            sp.dma_start(C["gb"][:, 3:4], I["ln_m_b"].rearrange("(p a) -> p a", a=1)).then_inc(loaded, 16)
            sp.dma_start(C["wg"][:], I["w_g"]).then_inc(loaded, 16)
            sp.wait_ge(consts, 1)
            for e in range(E):
                sp.dma_start(C["xslots"][e * CAP:(e + 1) * CAP, :].rearrange("(n p) d -> p n d", p=P),
                             zero[:, 0:ST, :]).then_inc(stored, 16)
            for b in range(B):
                sp.dma_start(C["vals"][b, :, TAIL:P, KC - 1, :].rearrange("s p c -> p s c"),
                             zero[0:P - TAIL, 0:PAIRS, :]).then_inc(stored, 16)
            sp.wait_ge(high, 2)
            sp.wait_ge(low, 2)
            for part, src in enumerate((stage_hi, stage_lo)):
                for kind in range(2):
                    sp.dma_start(f(C["wpair"][:, :, part, kind, :]).rearrange("s p c -> p s c"),
                                 f(src[:, kind, :, :]).rearrange("p (s h) c -> p s (h c)", h=2)).then_inc(stored, 16)

        @block.gpsimd
        def _(pool):
            pool.memset(zero[:], 0.0).then_inc(consts, 1)
            pool.memset(C["ident"][:], 0.0).then_inc(consts, 1)
            pool.memset(C["mask"][:], 0.0).then_inc(consts, 1)
            pool.memset(C["maskT"][:], 0.0).then_inc(consts, 1)
            pool.memset(C["ones"][:], 1.0).then_inc(consts, 1)
            pool.memset(C["upper"][:], 0.0).then_inc(consts, 1)
            pool.memset(C["aq_hi"][:].bitcast(F32), 0.0).then_inc(consts, 1)
            pool.memset(C["aq_lo"][:].bitcast(F32), 0.0).then_inc(consts, 1)
            pool.memset(C["wk_hi"][:].bitcast(F32), 0.0).then_inc(consts, 1)
            pool.memset(C["wk_lo"][:].bitcast(F32), 0.0).then_inc(consts, 1)
            pool.wait_ge(consts, 10)
            pool.affine_select(out=C["ident"][:], in_=C["ident"][:], compare_op=ALU.not_equal, fill=1.0, base=0,
                               pattern=[[-1, P]], channel_multiplier=1).then_inc(consts, 1)
            pool.affine_select(out=C["mask"][:], in_=C["mask"][:], compare_op=ALU.is_ge, fill=MASKED, base=0,
                               pattern=[[-1, P]], channel_multiplier=1).then_inc(consts, 1)
            pool.affine_select(out=C["maskT"][:], in_=C["maskT"][:], compare_op=ALU.is_ge, fill=MASKED, base=0,
                               pattern=[[1, P]], channel_multiplier=-1).then_inc(consts, 1)
            pool.affine_select(out=C["upper"][:], in_=C["upper"][:], compare_op=ALU.is_ge, fill=1.0, base=0,
                               pattern=[[-1, P]], channel_multiplier=1).then_inc(consts, 1)
            pool.wait_ge(consts, 14)
            pool.tensor_copy(C["ident_b"][:], C["ident"][:]).then_inc(consts, 1)

        @block.tensor
        def _(pe):
            pe.wait_ge(consts, 14)
            pe.wait_ge(loaded_self, 16 * 6)
            for h in range(HS):
                t = pe.transpose(pq[h // 4][:, h % 4, :], wq[:, h * D:(h + 1) * D], C["ident"][:])
                if h % 4 == 3:
                    t.then_inc(turned, 1)
            pe.transpose(pu[:, 0, :], wku[:], C["ident"][0:DL, 0:DL])
            pe.transpose(pu[:, 1, :], wvu[:], C["ident"][0:DL, 0:DL]).then_inc(turned, 1)
            pe.wait_ge(copied, 3)
            for h in range(HS):
                t = pe.matmul(pa[:, h, :], wqT[:, h, :], upT[:, 0, :], start=True, stop=True)
            t.then_inc(combined, 1)
            for h in range(HS):
                t = pe.matmul(pv[DL * (h % REP):DL * (h % REP) + DL, h // REP, :], upT[:, 1, :], wo[:, h, :],
                              start=True, stop=True)
            t.then_inc(combined, 1)

        @block.vector
        def _(dve):
            for k in range(2):
                dve.wait_ge(turned, k + 1)
                dve.tensor_copy(wqT[:, 4 * k:4 * k + 4, :], pq[k][:]).then_inc(copied, 1)
            dve.wait_ge(turned, 3)
            dve.tensor_copy(upT[:], pu[:]).then_inc(copied, 1)
            dve.wait_ge(loaded, 16 * 8)
            for kind, src in enumerate((cq[:], ckv[:, 0:HX * DH])):
                dve.wait_ge(high, kind + 1)
                dve.tensor_tensor(stage_lo[:, kind, :, :], src.rearrange("p (h c) -> p h c", c=DH),
                                  f(stage_hi[:, kind, :, :]), ALU.subtract).then_inc(low, 1)
            dve.wait_ge(high, 3)
            dve.tensor_tensor(C["wv_lo"][:], ckv[:, HX * DH:], f(C["wv_hi"][:]), ALU.subtract).then_inc(low, 1)
            dve.wait_ge(combined, 1)
            dve.wait_ge(consts, 10)
            for c in range(3):
                dve.wait_ge(high, 6)
                dve.tensor_tensor(C["aq_lo"][:, :, c * DL:(c + 1) * DL], pa[:], f(C["aq_hi"][:, :, c * DL:(c + 1) * DL]),
                                  ALU.subtract).then_inc(low, 1)
            for c in range(3):
                dve.wait_ge(high, 7 + c)
                dve.tensor_tensor(C["wk_lo"][:, :, c * DL:(c + 1) * DL], wkd[:].rearrange("p (g l) -> p g l", l=DL),
                                  f(C["wk_hi"][:, :, c * DL:(c + 1) * DL]), ALU.subtract).then_inc(low, 1)
            dve.wait_ge(combined, 2)
            dve.tensor_copy(C["bo"][:], pv[:]).then_inc(low, 1)

        @block.scalar
        def _(act):
            act.wait_ge(loaded, 16 * 8)
            for kind, src in enumerate((cq[:], ckv[:, 0:HX * DH])):
                act.activation(stage_hi[:, kind, :, :], src.rearrange("p (h c) -> p h c", c=DH),
                               ACT.Copy).then_inc(high, 1)
            act.activation(C["wv_hi"][:], ckv[:, HX * DH:], ACT.Copy).then_inc(high, 1)
            act.wait_ge(combined, 1)
            act.wait_ge(consts, 10)
            for c in range(3):
                act.activation(C["aq_hi"][:, :, c * DL:(c + 1) * DL], pa[:], ACT.Copy).then_inc(high, 1)
            act.wait_ge(loaded_self, 16 * 6)
            for c in range(3):
                act.activation(C["wk_hi"][:, :, c * DL:(c + 1) * DL],
                               wkd[:].rearrange("p (g l) -> p g l", l=DL), ACT.Copy).then_inc(high, 1)


SELF_UNITS = Names(
    ["xT", "k0", "k1", "v", "q0", "q1", "ma0", "mb0", "mc0"]
    + [u for h in range(HS)
       for u in [f"t{h}"] + ([f"q{h + 2}"] if h + 2 < HS else []) + ([f"m{c}{h + 1}" for c in "abc"] if h + 1 < HS else [])
       + [f"s{h}_{j}" for j in range(NT)]], RING)
TAIL_UNITS = Names(["y", "lT", "cT"] + [f"V{c}_{k}" for c in range(KC) for k in range(2)], TAIL_RING)


class Count:

    def __init__(self, sem, per, ahead=1):
        self.sem, self.per, self.ahead, self.n = sem, per, ahead, 0

    def credit(self, eng):
        eng.sem_inc(self.sem, self.per * self.ahead)

    def now(self, eng, i, k):
        eng.wait_ge(self.sem, (i + self.ahead) * self.per + k)

    def before(self, eng, i, k, turns=1):
        eng.wait_ge(self.sem, (i + self.ahead - turns) * self.per + k)

    def done(self, ins):
        self.n += 1
        ins.then_inc(self.sem, 1)

    def own(self, eng, i, at=None):
        eng.wait_ge(self.sem, (i + self.ahead) * self.per + (self.n - 1) % self.per + 1)
        if at is not None:
            eng.sem_inc(at, 1)


class Norm:

    def __init__(self, m, name, tiles):
        self.n = tiles
        self.stats = m.sb("stats_" + name, [P, tiles, 6])
        self.mv = m.sb("mv_" + name, [P, tiles, 2])
        self.half = m.sb("half_" + name, [P, tiles])
        self.root = m.sb("root_" + name, [P, tiles])
        self.tmp = m.sb("tmp_" + name, [P, tiles])

    def moments(self, dve, i, step, held, tiles):
        for k, t in enumerate(tiles):
            step.done(dve.bn_stats(self.stats[0:t.shape[0], k, :], t))
        step.own(dve, i, held)
        for k, t in enumerate(tiles):
            step.done(dve.bn_aggr(self.mv[0:t.shape[0], k, :], self.stats[0:t.shape[0], k, :]))
        step.own(dve, i)
        step.done(dve.tensor_scalar(self.half[:], self.mv[:, :, 1], EPS, 0.5, ALU.add, ALU.mult))
        step.own(dve, i)

    def roots(self, dve, i, step):
        r, h, a = self.root, self.half, self.tmp
        step.done(dve.tensor_scalar(r[:].bitcast(I32), h[:].bitcast(I32), -0.5, ROOT_MAGIC, ALU.mult, ALU.add))
        step.own(dve, i)
        for _ in range(3):
            step.done(dve.tensor_tensor(a[:], r[:], r[:], ALU.mult))
            step.own(dve, i)
            step.done(dve.tensor_tensor(a[:], a[:], h[:], ALU.mult))
            step.own(dve, i)
            step.done(dve.scalar_tensor_tensor(out=r[:], in0=a[:], scalar=1.5, in1=r[:], op0=ALU.subtract, op1=ALU.mult))
            step.own(dve, i)

    def apply(self, dve, tiles, outs, done, first=0):
        for k, (t, o) in enumerate(zip(tiles, outs), first):
            n = t.shape[0]
            done.done(dve.tensor_scalar(o, t, self.mv[0:n, k, 0:1], self.root[0:n, k:k + 1], ALU.subtract, ALU.mult))


def self_stage(nc, I, C):
    U, W = SELF_UNITS, TAIL_UNITS
    with ExitStack() as ctx:
        m = Mem(nc, ctx)
        xs = m.sb("xs", [P, NT, D])
        cs = m.sb("cs", [P, 2, D])
        xT = m.sb("xT", [P, T])
        xT_hi, xT_lo = m.split("xTs", [P, T])
        kop = m.sb("kop", [P, KVS, T], F32R)
        qop = m.sb("qop", [P, 4, T], F32R)
        vlat = m.sb("vlat", [P, NT, KVS * DL])
        nmax = m.sb("nmax", [P, 2, NT, P])
        probs = m.sb("probs", [P, HS, SELF_W])
        rden = m.sb("rden", [P, T])
        oT = m.sb("oT", [P, KVS, T])
        y = m.sb("y", [P, NT, D])
        x1 = m.sb("x1", [P, NT, D])
        lat = m.sb("lat", [P, NT, D])
        cn = m.sb("cn", [P, 2, D])
        norm1 = Norm(m, "x1", NT + 2)
        norm2 = Norm(m, "lat", NT)
        kvf = m.sb("kvf", [P, KEYS_E])
        kvT_hi, kvT_lo = m.split("kvT", [P, KPAD])
        vout = m.sb("vout", [P, VOUTS, HX * DH])
        ring = [m.pb(f"ring{k}", [P, T]) for k in range(RING)]
        tail_ring = [m.pb(f"tail_ring{k}", [P, T]) for k in range(TAIL_RING)]
        o_ps = m.pb("o_ps", [P, T])
        den_ps = m.pb("den_ps", [P, T])

        x_in = m.sem("x_in")
        c_in = m.sem("c_in")
        zeroed = m.sem("zeroed")
        unit = Count(m.sem("unit"), U.n)
        tail_unit = Count(m.sem("tail_unit"), W.n)
        high = Count(m.sem("high"), 3 + HS)
        low = Count(m.sem("low"), 3 + HS)
        xT_done = Count(m.sem("xT_done"), 1)
        vlat_done = Count(m.sem("vlat_done"), 1)
        max_done = Count(m.sem("max_done"), 3 * HS)
        row_done = Count(m.sem("row_done"), HS)
        probs_done = Count(m.sem("probs_done"), NT * HS)
        o_done = Count(m.sem("o_done"), KVS)
        rden_done = Count(m.sem("rden_done"), KVS)
        oT_done = Count(m.sem("oT_done"), KVS)
        y_done = Count(m.sem("y_done"), 1)
        step = Count(m.sem("step"), HS)
        tail_step = Count(m.sem("tail_step"), norm_steps(NT + 2) + norm_steps(NT) + 1)
        held = m.sem("held")
        x1_done = Count(m.sem("x1_done"), NT)
        x1_kept = Count(m.sem("x1_kept"), 16)
        lat_done = Count(m.sem("lat_done"), NT)
        cn_done = Count(m.sem("cn_done"), 2)
        kv_full = Count(m.sem("kv_full"), 2)
        kv_high = Count(m.sem("kv_high"), 2)
        kv_low = Count(m.sem("kv_low"), 2)
        kv_kept = Count(m.sem("kv_kept"), 32)
        v_act = Count(m.sem("v_act"), KC)
        v_dve = Count(m.sem("v_dve"), KC)
        v_kept = [Count(m.sem(f"v_kept{k}"), 16 * KC // VOUTS) for k in range(VOUTS)]
        block = ctx.enter_context(nc.Block())

        readers = {"xT": (xT_done, 1), "k0": (low, 2), "k1": (low, 3), "v": (vlat_done, 1), "y": (y_done, 1),
                   "lT": (kv_full, 1), "cT": (kv_full, 2)}
        for h in range(HS):
            readers[f"q{h}"] = (low, 4 + h)
            readers[f"t{h}"] = (row_done, 1 + h)
            for k, c in enumerate("abc"):
                readers[f"m{c}{h}"] = (max_done, 3 * h + k + 1)
            for j in range(NT):
                readers[f"s{h}_{j}"] = (probs_done, NT * h + j + 1)
        for c in range(KC):
            readers[f"V{c}_0"] = (v_act, c + 1)
            readers[f"V{c}_1"] = (v_dve, c + 1)

        def at_unit(eng, i, name):
            unit.now(eng, i, U.at[name] + 1)

        def at_tail(eng, i, name):
            tail_unit.now(eng, i, W.at[name] + 1)

        def ps(name):
            return ring[U.bank(name)]

        def tail_ps(name):
            return tail_ring[W.bank(name)]

        def vout_free(eng, i, c):
            kept = v_kept[c % VOUTS]
            kept.now(eng, i, 16 * (c // VOUTS)) if c >= VOUTS else kept.before(eng, i, kept.per)

        def turns(eng, body, tail):
            body(0, first=True)
            with eng.Fori(1, B) as i:
                body(i)
            tail(B - 1)

        @block.gpsimd
        def _(pool):
            pool.memset(norm1.mv[:], 0.0).then_inc(zeroed, 1)
            pool.memset(nmax[:], 0.0).then_inc(zeroed, 1)
            pool.wait_ge(zeroed, 2)
            pool.memset(f(kop[SHIFT_ROW:P, :, :]), 0.0).then_inc(zeroed, 1)
            pool.wait_ge(zeroed, 3)
            pool.memset(f(kvT_hi[:, KEYS_E:KPAD]), 0.0).then_inc(zeroed, 1)
            pool.memset(f(kvT_lo[:, KEYS_E:KPAD]), 0.0).then_inc(zeroed, 1)
            pool.wait_ge(zeroed, 5)
            pool.memset(f(kop[SHIFT_ROW:SHIFT_ROW + 1, :, :]), 1.0).then_inc(zeroed, 1)
            with pool.Fori(0, B) as i:
                unit.before(pool, i, U.at["xT"] + 1)
                pool.dma_start(xs[:], I["x"][bass.ds(i, 1), :, :].rearrange("b (n p) d -> p (b n) d", p=P)).then_inc(x_in, 16)
                cn_done.before(pool, i, 2)
                pool.dma_start(cs[:, 0, :], I["ctx"][bass.ds(i, 1), 0:P, :].rearrange("b p d -> p (b d)")).then_inc(c_in, 16)
                pool.dma_start(cs[0:CTX_TAIL, 1, :],
                               I["ctx"][bass.ds(i, 1), P:CTX, :].rearrange("b p d -> p (b d)")).then_inc(c_in, 16)

        @block.sync
        def _(sp):
            for c in (x1_kept, kv_kept, *v_kept):
                c.credit(sp)
            with sp.Fori(0, B) as i:
                x1_done.now(sp, i, NT)
                sp.dma_start(C["x1all"][:, bass.ds(i, 1), :, :], x1[:, None, :, :]).then_inc(x1_kept.sem, 16)
                kv_high.now(sp, i, 2)
                kv_low.now(sp, i, 2)
                sp.dma_start(f(C["kv_hi"][:, bass.ds(i, 1), :]), f(kvT_hi[:, None, 0:KEYS_E])).then_inc(kv_kept.sem, 16)
                sp.dma_start(f(C["kv_lo"][:, bass.ds(i, 1), :]), f(kvT_lo[:, None, 0:KEYS_E])).then_inc(kv_kept.sem, 16)
                for c in range(KC):
                    n = P if c < KC - 1 else TAIL
                    v_act.now(sp, i, c + 1)
                    v_dve.now(sp, i, c + 1)
                    sp.dma_start(C["vals"][bass.ds(i, 1), :, 0:n, c, :].rearrange("b s p c -> p (b s) c"),
                                 vout[0:n, c % VOUTS, :].rearrange("p (s c) -> p s c", s=PAIRS)).then_inc(v_kept[c % VOUTS].sem, 16)
            sp.wait_ge(C["stored"], 16 * SETUP_STORES)
            for c in (x1_kept, kv_kept, *v_kept):
                c.before(sp, B, c.per)

        @block.tensor
        def _(pe):
            for c in (unit, tail_unit, o_done):
                c.credit(pe)
            pe.wait_ge(zeroed, 6)

            def begin(i, name, names=U, banks=ring):
                other, earlier = names.before(name)
                count, n = readers[other]
                count.before(pe, i, n) if earlier else count.now(pe, i, n)
                return banks[names.bank(name)]

            def begin_tail(i, name):
                return begin(i, name, W, tail_ring)

            def three(out, hi, lo, mhi, mlo):
                pe.matmul(out, hi, mhi, start=True, stop=False)
                pe.matmul(out, hi, mlo, start=False, stop=False)
                return pe.matmul(out, lo, mhi, start=False, stop=True)

            def query(i, h):
                unit.done(three(begin(i, f"q{h}")[:], C["aq_hi"][:, h, :], C["aq_lo"][:, h, :], xT_hi[:], xT_lo[:]))

            def max_scores(i, h):
                g = h // REP
                low.now(pe, i, 4 + h)
                for name, tiles in (("ma", (0, 1)), ("mb", (2,)), ("mc", (3,))):
                    o = begin(i, f"{name}{h}")
                    for t in tiles:
                        n = max(256, P * (t + 1))
                        o0 = 256 * t if t < 2 else 0
                        pe.matmul(o[:, o0:o0 + n], qop[0:SHIFT_ROW, h % 4, t * P:(t + 1) * P],
                                  kop[0:SHIFT_ROW, g, 0:n], start=True, stop=False)
                        last = pe.matmul(o[:, o0 + t * P:o0 + (t + 1) * P], C["ident_b"][:], C["mask"][:],
                                         start=False, stop=True)
                    unit.done(last)

            def max_row(i, h):
                max_done.now(pe, i, 3 * h + 3)
                o = begin(i, f"t{h}")
                for t in range(NT):
                    last = pe.transpose(o[:, t * P:(t + 1) * P], nmax[:, h % 2, t, :], C["ident"][:])
                unit.done(last)

            def scores(i, h):
                g = h // REP
                row_done.now(pe, i, h + 1)
                for j in range(NT):
                    o = begin(i, f"s{h}_{j}")
                    pe.matmul(o[:, 0:SELF_N[j]], kop[:, g, j * P:(j + 1) * P], qop[:, h % 4, j * P:T],
                              start=True, stop=False)
                    unit.done(pe.matmul(o[:, 0:P], C["ident_b"][:], C["maskT"][:], start=False, stop=True))

            def values(i, g):
                probs_done.now(pe, i, NT * REP * (g + 1))
                vlat_done.now(pe, i, 1)
                oT_done.now(pe, i, g) if g else oT_done.before(pe, i, KVS)
                for o, first in ((o_ps, None), (den_ps, C["ones"][:, 0:DL])):
                    for j in range(NT):
                        for r in range(REP):
                            p = probs[:, REP * g + r, SELF_AT[j]:SELF_AT[j] + SELF_N[j]]
                            w = vlat[:, j, g * DL:(g + 1) * DL] if first is None else first
                            last = pe.matmul(o[DL * r:DL * r + DL, j * P:T], w, p, start=(j == 0),
                                             stop=(j == NT - 1))
                o_done.done(last)

            def output_rows(j):
                oT_done.now(pe, j, KVS)
                o = begin_tail(j, "y")
                for t in range(NT):
                    for g in range(KVS):
                        last = pe.matmul(o[:, t * P:(t + 1) * P], oT[:, g, t * P:(t + 1) * P], C["bo"][:, g, :],
                                         start=(g == 0), stop=(g == KVS - 1))
                tail_unit.done(last)

            def turn_inputs(j):
                lat_done.now(pe, j, NT)
                o = begin_tail(j, "lT")
                for t in range(NT):
                    last = pe.transpose(o[:, t * P:(t + 1) * P], lat[:, t, :], C["ident"][:])
                tail_unit.done(last)
                cn_done.now(pe, j, 2)
                o = begin_tail(j, "cT")
                pe.transpose(o[:, 0:P], cn[:, 0, :], C["ident"][:])
                tail_unit.done(pe.transpose(o[:, P:CTX], cn[0:CTX_TAIL, 1, :], C["ident"][0:CTX_TAIL, 0:CTX_TAIL]))

            def project_values(j, c):
                if c == 0:
                    kv_high.now(pe, j, 2)
                    kv_low.now(pe, j, 2)
                for k in range(2):
                    cols = slice(k * T, (k + 1) * T)
                    tail_unit.done(three(begin_tail(j, f"V{c}_{k}")[:], kvT_hi[:, c * P:(c + 1) * P], kvT_lo[:, c * P:(c + 1) * P],
                                         C["wv_hi"][:, cols], C["wv_lo"][:, cols]))

            def body(i, first=False):
                j = i - 1
                pe.wait_ge(x_in, 16 * i + 16)
                o = begin(i, "xT")
                for t in range(NT):
                    last = pe.transpose(o[:, t * P:(t + 1) * P], xs[:, t, :], C["ident"][:])
                unit.done(last)
                if not first:
                    values(j, 1)
                low.now(pe, i, 1)
                for g in range(KVS):
                    unit.done(three(begin(i, f"k{g}")[:], C["wk_hi"][:, g, :], C["wk_lo"][:, g, :], xT_hi[:], xT_lo[:]))
                o = begin(i, "v")
                xT_done.now(pe, i, 1)
                for t in range(NT):
                    last = pe.matmul(o[:, t * KVS * DL:(t + 1) * KVS * DL], xT[:, t * P:(t + 1) * P], C["wvd"][:],
                                     start=True, stop=True)
                unit.done(last)
                query(i, 0)
                query(i, 1)
                max_scores(i, 0)
                for h in range(HS):
                    max_row(i, h)
                    if h + 2 < HS:
                        query(i, h + 2)
                    if h + 1 < HS:
                        max_scores(i, h + 1)
                    scores(i, h)
                    if h == REP - 1:
                        values(i, 0)
                    if first:
                        continue
                    if h == 0:
                        output_rows(j)
                    elif h == 3:
                        turn_inputs(j)
                    elif h > 4:
                        project_values(j, 2 * (h - 5))
                        project_values(j, 2 * (h - 5) + 1)

            def tail(j):
                values(j, 1)
                output_rows(j)
                turn_inputs(j)
                for c in range(KC):
                    project_values(j, c)

            turns(pe, body, tail)

        @block.scalar
        def _(act):
            for c in (high, row_done, probs_done, kv_high, v_act):
                c.credit(act)

            def high_part(i, name, out, rows):
                at_unit(act, i, name)
                high.done(act.activation(out, ps(name)[0:rows, :], ACT.Copy))

            def row(i, h):
                at_unit(act, i, f"t{h}")
                row_done.done(act.activation(qop[SHIFT_ROW:P, h % 4, :], ps(f"t{h}")[SHIFT_ROW:P, :], ACT.Copy))

            def exponentials(i, h):
                for j in range(NT):
                    at_unit(act, i, f"s{h}_{j}")
                    probs_done.done(act.activation(probs[:, h, SELF_AT[j]:SELF_AT[j] + SELF_N[j]],
                                                   ps(f"s{h}_{j}")[:, 0:SELF_N[j]], ACT.Exp, scale=SELF_SCALE))

            def inputs_high(j):
                for k, (a, b) in enumerate(((0, T), (T, KEYS_E))):
                    kv_full.now(act, j, k + 1)
                    if k == 0:
                        kv_kept.before(act, j, 32)
                    kv_high.done(act.activation(kvT_hi[:, a:b], kvf[:, a:b], ACT.Copy))

            def values_out(j, c):
                n = P if c < KC - 1 else TAIL
                at_tail(act, j, f"V{c}_0")
                vout_free(act, j, c)
                v_act.done(act.activation(vout[0:n, c % VOUTS, 0:T], tail_ps(f"V{c}_0")[0:n, :], ACT.Copy))

            def body(i, first=False):
                j = i - 1
                high_part(i, "xT", xT_hi[:], P)
                for g in range(KVS):
                    high_part(i, f"k{g}", kop[0:SHIFT_ROW, g, :], SHIFT_ROW)
                high_part(i, "q0", qop[0:SHIFT_ROW, 0, :], SHIFT_ROW)
                high_part(i, "q1", qop[0:SHIFT_ROW, 1, :], SHIFT_ROW)
                for h in range(HS):
                    row(i, h)
                    if h + 2 < HS:
                        high_part(i, f"q{h + 2}", qop[0:SHIFT_ROW, (h + 2) % 4, :], SHIFT_ROW)
                    exponentials(i, h)
                    if first:
                        continue
                    if h == 4:
                        inputs_high(j)
                    elif h > 4:
                        values_out(j, 2 * (h - 5))
                        values_out(j, 2 * (h - 5) + 1)

            def tail(j):
                inputs_high(j)
                for c in range(KC):
                    values_out(j, c)

            turns(act, body, tail)

        @block.vector
        def _(dve):
            for c in (low, xT_done, vlat_done, max_done, rden_done, oT_done, y_done, step, tail_step, x1_done, lat_done,
                      cn_done, kv_full, kv_low, v_dve):
                c.credit(dve)
            dve.wait_ge(zeroed, 6)
            rows = [y[:, t, :] for t in range(NT)]
            contexts = [cs[:, 0, :], cs[0:CTX_TAIL, 1, :]]
            normed = [x1[:, t, :] for t in range(NT)]
            latents = [lat[:, t, :] for t in range(NT)]

            def low_of(i, name):
                if name[0] == "k":
                    n, o, r = 2 + int(name[1:]), kop[:, int(name[1:]), :], slice(2 * DL, 3 * DL)
                else:
                    n, o, r = 4 + int(name[1:]), qop[:, int(name[1:]) % 4, :], slice(DL, 2 * DL)
                high.now(dve, i, n)
                low.done(dve.tensor_tensor(o[r, :], ps(name)[r, :], f(o[r, :]), ALU.subtract))

            def maxima(i, h):
                for name, tiles in (("ma", (0, 1)), ("mb", (2,)), ("mc", (3,))):
                    at_unit(dve, i, f"{name}{h}")
                    for t in tiles:
                        o0 = 256 * t if t < 2 else 0
                        last = dve.tensor_reduce(nmax[:, h % 2, t, SHIFT_ROW:SHIFT_ROW + 1],
                                                 ps(f"{name}{h}")[:, o0:o0 + P * (t + 1)], AX_X, ALU.max, negate=True)
                        if t == 0:
                            step.done(last)
                    max_done.done(last)

            def outputs(i, g):
                o_done.now(dve, i, g + 1)
                oT_done.now(dve, i, g) if g else oT_done.before(dve, i, KVS)
                rden_done.done(dve.reciprocal(rden[:], den_ps[:]))
                rden_done.now(dve, i, g + 1)
                oT_done.done(dve.tensor_tensor(oT[:, g, :], o_ps[:], rden[:], ALU.mult))

            def sum_rows(j):
                at_tail(dve, j, "y")
                y_done.done(dve.tensor_tensor(y[:].rearrange("p n d -> p (n d)"), tail_ps("y")[:],
                                              C["xall"][:, bass.ds(j * NT, NT), :].rearrange("p n d -> p (n d)"), ALU.add))
                dve.wait_ge(c_in, 32 * j + 32)
                y_done.now(dve, j, 1)
                norm1.moments(dve, j, tail_step, held, rows + contexts)
                norm1.roots(dve, j, tail_step)

            def norm_rows(j):
                x1_kept.before(dve, j, 16)
                norm1.apply(dve, rows, normed, x1_done)
                norm1.apply(dve, contexts, [cn[:, 0, :], cn[0:CTX_TAIL, 1, :]], cn_done, NT)
                x1_done.now(dve, j, NT)
                norm2.moments(dve, j, tail_step, held, normed)

            def norm_latents(j):
                norm2.roots(dve, j, tail_step)
                norm2.apply(dve, normed, latents, lat_done)

            def inputs(j):
                for k, (name, a, b, g) in enumerate((("lT", 0, T, 0), ("cT", T, KEYS, 2))):
                    at_tail(dve, j, name)
                    gain, bias = C["gb"][:, g:g + 1], C["gb"][:, g + 1:g + 2]
                    if k:
                        tail_step.done(dve.tensor_scalar(kvf[:, KEYS:KEYS_E], tail_ps(name)[:, CTX - 2:CTX], gain, bias,
                                                         ALU.mult, ALU.add))
                    kv_full.done(dve.tensor_scalar(kvf[:, a:b], tail_ps(name)[:, 0:b - a], gain, bias, ALU.mult, ALU.add))
                for k, (a, b) in enumerate(((0, T), (T, KEYS_E))):
                    kv_high.now(dve, j, k + 1)
                    kv_full.now(dve, j, k + 1)
                    kv_low.done(dve.tensor_tensor(kvT_lo[:, a:b], kvf[:, a:b], f(kvT_hi[:, a:b]), ALU.subtract))

            def values_out(j, c):
                n = P if c < KC - 1 else TAIL
                at_tail(dve, j, f"V{c}_1")
                vout_free(dve, j, c)
                v_dve.done(dve.tensor_copy(vout[0:n, c % VOUTS, T:], tail_ps(f"V{c}_1")[0:n, :]))

            def body(i, first=False):
                j = i - 1
                high.now(dve, i, 1)
                low.done(dve.tensor_tensor(xT_lo[:], ps("xT")[:], f(xT_hi[:]), ALU.subtract))
                xT_done.done(dve.tensor_copy(xT[:], ps("xT")[:]))
                low_of(i, "k0")
                low_of(i, "k1")
                at_unit(dve, i, "v")
                vlat_done.done(dve.tensor_copy(vlat[:], ps("v")[:, 0:NT * KVS * DL].rearrange("p (t l) -> p t l", t=NT)))
                low_of(i, "q0")
                low_of(i, "q1")
                maxima(i, 0)
                if not first:
                    outputs(j, 1)
                for h in range(HS):
                    if h + 2 < HS:
                        low_of(i, f"q{h + 2}")
                    if h + 1 < HS:
                        maxima(i, h + 1)
                    if not first:
                        if h == 1:
                            sum_rows(j)
                        elif h == 2:
                            norm_rows(j)
                        elif h == 3:
                            norm_latents(j)
                        elif h == 4:
                            inputs(j)
                        elif h > 4:
                            values_out(j, 2 * (h - 5))
                            values_out(j, 2 * (h - 5) + 1)
                    if h == 5:
                        outputs(i, 0)
                assert step.n % step.per == 0

            def tail(j):
                outputs(j, 1)
                sum_rows(j)
                norm_rows(j)
                norm_latents(j)
                inputs(j)
                for c in range(KC):
                    values_out(j, c)

            turns(dve, body, tail)


FRONT = ["q", "k", "m0_0", "m0_1", "m0_2", "m0_3", "m1_0", "m1_1", "t0", "m1_2", "m1_3", "t1"]


def cross_stage(nc, I, C):
    F_AT = {n: k for k, n in enumerate(FRONT)}
    NF = len(FRONT)
    with ExitStack() as ctx:
        m = Mem(nc, ctx)
        w = [m.sb(f"w{s}", [P, 2, 2, P], F32R) for s in range(2)]
        v = [m.sb(f"v{s}", [P, KC, P]) for s in range(2)]
        qa = [m.sb(f"qa{s}", [P, 2, T], F32R) for s in range(2)]
        qb = [m.sb(f"qb{s}", [P, 2, T], F32R) for s in range(2)]
        ka = [m.sb(f"ka{s}", [P, 2, KPAD], F32R) for s in range(2)]
        kb = [m.sb(f"kb{s}", [P, 2, KPAD], F32R) for s in range(2)]
        nmax = m.sb("nmaxx", [P, 2, NT, P])
        probs = m.sb("probsx", [P, 2, KC, T])
        psum = [m.sb(f"psum{s}", [P, 2, T]) for s in range(2)]
        oraw = [m.sb(f"oraw{s}", [P, T]) for s in range(2)]
        rden = m.sb("rdenx", [P, T])
        front = [m.pb(f"front{k}", [P, 2, T]) for k in range(2)]
        sc = [m.pb(f"sc{k}", [P, T]) for k in range(2)]
        o_ps = m.pb("o_psx", [P, T])
        den_ps = m.pb("den_psx", [P, T])

        w_in = [m.sem(f"w_in{s}") for s in range(2)]
        v_in = [m.sem(f"v_in{s}") for s in range(2)]
        zeroed = m.sem("zeroedx")
        unit = Count(m.sem("unitx"), NF, 2)
        score = Count(m.sem("score"), 2 * KC, 2)
        qa_high = Count(m.sem("qa_high"), 2, 2)
        qb_high = Count(m.sem("qb_high"), 2, 2)
        ka_high = Count(m.sem("ka_high"), 2, 2)
        ka_again = Count(m.sem("ka_again"), 2, 2)
        qa_low = Count(m.sem("qa_low"), 2, 2)
        kb_low = Count(m.sem("kb_low"), 2, 2)
        maxed = Count(m.sem("maxed"), 2 * NT, 2)
        row_in = Count(m.sem("row_in"), 2, 2)
        expd = Count(m.sem("expd"), 2 * KC, 2)
        summed = Count(m.sem("summed"), 2 * (KC - 1), 2)
        o_done = Count(m.sem("o_donex"), 1, 2)
        den_done = Count(m.sem("den_done"), 1, 2)
        o_out = Count(m.sem("o_out"), 1, 2)
        recip = Count(m.sem("recip"), 1, 2)
        norm = Count(m.sem("norm"), 1, 2)
        block = ctx.enter_context(nc.Block())

        readers = {"q": (qa_low, 2), "k": (kb_low, 2), "t0": (row_in, 1), "t1": (row_in, 2)}
        for h in range(2):
            for t in range(NT):
                readers[f"m{h}_{t}"] = (maxed, NT * h + t + 1)

        own = [slice(0, DH), slice(DH, P)]
        other = [slice(DH, P), slice(0, DH)]

        def front_of(s, name):
            return front[(s * NF + F_AT[name]) % 2]

        def turns(eng, body):
            body(0, 0, 0, first=True)
            body(1, 1, 0)
            with eng.Fori(1, STEPS // 2 - 1) as i:
                body(2 * i, 0, i)
                body(2 * i + 1, 1, i)
            body(STEPS - 2, 0, STEPS // 2 - 1)
            body(STEPS - 1, 1, STEPS // 2 - 1, last=True)

        def after(s, u):
            return 1 - s, u + s

        @block.sync
        def _(sp):
            def load(j, s, u, first=False, last=False):
                unit.before(sp, j, F_AT["k"] + 1, 2)
                sp.dma_start(f(w[s][:]).rearrange("p a b c -> p (a b c)"),
                             f(C["wpair"][bass.ds(j % PAIRS, 1)]).rearrange("s p a b c -> p (s a b c)")).then_inc(w_in[s], 16)
                o_done.before(sp, j, 1, 2)
                sp.dma_start(v[s][:].rearrange("p k c -> p (k c)"),
                             C["vals"].rearrange("b s p k c -> (b s) p (k c)")[bass.ds(j, 1)].rearrange("s p c -> p (s c)")
                             ).then_inc(v_in[s], 16)

            turns(sp, load)

        @block.gpsimd
        def _(pool):
            summed.credit(pool)
            for s in range(2):
                pool.memset(f(kb[s][:]), 0.0).then_inc(zeroed, 1)
                pool.memset(f(ka[s][:, :, KEYS_E:KPAD]), 0.0).then_inc(zeroed, 1)
            pool.memset(probs[:, :, KC - 1, :], 0.0).then_inc(zeroed, 1)
            pool.memset(nmax[:], 0.0).then_inc(zeroed, 1)
            pool.wait_ge(zeroed, 6)
            for s in range(2):
                for h in range(2):
                    one = other[h].start
                    pool.memset(f(kb[s][one:one + 1, h, :]), 1.0).then_inc(zeroed, 1)

            def sums(j, s, u, first=False, last=False):
                den_done.before(pool, j, 1, 2)
                for c in range(1, KC):
                    expd.now(pool, j, 2 * c + 2)
                    for h in range(2):
                        n = P if c < KC - 1 else TAIL
                        if c > 1:
                            summed.now(pool, j, 2 * (c - 2) + h + 1)
                        summed.done(pool.tensor_tensor(psum[s][0:n, h, :], probs[0:n, h, 0, :] if c == 1 else psum[s][0:n, h, :],
                                                       probs[0:n, h, c, :], ALU.add))

            turns(pool, sums)

        @block.tensor
        def _(pe):
            for c in (unit, score, o_done, den_done):
                c.credit(pe)
            pe.wait_ge(zeroed, 10)

            def begin(j, s, name):
                k = F_AT[name]
                count, n = readers[FRONT[(k - 2) % NF]]
                count.now(pe, j, n) if k >= 2 else count.before(pe, j, n)
                return front_of(s, name)

            def project(j, s, kind, out, cols):
                hi, lo = w[s][:, 0, kind, :], w[s][:, 1, kind, :]
                khi = C["kv_hi"][:, bass.ds(j // PAIRS, 1), cols].rearrange("p b n -> p (b n)")
                klo = C["kv_lo"][:, bass.ds(j // PAIRS, 1), cols].rearrange("p b n -> p (b n)")
                pe.matmul(out, hi, khi, start=True, stop=False)
                pe.matmul(out, hi, klo, start=False, stop=False)
                return pe.matmul(out, lo, khi, start=False, stop=True)

            def queries(j, s, u):
                pe.wait_ge(w_in[s], 16 * (u + 1))
                unit.done(project(j, s, 0, begin(j, s, "q")[:, 0, :], slice(0, T)))

            def keys(j, s):
                o = begin(j, s, "k")
                for k in range(2):
                    last = project(j, s, 1, o[:, k, 0:HALF], slice(k * HALF, (k + 1) * HALF))
                unit.done(last)

            def max_scores(j, s, h, t):
                if t == 0:
                    qa_low.now(pe, j, h + 1)
                    ka_again.now(pe, j, h + 1)
                o = begin(j, s, f"m{h}_{t}")
                for k in range(2):
                    last = pe.matmul(o[:, k, 0:HALF], qa[s][:, h, t * P:(t + 1) * P],
                                     ka[s][:, h, k * HALF:(k + 1) * HALF], start=True, stop=True)
                unit.done(last)

            def max_row(j, s, h):
                maxed.now(pe, j, NT * (h + 1))
                o = begin(j, s, f"t{h}")
                for t in range(NT):
                    last = pe.transpose(o[:, 0, t * P:(t + 1) * P], nmax[:, h, t, :], C["ident"][:])
                unit.done(last)

            def score_tile(j, s, c, h):
                k = 2 * c + h
                expd.now(pe, j, k - 1) if k >= 2 else expd.before(pe, j, 2 * KC - 1 + k)
                if c == 0:
                    row_in.now(pe, j, h + 1)
                    kb_low.now(pe, j, h + 1)
                pe.matmul(sc[h][:], ka[s][:, h, c * P:(c + 1) * P], qa[s][:, h, :], start=True, stop=False)
                score.done(pe.matmul(sc[h][:], kb[s][:, h, c * P:(c + 1) * P], qb[s][:, h, :], start=False, stop=True))

            def scores(j, s, c):
                score_tile(j, s, c, 0)
                score_tile(j, s, c, 1)

            def values(j, s, u, c):
                if c == 0:
                    pe.wait_ge(v_in[s], 16 * (u + 1))
                    o_out.before(pe, j, 1)
                expd.now(pe, j, 2 * c + 2)
                for h in range(2):
                    last = pe.matmul(o_ps[h * DH:(h + 1) * DH, :], v[s][:, c, h * DH:(h + 1) * DH], probs[:, h, c, :],
                                     start=(c == 0), stop=(c == KC - 1))
                if c == KC - 1:
                    o_done.done(last)

            def denominators(j, s):
                summed.now(pe, j, 2 * (KC - 1))
                recip.before(pe, j, 1)
                for h in range(2):
                    last = pe.matmul(den_ps[h * DH:(h + 1) * DH, :], C["ones"][:, 0:DH], psum[s][:, h, :], start=True, stop=True)
                den_done.done(last)

            def maxima(j, s, k, last):
                if not last:
                    max_scores(j, s, k // NT, k % NT)

            def step(j, s, u, first=False, last=False):
                n, (ns, nu) = j + 1, after(s, u)
                scores(j, s, 0)
                if not last:
                    queries(n, ns, nu)
                scores(j, s, 1)
                if not first:
                    denominators(j - 1, 1 - s)
                if not last:
                    keys(n, ns)
                values(j, s, u, 0)
                scores(j, s, 2)
                values(j, s, u, 1)
                maxima(n, ns, 0, last)
                maxima(n, ns, 1, last)
                scores(j, s, 3)
                maxima(n, ns, 2, last)
                values(j, s, u, 2)
                maxima(n, ns, 3, last)
                scores(j, s, 4)
                maxima(n, ns, 4, last)
                values(j, s, u, 3)
                maxima(n, ns, 5, last)
                score_tile(j, s, 5, 0)
                if not last:
                    max_row(n, ns, 0)
                maxima(n, ns, 6, last)
                score_tile(j, s, 5, 1)
                maxima(n, ns, 7, last)
                values(j, s, u, 4)
                if not last:
                    max_row(n, ns, 1)
                values(j, s, u, 5)

            queries(0, 0, 0)
            keys(0, 0)
            for k in range(2 * NT):
                maxima(0, 0, k, False)
                if k == 5:
                    max_row(0, 0, 0)
            max_row(0, 0, 1)
            turns(pe, step)
            denominators(STEPS - 1, 1)

        @block.scalar
        def _(act):
            for c in (qa_high, qb_high, ka_high, ka_again, row_in, expd):
                c.credit(act)

            def q_high(j, s):
                unit.now(act, j, F_AT["q"] + 1)
                for h in range(2):
                    qa_high.done(act.activation(qa[s][own[h], h, :], front_of(s, "q")[own[h], 0, :], ACT.Copy))

            def q_again(j, s):
                for h in range(2):
                    qa_high.now(act, j, h + 1)
                    qb_high.done(act.activation(qb[s][own[h], h, :], f(qa[s][own[h], h, :]), ACT.Copy))

            def k_high(j, s):
                unit.now(act, j, F_AT["k"] + 1)
                for h in range(2):
                    ka_high.done(act.activation(ka[s][own[h], h, 0:KEYS_E].rearrange("p (a n) -> p a n", a=2),
                                                front_of(s, "k")[own[h], :, 0:HALF], ACT.Copy))
                for h in range(2):
                    ka_high.now(act, j, h + 1)
                    ka_again.done(act.activation(ka[s][other[h], h, 0:KEYS_E], f(ka[s][own[h], h, 0:KEYS_E]), ACT.Copy))

            def row(j, s, h):
                unit.now(act, j, F_AT[f"t{h}"] + 1)
                row_in.done(act.activation(qb[s][other[h], h, :], front_of(s, f"t{h}")[other[h], 0, :], ACT.Copy))

            def exponential(j, c, h):
                score.now(act, j, 2 * c + h + 1)
                summed.before(act, j, 2 * (max(c, 1) - 1) + h + 1)
                rows = P if c < KC - 1 else TAIL
                expd.done(act.activation(probs[0:rows, h, c, :], sc[h][0:rows, :], ACT.Exp, scale=CROSS_SCALE))

            def step(j, s, u, first=False, last=False):
                n, (ns, nu) = j + 1, after(s, u)
                for c in range(KC):
                    exponential(j, c, 0)
                    if c == KC - 1 and not last:
                        row(n, ns, 0)
                    exponential(j, c, 1)
                    if last:
                        continue
                    if c == 0:
                        q_high(n, ns)
                    elif c == 1:
                        k_high(n, ns)
                    elif c == 2:
                        q_again(n, ns)
                if not last:
                    row(n, ns, 1)

            q_high(0, 0)
            q_again(0, 0)
            k_high(0, 0)
            row(0, 0, 0)
            row(0, 0, 1)
            turns(act, step)

        @block.vector
        def _(dve):
            for c in (qa_low, kb_low, maxed, o_out, recip, norm):
                c.credit(dve)

            def q_low(j, s):
                for h in range(2):
                    qa_high.now(dve, j, h + 1)
                    qa_low.done(dve.tensor_tensor(qa[s][other[h], h, :], front_of(s, "q")[own[h], 0, :],
                                                  f(qa[s][own[h], h, :]), ALU.subtract))

            def k_low(j, s):
                view = lambda x, h: x[s][own[h], h, 0:KEYS_E].rearrange("p (a n) -> p a n", a=2)
                for h in range(2):
                    ka_high.now(dve, j, h + 1)
                    kb_low.done(dve.tensor_tensor(view(kb, h), front_of(s, "k")[own[h], :, 0:HALF], f(view(ka, h)),
                                                  ALU.subtract))

            def maxima(j, s, h):
                for t in range(NT):
                    unit.now(dve, j, F_AT[f"m{h}_{t}"] + 1)
                    maxed.done(dve.tensor_reduce(nmax[:, h, t, other[h].start:other[h].start + 1], front_of(s, f"m{h}_{t}")[:, :, 0:HALF],
                                                 mybir.AxisListType.XY, ALU.max, negate=True))

            def reciprocals(j):
                den_done.now(dve, j, 1)
                norm.before(dve, j, 1)
                recip.done(dve.reciprocal(rden[:], den_ps[:]))

            def outputs(j, s):
                o_done.now(dve, j, 1)
                norm.before(dve, j, 1, 2)
                o_out.done(dve.tensor_copy(oraw[s][:], o_ps[:]))

            def normalise(j, s):
                recip.now(dve, j, 1)
                o_out.now(dve, j, 1)
                out = C["oall"][:, bass.ds(j, 1), :].rearrange("p a n -> p (a n)")
                norm.done(dve.tensor_tensor(out, oraw[s][:], rden[:], ALU.mult))

            def step(j, s, u, first=False, last=False):
                n, (ns, nu) = j + 1, after(s, u)
                if not last:
                    q_low(n, ns)
                    k_low(n, ns)
                    maxima(n, ns, 0)
                    maxima(n, ns, 1)
                if not first:
                    reciprocals(j - 1)
                outputs(j, s)
                if not first:
                    normalise(j - 1, 1 - s)

            dve.wait_ge(zeroed, 10)
            q_low(0, 0)
            k_low(0, 0)
            maxima(0, 0, 0)
            maxima(0, 0, 1)
            turns(dve, step)
            reciprocals(STEPS - 1)
            normalise(STEPS - 1, 1)


def close_stage(nc, I, C):
    names = ["out", "back", "turn", "logit"]
    with ExitStack() as ctx:
        m = Mem(nc, ctx)
        wout = m.sb("wout", [P, PAIRS, D])
        t1 = m.sb("t1", [P, T])
        y = m.sb("yc", [P, NT, D])
        x2 = m.sb("x2", [P, NT, D])
        x2T = m.sb("x2T", [P, T])
        norm = Norm(m, "x2", NT)
        lg = m.sb("lg", [P, NT, E])
        top = m.sb("top", [P, NT, E])
        idx = m.sb("idx", [P, NT, E], U32)
        ps = [m.pb(f"cps{k}", [P, T]) for k in range(4)]
        w_in = m.sem("wout_in")
        unit = Count(m.sem("cunit"), 4)
        t1_done = Count(m.sem("t1_done"), 1)
        y_done = Count(m.sem("y_donec"), 1)
        step = Count(m.sem("stepc"), norm_steps(NT) + 2 * NT + 2)
        held = m.sem("heldc")
        x2_done = Count(m.sem("x2_done"), NT)
        x2_kept = Count(m.sem("x2_kept"), 16)
        x2T_done = Count(m.sem("x2T_done"), 1)
        lg_done = Count(m.sem("lg_done"), 1)
        block = ctx.enter_context(nc.Block())

        @block.sync
        def _(sp):
            x2_kept.credit(sp)
            sp.dma_start(wout[:], I["Wout"].rearrange("(s p) n -> p s n", p=P)).then_inc(w_in, 16)
            with sp.Fori(0, B) as i:
                x2_done.now(sp, i, NT)
                sp.dma_start(C["x2all"][:, bass.ds(i * NT, NT), :], x2[:]).then_inc(x2_kept.sem, 16)
            sp.wait_ge(x2_kept.sem, 16 * (B + 1))

        @block.tensor
        def _(pe):
            unit.credit(pe)
            pe.wait_ge(w_in, 16)
            with pe.Fori(0, B) as i:
                t1_done.before(pe, i, 1)
                for s in range(PAIRS):
                    last = pe.matmul(ps[0][:], wout[:, s, :], C["oall"][:, bass.ds(i * PAIRS + s, 1), :].rearrange("p a n -> p (a n)"),
                                     start=(s == 0), stop=(s == PAIRS - 1))
                unit.done(last)
                t1_done.now(pe, i, 1)
                y_done.before(pe, i, 1)
                for t in range(NT):
                    last = pe.transpose(ps[1][:, t * P:(t + 1) * P], t1[:, t * P:(t + 1) * P], C["ident"][:])
                unit.done(last)
                x2_done.now(pe, i, NT)
                x2T_done.before(pe, i, 1)
                for t in range(NT):
                    last = pe.transpose(ps[2][:, t * P:(t + 1) * P], x2[:, t, :], C["ident"][:])
                unit.done(last)
                x2T_done.now(pe, i, 1)
                lg_done.before(pe, i, 1)
                for t in range(NT):
                    last = pe.matmul(ps[3][:, t * E:(t + 1) * E], x2T[:, t * P:(t + 1) * P], C["wg"][:], start=True, stop=True)
                unit.done(last)

        @block.scalar
        def _(act):
            x2T_done.credit(act)
            with act.Fori(0, B) as i:
                unit.now(act, i, 3)
                x2T_done.done(act.activation(x2T[:], ps[2][:], ACT.Copy))

        @block.vector
        def _(dve):
            for c in (t1_done, y_done, step, x2_done, lg_done):
                c.credit(dve)
            with dve.Fori(0, B) as i:
                unit.now(dve, i, 1)
                t1_done.done(dve.tensor_copy(t1[:], ps[0][:]))
                unit.now(dve, i, 2)
                y_done.done(dve.tensor_tensor(y[:], ps[1][:].rearrange("p (n d) -> p n d", n=NT),
                                              C["x1all"][:, bass.ds(i, 1), :, :].rearrange("p b n d -> p (b n) d"), ALU.add))
                y_done.now(dve, i, 1)
                yt = [y[:, t, :] for t in range(NT)]
                norm.moments(dve, i, step, held, yt)
                norm.roots(dve, i, step)
                x2_kept.before(dve, i, 16)
                norm.apply(dve, yt, [x2[:, t, :] for t in range(NT)], x2_done)
                unit.now(dve, i, 4)
                lg_done.done(dve.tensor_copy(lg[:], ps[3][:, 0:NT * E].rearrange("p (n e) -> p n e", n=NT)))
                lg_done.now(dve, i, 1)
                dve.sem_inc(held, 1)
                for t in range(NT):
                    step.done(dve.max(top[:, t, :], lg[:, t, :]))
                step.own(dve, i, held)
                for t in range(NT):
                    step.done(dve.max_index(idx[:, t, :], top[:, t, :], lg[:, t, :]))
                step.own(dve, i)
                step.done(dve.tensor_copy(C["topv"][:, :, bass.ds(i * NT, NT)], top[:, :, 0:2].rearrange("p n k -> p k n")))
                step.done(dve.tensor_copy(C["topi"][:, :, bass.ds(i * NT, NT)], idx[:, :, 0:2].rearrange("p n k -> p k n")))
                assert step.n == step.per


def route_stage(nc, I, C):
    K2 = 2 * TILES
    with ExitStack() as ctx:
        m = Mem(nc, ctx)
        eio = m.sb("eio", [P, E], U32)
        ef = m.sb("ef", [P, E])
        oh = m.sb("oh", [P, K2, E])
        tot = m.sb("tot", [P, K2, E])
        run = [m.sb(f"run{k}", [P, K2, E]) for k in range(2)]
        rank = m.sb("rank", [P, K2])
        over = m.sb("over", [P, K2])
        slotf = m.sb("slotf", [P, K2])
        e2 = m.sb("e2", [P, TILES])
        den = m.sb("denr", [P, TILES])
        ps_u = m.pb("ps_u", [P, K2, E])
        ps_t = m.pb("ps_t", [P, K2, E])
        pool_done = m.sem("pool_done")
        step = m.sem("stepr")
        oh_done = m.sem("oh_done")
        counted = m.sem("counted")
        diff_done = m.sem("diff_done")
        exp_done = m.sem("exp_done")
        slot_done = m.sem("slot_done")
        scattered = m.sem("scattered")
        block = ctx.enter_context(nc.Block())

        @block.gpsimd
        def _(pool):
            pool.iota(eio[:], pattern=[[1, E]], base=0, channel_multiplier=0).then_inc(pool_done, 1)
            pool.memset(C["yg"][:], 0.0).then_inc(pool_done, 1)
            pool.wait_ge(slot_done, 1)
            for k in range(2):
                for t in range(TILES):
                    n = k * TILES + t
                    pool.indirect_dma_start(C["xslots"], bass.IndirectOffsetOnAxis(ap=C["slot"][:, n:n + 1], axis=0),
                                            C["x2all"][:, t, :], None, bounds_check=SLOTS - 1,
                                            oob_is_err=False).then_inc(scattered, 16)
            pool.wait_ge(scattered, 16 * K2)

        @block.scalar
        def _(act):
            act.wait_ge(diff_done, 1)
            act.activation(e2[:], e2[:], ACT.Exp).then_inc(exp_done, 1)

        @block.tensor
        def _(pe):
            pe.wait_ge(oh_done, 1)
            flat = oh[:].rearrange("p n e -> p (n e)")
            pe.matmul(ps_u[:].rearrange("p n e -> p (n e)"), C["upper"][:], flat, start=True, stop=True)
            pe.matmul(ps_t[:].rearrange("p n e -> p (n e)"), C["ones"][:], flat, start=True, stop=True).then_inc(counted, 1)

        @block.vector
        def _(dve):
            n = [0]

            def then(ins):
                n[0] += 1
                ins.then_inc(step, 1)
                dve.wait_ge(step, n[0])

            topi = C["topi"][:].rearrange("p k n -> p (k n)")
            dve.tensor_tensor(e2[:], C["topv"][:, 1, :], C["topv"][:, 0, :], ALU.subtract).then_inc(diff_done, 1)
            dve.wait_ge(pool_done, 1)
            then(dve.tensor_copy(ef[:], eio[:]))
            dve.tensor_tensor(oh[:], topi.unsqueeze(2).broadcast_to([P, K2, E]), ef[:].unsqueeze(1).broadcast_to([P, K2, E]),
                              ALU.is_equal).then_inc(oh_done, 1)
            dve.wait_ge(counted, 1)
            then(dve.tensor_copy(tot[:], ps_t[:]))
            src, k, d = tot, 0, 1
            while d < K2:
                then(dve.tensor_copy(run[k][:, 0:d, :], src[:, 0:d, :]))
                then(dve.tensor_tensor(run[k][:, d:K2, :], src[:, d:K2, :], src[:, 0:K2 - d, :], ALU.add))
                src, k, d = run[k], 1 - k, 2 * d
            free = run[k]
            then(dve.tensor_tensor(src[:], src[:], tot[:], ALU.subtract))
            then(dve.tensor_tensor(free[:], ps_u[:], src[:], ALU.add))
            dve.wait_ge(oh_done, 1)
            then(dve.tensor_tensor(free[:], free[:], oh[:], ALU.mult))
            then(dve.tensor_reduce(rank[:], free[:], AX_X, ALU.add))
            then(dve.tensor_scalar(over[:], rank[:], float(CAP), None, ALU.is_ge))
            then(dve.scalar_tensor_tensor(out=slotf[:], in0=topi, scalar=float(CAP), in1=rank[:], op0=ALU.mult, op1=ALU.add))
            then(dve.scalar_tensor_tensor(out=slotf[:], in0=over[:], scalar=DROPPED, in1=slotf[:], op0=ALU.mult, op1=ALU.add))
            dve.tensor_copy(C["slot"][:], slotf[:]).then_inc(slot_done, 1)
            dve.wait_ge(exp_done, 1)
            then(dve.tensor_scalar(den[:], e2[:], 1.0, None, ALU.add))
            then(dve.reciprocal(C["wt"][:, 0:TILES], den[:]))
            then(dve.tensor_tensor(C["wt"][:, TILES:K2], C["wt"][:, 0:TILES], e2[:], ALU.mult))
            then(dve.tensor_scalar(over[:], over[:], -1.0, 1.0, ALU.mult, ALU.add))
            then(dve.tensor_tensor(C["wt"][:], C["wt"][:], over[:], ALU.mult))


def expert_stage(nc, I, C):
    N2 = CAP // 2
    with ExitStack() as ctx:
        m = Mem(nc, ctx)
        xe = [m.sb(f"xe{s}", [P, ST, D]) for s in range(2)]
        wf = [m.sb(f"wf{s}", [P, FF]) for s in range(2)]
        wp = [m.sb(f"wp{s}", [P, FC, D]) for s in range(2)]
        xeT = [m.sb(f"xeT{s}", [P, CAP]) for s in range(2)]
        hT = m.sb("hT", [P, FC, CAP])
        ye = [m.sb(f"ye{s}", [P, ST, D]) for s in range(2)]
        ps_x = m.pb("ps_x", [P, 2, T])
        ps_h = [m.pb(f"ps_h{k}", [P, 2, T]) for k in range(2)]
        ps_y = m.pb("ps_y", [P, 2, T])
        x_in = [m.sem(f"xe_in{s}") for s in range(2)]
        w_in = [m.sem(f"we_in{s}") for s in range(2)]
        turned = Count(m.sem("turned_e"), 1, 2)
        xeT_done = Count(m.sem("xeT_done"), 2, 2)
        h_done = Count(m.sem("h_done"), FC, 2)
        act_done = Count(m.sem("act_done"), FC, 2)
        y_done = Count(m.sem("y_done_e"), 1, 2)
        y_out = Count(m.sem("y_out"), 2, 2)
        y_kept = [Count(m.sem(f"y_kept{s}"), 16, 1) for s in range(2)]
        block = ctx.enter_context(nc.Block())

        def turns(eng, body):
            with eng.Fori(0, E // 2) as i:
                body(2 * i, 0, i)
                body(2 * i + 1, 1, i)

        @block.sync
        def _(sp):
            def load(e, s, i):
                turned.before(sp, e, 1, 2)
                sp.dma_start(xe[s][:], C["xslots"].rearrange("(e n p) d -> e p n d", p=P, n=ST)[bass.ds(e, 1)]
                             .rearrange("e p n d -> p (e n) d")).then_inc(x_in[s], 16)
                y_done.before(sp, e, 1, 2)
                sp.dma_start(wf[s][:], I["c_fc"][bass.ds(e, 1)].rearrange("e p n -> p (e n)")).then_inc(w_in[s], 16)
                sp.dma_start(wp[s][:], I["c_proj"][bass.ds(e, 1)].rearrange("e (c p) d -> p (e c) d", p=P)).then_inc(w_in[s], 16)

            turns(sp, load)

        @block.gpsimd
        def _(pool):
            for c in y_kept:
                c.credit(pool)

        @block.tensor
        def _(pe):
            for c in (turned, h_done, y_done):
                c.credit(pe)

            def expert(e, s, i):
                pe.wait_ge(x_in[s], 16 * (i + 1))
                xeT_done.before(pe, e, 2)
                for t in range(ST):
                    last = pe.transpose(ps_x[:, t // NT, (t % NT) * P:(t % NT) * P + P], xe[s][:, t, :], C["ident"][:])
                turned.done(last)
                pe.wait_ge(w_in[s], 32 * (i + 1))
                xeT_done.now(pe, e, 2)
                for c in range(FC):
                    act_done.now(pe, e, c - 1) if c >= 2 else act_done.before(pe, e, FC - 1 + c)
                    for k in range(2):
                        last = pe.matmul(ps_h[c % 2][:, k, 0:N2], wf[s][:, c * P:(c + 1) * P], xeT[s][:, k * N2:(k + 1) * N2],
                                         start=True, stop=True)
                    h_done.done(last)
                act_done.now(pe, e, FC)
                y_out.before(pe, e, 2)
                for t in range(ST):
                    for c in range(FC):
                        last = pe.matmul(ps_y[:, t // NT, (t % NT) * P:(t % NT) * P + P], hT[:, c, t * P:(t + 1) * P],
                                         wp[s][:, c, :], start=(c == 0), stop=(c == FC - 1))
                y_done.done(last)

            turns(pe, expert)

        @block.scalar
        def _(act):
            for c in (act_done,):
                c.credit(act)

            def expert(e, s, i):
                for c in range(FC):
                    h_done.now(act, e, c + 1)
                    if c == 0:
                        y_done.before(act, e, 1)
                    act_done.done(act.activation(hT[:, c, :].rearrange("p (k n) -> p k n", k=2), ps_h[c % 2][:, :, 0:N2], ACT.Gelu))
                y_out.now(act, e, 2)
                act.dma_start(C["yslots"].rearrange("(e n p) d -> e p n d", p=P, n=ST)[bass.ds(e, 1)]
                              .rearrange("e p n d -> p (e n) d"), ye[s][:]).then_inc(y_kept[s].sem, 16)

            turns(act, expert)
            for c in y_kept:
                act.wait_ge(c.sem, 16 * (E // 2 + 1))

        @block.vector
        def _(dve):
            for c in (xeT_done, y_out):
                c.credit(dve)

            def expert(e, s, i):
                turned.now(dve, e, 1)
                xeT_done.done(dve.tensor_copy(xeT[s][:, 0:T], ps_x[:, 0, :]))
                xeT_done.done(dve.tensor_copy(xeT[s][:, T:CAP], ps_x[:, 1, 0:CAP - T]))
                y_done.now(dve, e, 1)
                y_kept[s].before(dve, i, 16)
                y_out.done(dve.tensor_copy(ye[s][:, 0:NT, :], ps_y[:, 0, :].rearrange("p (n d) -> p n d", n=NT)))
                y_out.done(dve.tensor_copy(ye[s][:, NT:ST, :], ps_y[:, 1:2, 0:D]))

            turns(dve, expert)


def combine_stage(nc, I, C, out):
    with ExitStack() as ctx:
        m = Mem(nc, ctx)
        y = m.sb("yf", [P, TILES, D])
        z = m.sb("zf", [P, TILES, D])
        norm = Norm(m, "x3", NT)
        got = [m.sem(f"got{b}") for b in range(B)]
        step = Count(m.sem("stepf"), 2 * NT + norm_steps(NT))
        held = m.sem("heldf")
        z_done = Count(m.sem("z_done"), NT)
        stored = m.sem("storedf")
        block = ctx.enter_context(nc.Block())

        @block.gpsimd
        def _(pool):
            for b in range(B):
                for k in range(2):
                    for t in range(b * NT, (b + 1) * NT):
                        n = k * TILES + t
                        pool.indirect_dma_start(C["yg"][:, n, :], None, C["yslots"],
                                                bass.IndirectOffsetOnAxis(ap=C["slot"][:, n:n + 1], axis=0),
                                                bounds_check=SLOTS - 1, oob_is_err=False).then_inc(got[b], 16)

        @block.sync
        def _(sp):
            for b in range(B):
                z_done.now(sp, b, NT)
                sp.dma_start(out[b].rearrange("(n p) d -> p n d", p=P), z[:, b * NT:(b + 1) * NT, :]).then_inc(stored, 16)
            sp.wait_ge(stored, 16 * B)

        @block.vector
        def _(dve):
            for c in (step, z_done):
                c.credit(dve)
            for b in range(B):
                dve.wait_ge(got[b], 16 * 2 * NT)
                for k in range(2):
                    for t in range(b * NT, (b + 1) * NT):
                        n = k * TILES + t
                        step.done(dve.scalar_tensor_tensor(out=y[:, t, :], in0=C["yg"][:, n, :], scalar=C["wt"][:, n:n + 1],
                                                           in1=C["x2all"][:, t, :] if k == 0 else y[:, t, :],
                                                           op0=ALU.mult, op1=ALU.add))
                    step.own(dve, b)
                yt = [y[:, t, :] for t in range(b * NT, (b + 1) * NT)]
                if b:
                    z_done.before(dve, b, NT)
                norm.moments(dve, b, step, held, yt)
                norm.roots(dve, b, step)
                norm.apply(dve, yt, [z[:, t, :] for t in range(b * NT, (b + 1) * NT)], z_done)


def common(m):
    C = {}
    C["ident"] = m.sb("ident", [P, P])
    C["ident_b"] = m.sb("ident_b", [P, P], BF16)
    C["mask"] = m.sb("mask", [P, P], BF16)
    C["maskT"] = m.sb("maskT", [P, P], BF16)
    C["ones"] = m.sb("ones", [P, P])
    C["upper"] = m.sb("upper", [P, P])
    C["gb"] = m.sb("gb", [P, 4])
    C["wg"] = m.sb("wg", [P, E])
    C["x1all"] = m.sb("x1all", [P, B, NT, D])
    C["kv_hi"], C["kv_lo"] = m.split("kvall", [P, B, KEYS_E])
    return C


def self_common(m, C):
    C["aq_hi"], C["aq_lo"] = m.split("aq", [P, HS, P])
    C["wk_hi"], C["wk_lo"] = m.split("wk", [P, KVS, P])
    C["wv_hi"], C["wv_lo"] = m.split("wv", [P, HX * DH])
    C["wvd"] = m.sb("wvd", [P, KVS * DL])
    C["bo"] = m.sb("bo", [P, KVS, D])
    C["xall"] = m.sb("xall", [P, TILES, D])
    C["stage_hi"], C["stage_lo"] = m.split("stage", [P, 2, HX, DH])
    C["zero"] = m.sb("zero", [P, 8, P])
    C["stored"] = m.sem("stored")


def decoder(nc, I, out):
    with ExitStack() as ctx:
        m = Mem(nc, ctx)
        C = common(m)
        late_common(m, C)
        dram = lambda name, shape, dt=F32: nc.dram_tensor(name, shape, dt, kind="Internal").ap()
        C["xslots"] = dram("xslots", (SLOTS, D))
        C["yslots"] = dram("yslots", (SLOTS, D))
        C["wpair"] = dram("wpair", (PAIRS, P, 2, 2, P), F32R)
        C["vals"] = dram("vals", (B, PAIRS, P, KC, P))
        with ExitStack() as early:
            self_common(Mem(nc, early), C)
            setup_stage(nc, I, C)
            self_stage(nc, I, C)
        with ExitStack() as mid:
            C["oall"] = Mem(nc, mid).sb("oall", [P, STEPS, T])
            cross_stage(nc, I, C)
            close_stage(nc, I, C)
        C["yg"] = m.sb("yg", [P, 2 * TILES, D])
        route_stage(nc, I, C)
        expert_stage(nc, I, C)
        combine_stage(nc, I, C, out)


def late_common(m, C):
    C["x2all"] = m.sb("x2all", [P, TILES, D])
    C["topv"] = m.sb("topv", [P, 2, TILES])
    C["topi"] = m.sb("topi", [P, 2, TILES])
    C["slot"] = m.sb("slot", [P, 2 * TILES], U32)
    C["wt"] = m.sb("wt", [P, 2 * TILES])


INPUTS = {"x": "x", "ctx_1024": "ctx", "L0_attn_wq": "wq", "L0_attn_wk_down": "wk_down", "L0_attn_wv_down": "wv_down",
          "L0_attn_wk_up": "wk_up", "L0_attn_wv_up": "wv_up", "L0_attn_wo": "wo", "L0_xattn_ln_m_g": "ln_m_g",
          "L0_xattn_ln_m_b": "ln_m_b", "L0_xattn_ln_l_g": "ln_l_g", "L0_xattn_ln_l_b": "ln_l_b", "L0_xattn_Wq": "Wq",
          "L0_xattn_Wkv": "Wkv", "L0_xattn_Wout": "Wout", "L0_ffn_w_g": "w_g", "L0_ffn_c_fc": "c_fc",
          "L0_ffn_c_proj": "c_proj"}


def kernel(**inputs):
    import numpy as np
    import concourse.bacc as bacc
    from concourse import mybir as mb
    from concourse.bass_utils import run_bass_kernel_spmd

    nc = bacc.Bacc("TRN2", target_bir_lowering=False, num_devices=1)
    arrays, I = {}, {}
    for name, short in INPUTS.items():
        a = np.ascontiguousarray(inputs[name])
        arrays[f"in_{name}"] = a
        I[short] = nc.dram_tensor(f"in_{name}", a.shape, mb.dt.from_np(a.dtype), kind="ExternalInput").ap()
    out = nc.dram_tensor("out_0", (B, T, D), F32, kind="ExternalOutput").ap()
    decoder(nc, I, out)
    return run_bass_kernel_spmd(nc, [arrays], core_ids=[0]).results[0]["out_0"]
```

```python
from contextlib import ExitStack

import concourse.bass as bass
from concourse import mybir

ALU = mybir.AluOpType
ACT = mybir.ActivationFunctionType
AX_X = mybir.AxisListType.X
F32 = mybir.dt.float32
F32R = mybir.dt.float32r
BF16 = mybir.dt.bfloat16
U32 = mybir.dt.uint32
I32 = mybir.dt.int32

P = 128
B = 4
T = 512
D = 128
NT = T // P
TILES = B * NT
EPS = 1e-5
INPUTS_AT = 3
VALUES_AT = {4: (0,), 5: (1,), 6: (2, 3), 7: (4, 5)}
VOUTS = 3

HS, KVS, REP, DL = 8, 2, 4, 32
SELF_SCALE = float(D) ** -0.5
SHIFT_ROW = 3 * DL
SELF_N = [T - P * j for j in range(NT)]
SELF_AT = [sum(SELF_N[:j]) for j in range(NT)]
SELF_W = sum(SELF_N)
MASKED = -1.0e30

HX, DH = 16, 64
CROSS_SCALE = float(DH) ** -0.5
CTX = 154
CTX_TAIL = CTX - P
KEYS = T + CTX
KEYS_E = KEYS + 2
HALF = KEYS_E // 2
KC = (KEYS + P - 1) // P
KPAD = KC * P
TAIL = KEYS - (KC - 1) * P
PAIRS = HX // 2
STEPS = B * PAIRS

E, FF = 8, 512
FC = FF // P
CAP = 640
SLOTS = E * CAP
ST = CAP // P
ROW = D + 2
SETUP_STORES = E + B + 4 + 4
DROPPED = 8192.0

RING = 4
TAIL_RING = 2
ROOT_MAGIC = float(0x5F3759DF - (1 << 22) - (1 << 31))


def norm_steps(tiles):
    return 2 * tiles + 11


class Names:

    def __init__(self, names, ring):
        self.names = names
        self.at = {n: k for k, n in enumerate(names)}
        self.n = len(names)
        self.ring = ring

    def bank(self, name):
        return self.at[name] % self.ring

    def before(self, name):
        k = self.at[name]
        if k >= self.ring:
            return self.names[k - self.ring], False
        return self.names[max(x for x in range(self.n) if x % self.ring == k)], True


def f(ap):
    return ap.bitcast(F32)


class Mem:

    def __init__(self, nc, ctx):
        self.nc, self.ctx = nc, ctx

    def sb(self, name, shape, dt=F32):
        return self.ctx.enter_context(self.nc.sbuf_tensor(name, shape, dt))

    def pb(self, name, shape):
        return self.ctx.enter_context(self.nc.psum_tensor(name, shape, F32))

    def sem(self, name):
        return self.ctx.enter_context(self.nc.semaphore(name))

    def split(self, name, shape):
        return self.sb(name + "_hi", shape, F32R), self.sb(name + "_lo", shape, F32R)


def setup_stage(nc, I, C):
    with ExitStack() as ctx:
        m = Mem(nc, ctx)
        wq = m.sb("wq", [P, HS * D])
        wkd = m.sb("wkd", [P, KVS * DL])
        wku = m.sb("wku", [DL, D])
        wvu = m.sb("wvu", [DL, D])
        wo = m.sb("wo", [P, HS, D])
        cq = m.sb("cq", [P, HX * DH])
        ckv = m.sb("ckv", [P, 2 * HX * DH])
        wqT = m.sb("wqT", [P, HS, P])
        upT = m.sb("upT", [P, 2, DL])
        stage_hi, stage_lo, zero, empty, stored = (C[k] for k in ("stage_hi", "stage_lo", "zero", "empty", "stored"))
        pq = [m.pb(f"pq{k}", [P, 4, P]) for k in range(2)]
        pu = m.pb("pu", [P, 2, DL])
        pa = m.pb("pa", [P, HS, DL])
        pv = m.pb("pv", [P, KVS, D])
        loaded = m.sem("loaded")
        loaded_self = m.sem("loaded_self")
        consts = m.sem("consts")
        turned = m.sem("turned")
        copied = m.sem("copied")
        high = m.sem("high")
        low = m.sem("low")
        combined = m.sem("combined")
        block = ctx.enter_context(nc.Block())

        @block.sync
        def _(sp):
            sp.dma_start(wq[:], I["wq"]).then_inc(loaded_self, 16)
            sp.dma_start(wku[:], I["wk_up"]).then_inc(loaded_self, 16)
            sp.dma_start(wvu[:], I["wv_up"]).then_inc(loaded_self, 16)
            sp.dma_start(wo[:], I["wo"].rearrange("(h p) n -> p h n", p=P)).then_inc(loaded_self, 16)
            sp.dma_start(wkd[:], I["wk_down"]).then_inc(loaded_self, 16)
            sp.dma_start(C["wvd"][:], I["wv_down"]).then_inc(loaded_self, 16)
            sp.dma_start(cq[:], I["Wq"]).then_inc(loaded, 16)
            sp.dma_start(ckv[:], I["Wkv"]).then_inc(loaded, 16)
            sp.dma_start(C["xall"][:], I["x"].rearrange("b (n p) d -> p (b n) d", p=P)).then_inc(loaded, 16)
            sp.dma_start(C["wg"][:], I["w_g"]).then_inc(loaded, 16)
            sp.wait_ge(consts, 3)
            for e in range(E):
                sp.dma_start(C["xslots"][e * CAP:(e + 1) * CAP, :].rearrange("(n p) d -> p n d", p=P),
                             empty[:]).then_inc(stored, 16)
            for k in range(4):
                sp.dma_start(C["yrows"][k * 8 * P:(k + 1) * 8 * P, :].rearrange("(n p) d -> p n d", p=P),
                             zero[:]).then_inc(stored, 16)
            for b in range(B):
                sp.dma_start(C["vals"][b, :, TAIL:P, KC - 1, :].rearrange("s p c -> p s c"),
                             zero[0:P - TAIL, 0:PAIRS, :]).then_inc(stored, 16)
            sp.wait_ge(high, 2)
            sp.wait_ge(low, 2)
            for part, src in enumerate((stage_hi, stage_lo)):
                for kind in range(2):
                    sp.dma_start(f(C["wpair"][:, :, part, kind, :]).rearrange("s p c -> p s c"),
                                 f(src[:, kind, :, :]).rearrange("p (s h) c -> p s (h c)", h=2)).then_inc(stored, 16)

        @block.gpsimd
        def _(pool):
            pool.dma_start(C["xs"][:], I["x"][0].rearrange("(n p) d -> p n d", p=P)).then_inc(C["x_in"], 16)
            pool.memset(zero[:], 0.0).then_inc(consts, 1)
            pool.memset(empty[:, :, 0:D + 1], 0.0).then_inc(consts, 1)
            pool.memset(empty[:, :, D + 1:ROW], 1.0).then_inc(consts, 1)
            pool.memset(C["ident"][:], 0.0).then_inc(consts, 1)
            pool.memset(C["mask"][:], 0.0).then_inc(consts, 1)
            pool.memset(C["maskT"][:], 0.0).then_inc(consts, 1)
            pool.memset(C["ones"][:], 1.0).then_inc(consts, 1)
            pool.memset(C["upper"][:], 0.0).then_inc(consts, 1)
            pool.iota(C["expert_u"][:], pattern=[[1, E]], base=0, channel_multiplier=0).then_inc(consts, 1)
            pool.memset(C["aq_hi"][:].bitcast(F32), 0.0).then_inc(consts, 1)
            pool.memset(C["aq_lo"][:].bitcast(F32), 0.0).then_inc(consts, 1)
            pool.memset(C["wk_hi"][:].bitcast(F32), 0.0).then_inc(consts, 1)
            pool.memset(C["wk_lo"][:].bitcast(F32), 0.0).then_inc(consts, 1)
            pool.wait_ge(consts, 13)
            pool.affine_select(out=C["ident"][:], in_=C["ident"][:], compare_op=ALU.not_equal, fill=1.0, base=0,
                               pattern=[[-1, P]], channel_multiplier=1).then_inc(consts, 1)
            pool.affine_select(out=C["mask"][:], in_=C["mask"][:], compare_op=ALU.is_ge, fill=MASKED, base=0,
                               pattern=[[-1, P]], channel_multiplier=1).then_inc(consts, 1)
            pool.affine_select(out=C["maskT"][:], in_=C["maskT"][:], compare_op=ALU.is_ge, fill=MASKED, base=0,
                               pattern=[[1, P]], channel_multiplier=-1).then_inc(consts, 1)
            pool.affine_select(out=C["upper"][:], in_=C["upper"][:], compare_op=ALU.is_ge, fill=1.0, base=0,
                               pattern=[[-1, P]], channel_multiplier=1).then_inc(consts, 1)
            pool.wait_ge(consts, 17)
            pool.tensor_copy(C["ident_b"][:], C["ident"][:]).then_inc(consts, 1)
            pool.tensor_copy(C["expert"][:], C["expert_u"][:]).then_inc(consts, 1)
            kop, zeroed = C["kop"], C["zeroed"]
            pool.memset(C["nmax"][:], 0.0).then_inc(zeroed, 1)
            pool.memset(f(C["kvT_hi"][:, KEYS_E:KPAD]), 0.0).then_inc(zeroed, 1)
            pool.memset(f(C["kvT_lo"][:, KEYS_E:KPAD]), 0.0).then_inc(zeroed, 1)
            pool.memset(C["norm1"].mv[:], 0.0).then_inc(zeroed, 1)
            pool.wait_ge(zeroed, 4)
            pool.memset(f(kop[SHIFT_ROW:P, :, :]), 0.0).then_inc(zeroed, 1)
            pool.wait_ge(zeroed, 5)
            pool.memset(f(kop[SHIFT_ROW:SHIFT_ROW + 1, :, :]), 1.0).then_inc(zeroed, 1)

        @block.tensor
        def _(pe):
            pe.wait_ge(consts, 17)
            pe.wait_ge(loaded_self, 16 * 6)
            for h in range(HS):
                t = pe.transpose(pq[h // 4][:, h % 4, :], wq[:, h * D:(h + 1) * D], C["ident"][:])
                if h % 4 == 3:
                    t.then_inc(turned, 1)
            pe.transpose(pu[:, 0, :], wku[:], C["ident"][0:DL, 0:DL])
            pe.transpose(pu[:, 1, :], wvu[:], C["ident"][0:DL, 0:DL]).then_inc(turned, 1)
            pe.wait_ge(copied, 3)
            for h in range(HS):
                t = pe.matmul(pa[:, h, :], wqT[:, h, :], upT[:, 0, :], start=True, stop=True)
            t.then_inc(combined, 1)
            for h in range(HS):
                t = pe.matmul(pv[DL * (h % REP):DL * (h % REP) + DL, h // REP, :], upT[:, 1, :], wo[:, h, :],
                              start=True, stop=True)
            t.then_inc(combined, 1)

        @block.vector
        def _(dve):
            for k in range(2):
                dve.wait_ge(turned, k + 1)
                dve.tensor_copy(wqT[:, 4 * k:4 * k + 4, :], pq[k][:]).then_inc(copied, 1)
            dve.wait_ge(turned, 3)
            dve.tensor_copy(upT[:], pu[:]).then_inc(copied, 1)
            dve.wait_ge(loaded, 16 * 8)
            for kind, src in enumerate((cq[:], ckv[:, 0:HX * DH])):
                dve.wait_ge(high, kind + 1)
                dve.tensor_tensor(stage_lo[:, kind, :, :], src.rearrange("p (h c) -> p h c", c=DH),
                                  f(stage_hi[:, kind, :, :]), ALU.subtract).then_inc(low, 1)
            dve.wait_ge(high, 3)
            dve.tensor_tensor(C["wv_lo"][:], ckv[:, HX * DH:], f(C["wv_hi"][:]), ALU.subtract).then_inc(low, 1)
            dve.wait_ge(combined, 1)
            dve.wait_ge(consts, 13)
            for c in range(3):
                dve.wait_ge(high, 6)
                dve.tensor_tensor(C["aq_lo"][:, :, c * DL:(c + 1) * DL], pa[:], f(C["aq_hi"][:, :, c * DL:(c + 1) * DL]),
                                  ALU.subtract).then_inc(low, 1)
            for c in range(3):
                dve.wait_ge(high, 7 + c)
                dve.tensor_tensor(C["wk_lo"][:, :, c * DL:(c + 1) * DL], wkd[:].rearrange("p (g l) -> p g l", l=DL),
                                  f(C["wk_hi"][:, :, c * DL:(c + 1) * DL]), ALU.subtract).then_inc(low, 1)
            dve.wait_ge(combined, 2)
            dve.tensor_copy(C["bo"][:], pv[:]).then_inc(low, 1)

        @block.scalar
        def _(act):
            for k, name in enumerate(("ln_l_g", "ln_l_b", "ln_m_g", "ln_m_b")):
                act.dma_start(C["gb"][:, k:k + 1], I[name].rearrange("(p a) -> p a", a=1)).then_inc(loaded, 16)
            act.wait_ge(loaded, 16 * 8)
            for kind, src in enumerate((cq[:], ckv[:, 0:HX * DH])):
                act.activation(stage_hi[:, kind, :, :], src.rearrange("p (h c) -> p h c", c=DH),
                               ACT.Copy).then_inc(high, 1)
            act.activation(C["wv_hi"][:], ckv[:, HX * DH:], ACT.Copy).then_inc(high, 1)
            act.wait_ge(combined, 1)
            act.wait_ge(consts, 13)
            for c in range(3):
                act.activation(C["aq_hi"][:, :, c * DL:(c + 1) * DL], pa[:], ACT.Copy).then_inc(high, 1)
            act.wait_ge(loaded_self, 16 * 6)
            for c in range(3):
                act.activation(C["wk_hi"][:, :, c * DL:(c + 1) * DL],
                               wkd[:].rearrange("p (g l) -> p g l", l=DL), ACT.Copy).then_inc(high, 1)


SELF_UNITS = Names(
    ["xT", "k0", "k1", "q0", "q1", "ma0", "mb0", "mc0", "v"]
    + [u for h in range(HS)
       for u in [f"t{h}"] + ([f"q{h + 2}"] if h + 2 < HS else []) + ([f"m{c}{h + 1}" for c in "abc"] if h + 1 < HS else [])
       + [f"s{h}_{j}" for j in range(NT)]], RING)
TAIL_UNITS = Names(["y", "lT", "cT"] + [f"V{c}_{k}" for c in range(KC) for k in range(2)], TAIL_RING)


class Count:

    def __init__(self, sem, per, ahead=1):
        self.sem, self.per, self.ahead, self.n = sem, per, ahead, 0

    def credit(self, eng):
        eng.sem_inc(self.sem, self.per * self.ahead)

    def now(self, eng, i, k):
        eng.wait_ge(self.sem, (i + self.ahead) * self.per + k)

    def before(self, eng, i, k, turns=1):
        eng.wait_ge(self.sem, (i + self.ahead - turns) * self.per + k)

    def done(self, ins):
        self.n += 1
        ins.then_inc(self.sem, 1)

    def own(self, eng, i, at=None):
        eng.wait_ge(self.sem, (i + self.ahead) * self.per + (self.n - 1) % self.per + 1)
        if at is not None:
            eng.sem_inc(at, 1)


class Norm:

    def __init__(self, m, name, tiles, twice=0):
        self.n, self.twice = tiles, twice
        self.stats = m.sb("stats_" + name, [P, tiles, 6])
        self.mv = m.sb("mv_" + name, [P, tiles, 2])
        self.half = m.sb("half_" + name, [P, tiles + twice])
        self.root = m.sb("root_" + name, [P, tiles + twice])
        self.tmp = m.sb("tmp_" + name, [P, tiles + twice])

    def moments(self, dve, i, step, held, tiles):
        for k, t in enumerate(tiles):
            step.done(dve.bn_stats(self.stats[0:t.shape[0], k, :], t))
        step.own(dve, i, held)
        for k, t in enumerate(tiles):
            step.done(dve.bn_aggr(self.mv[0:t.shape[0], k, :], self.stats[0:t.shape[0], k, :]))
        step.own(dve, i)
        step.done(dve.tensor_scalar(self.half[:, 0:self.n], self.mv[:, :, 1], EPS, 0.5, ALU.add, ALU.mult))
        if self.twice:
            step.done(dve.tensor_scalar(self.half[:, self.n:], self.mv[:, 0:self.twice, 1], 0.5 * (1.0 + EPS), 0.5 * EPS * EPS,
                                        ALU.mult, ALU.add))
        step.own(dve, i)

    def roots(self, dve, i, step):
        r, h, a = self.root, self.half, self.tmp
        step.done(dve.tensor_scalar(r[:].bitcast(I32), h[:].bitcast(I32), -0.5, ROOT_MAGIC, ALU.mult, ALU.add))
        step.own(dve, i)
        for _ in range(3):
            step.done(dve.tensor_tensor(a[:], r[:], r[:], ALU.mult))
            step.own(dve, i)
            step.done(dve.tensor_tensor(a[:], a[:], h[:], ALU.mult))
            step.own(dve, i)
            step.done(dve.scalar_tensor_tensor(out=r[:], in0=a[:], scalar=1.5, in1=r[:], op0=ALU.subtract, op1=ALU.mult))
            step.own(dve, i)

    def apply(self, dve, tiles, outs, done, first=0, again=False):
        for k, (t, o) in enumerate(zip(tiles, outs), first):
            n, r = t.shape[0], k + self.n * again
            done.done(dve.tensor_scalar(o, t, self.mv[0:n, k, 0:1], self.root[0:n, r:r + 1], ALU.subtract, ALU.mult))


def self_stage(nc, I, C):
    U, W = SELF_UNITS, TAIL_UNITS
    with ExitStack() as ctx:
        m = Mem(nc, ctx)
        xs, kop, nmax, norm1, kvT_hi, kvT_lo = (C[k] for k in ("xs", "kop", "nmax", "norm1", "kvT_hi", "kvT_lo"))
        cs = m.sb("cs", [P, 2, D])
        xT = m.sb("xT", [P, T])
        xT_hi, xT_lo = m.split("xTs", [P, T])
        qop = m.sb("qop", [P, 4, T], F32R)
        vlat = m.sb("vlat", [P, NT, KVS * DL])
        probs = m.sb("probs", [P, HS, SELF_W])
        rden = m.sb("rden", [P, T])
        oT = m.sb("oT", [P, KVS, T])
        y = m.sb("y", [P, NT, D])
        x1 = m.sb("x1", [P, NT, D])
        lat = m.sb("lat", [P, NT, D])
        cn = m.sb("cn", [P, 2, D])
        kvf = m.sb("kvf", [P, KEYS_E])
        vout = m.sb("vout", [P, VOUTS, HX * DH])
        ring = [m.pb(f"ring{k}", [P, T]) for k in range(RING)]
        tail_ring = [m.pb(f"tail_ring{k}", [P, T]) for k in range(TAIL_RING)]
        o_ps = m.pb("o_ps", [P, T])
        den_ps = m.pb("den_ps", [P, T])

        x_in, zeroed = C["x_in"], C["zeroed"]
        c_in = m.sem("c_in")
        unit = Count(m.sem("unit"), U.n)
        tail_unit = Count(m.sem("tail_unit"), W.n)
        high = Count(m.sem("high"), 3 + HS)
        low = Count(m.sem("low"), 3 + HS)
        xT_done = Count(m.sem("xT_done"), 1)
        vlat_done = Count(m.sem("vlat_done"), 1)
        max_done = Count(m.sem("max_done"), 3 * HS)
        row_done = Count(m.sem("row_done"), HS)
        probs_done = Count(m.sem("probs_done"), NT * HS)
        o_done = Count(m.sem("o_done"), KVS)
        sum_done = Count(m.sem("sum_done"), KVS)
        rden_done = Count(m.sem("rden_done"), KVS)
        oT_done = Count(m.sem("oT_done"), KVS)
        y_done = Count(m.sem("y_done"), 1)
        step = Count(m.sem("step"), HS)
        tail_step = Count(m.sem("tail_step"), norm_steps(NT + 2) + 2)
        held = m.sem("held")
        x1_done = Count(m.sem("x1_done"), NT)
        x1_kept = Count(m.sem("x1_kept"), 16)
        lat_done = Count(m.sem("lat_done"), NT)
        cn_done = Count(m.sem("cn_done"), 2)
        kv_full = Count(m.sem("kv_full"), 2)
        kv_high = Count(m.sem("kv_high"), 2)
        kv_low = Count(m.sem("kv_low"), 2)
        kv_kept = Count(m.sem("kv_kept"), 32)
        v_act = Count(m.sem("v_act"), KC)
        v_dve = Count(m.sem("v_dve"), KC)
        v_kept = [Count(m.sem(f"v_kept{k}"), 16 * KC // VOUTS) for k in range(VOUTS)]
        block = ctx.enter_context(nc.Block())

        readers = {"xT": (xT_done, 1), "k0": (low, 2), "k1": (low, 3), "v": (vlat_done, 1), "y": (y_done, 1),
                   "lT": (kv_full, 1), "cT": (kv_full, 2)}
        for h in range(HS):
            readers[f"q{h}"] = (low, 4 + h)
            readers[f"t{h}"] = (row_done, 1 + h)
            for k, c in enumerate("abc"):
                readers[f"m{c}{h}"] = (max_done, 3 * h + k + 1)
            for j in range(NT):
                readers[f"s{h}_{j}"] = (probs_done, NT * h + j + 1)
        for c in range(KC):
            readers[f"V{c}_0"] = (v_act, c + 1)
            readers[f"V{c}_1"] = (v_dve, c + 1)

        def at_unit(eng, i, name):
            unit.now(eng, i, U.at[name] + 1)

        def at_tail(eng, i, name):
            tail_unit.now(eng, i, W.at[name] + 1)

        def ps(name):
            return ring[U.bank(name)]

        def tail_ps(name):
            return tail_ring[W.bank(name)]

        def vout_free(eng, i, c):
            kept = v_kept[c % VOUTS]
            kept.now(eng, i, 16 * (c // VOUTS)) if c >= VOUTS else kept.before(eng, i, kept.per)

        def turns(eng, body, tail):
            body(0, first=True)
            with eng.Fori(1, B) as i:
                body(i)
            tail(B - 1)

        @block.gpsimd
        def _(pool):
            def context(i):
                pool.dma_start(cs[:, 0, :], I["ctx"][bass.ds(i, 1), 0:P, :].rearrange("b p d -> p (b d)")).then_inc(c_in, 16)
                pool.dma_start(cs[0:CTX_TAIL, 1, :],
                               I["ctx"][bass.ds(i, 1), P:CTX, :].rearrange("b p d -> p (b d)")).then_inc(c_in, 16)

            context(0)
            with pool.Fori(1, B) as i:
                unit.before(pool, i, U.at["xT"] + 1)
                pool.dma_start(xs[:], I["x"][bass.ds(i, 1), :, :].rearrange("b (n p) d -> p (b n) d", p=P)).then_inc(x_in, 16)
                cn_done.before(pool, i, 2)
                context(i)

        @block.sync
        def _(sp):
            for c in (x1_kept, kv_kept, *v_kept):
                c.credit(sp)
            with sp.Fori(0, B) as i:
                x1_done.now(sp, i, NT)
                sp.dma_start(C["x1all"][:, bass.ds(i, 1), :, :], x1[:, None, :, :]).then_inc(x1_kept.sem, 16)
                kv_high.now(sp, i, 2)
                kv_low.now(sp, i, 2)
                sp.dma_start(f(C["kv_hi"][:, bass.ds(i, 1), :]), f(kvT_hi[:, None, 0:KEYS_E])).then_inc(kv_kept.sem, 16)
                sp.dma_start(f(C["kv_lo"][:, bass.ds(i, 1), :]), f(kvT_lo[:, None, 0:KEYS_E])).then_inc(kv_kept.sem, 16)
                for c in range(KC):
                    n = P if c < KC - 1 else TAIL
                    v_act.now(sp, i, c + 1)
                    v_dve.now(sp, i, c + 1)
                    sp.dma_start(C["vals"][bass.ds(i, 1), :, 0:n, c, :].rearrange("b s p c -> p (b s) c"),
                                 vout[0:n, c % VOUTS, :].rearrange("p (s c) -> p s c", s=PAIRS)).then_inc(v_kept[c % VOUTS].sem, 16)
            sp.wait_ge(C["stored"], 16 * SETUP_STORES)
            for c in (x1_kept, kv_kept, *v_kept):
                c.before(sp, B, c.per)

        @block.tensor
        def _(pe):
            for c in (unit, tail_unit, o_done, sum_done):
                c.credit(pe)
            pe.wait_ge(zeroed, 6)

            def begin(i, name, names=U, banks=ring):
                other, earlier = names.before(name)
                count, n = readers[other]
                count.before(pe, i, n) if earlier else count.now(pe, i, n)
                return banks[names.bank(name)]

            def begin_tail(i, name):
                return begin(i, name, W, tail_ring)

            def three(out, hi, lo, mhi, mlo):
                pe.matmul(out, hi, mhi, start=True, stop=False)
                pe.matmul(out, hi, mlo, start=False, stop=False)
                return pe.matmul(out, lo, mhi, start=False, stop=True)

            def query(i, h):
                unit.done(three(begin(i, f"q{h}")[:], C["aq_hi"][:, h, :], C["aq_lo"][:, h, :], xT_hi[:], xT_lo[:]))

            def max_scores(i, h):
                g = h // REP
                low.now(pe, i, 4 + h)
                for name, tiles in (("ma", (0, 1)), ("mb", (2,)), ("mc", (3,))):
                    o = begin(i, f"{name}{h}")
                    for t in tiles:
                        n = max(256, P * (t + 1))
                        o0 = 256 * t if t < 2 else 0
                        pe.matmul(o[:, o0:o0 + n], qop[0:SHIFT_ROW, h % 4, t * P:(t + 1) * P],
                                  kop[0:SHIFT_ROW, g, 0:n], start=True, stop=False)
                        last = pe.matmul(o[:, o0 + t * P:o0 + (t + 1) * P], C["ident_b"][:], C["mask"][:],
                                         start=False, stop=True)
                    unit.done(last)

            def max_row(i, h):
                max_done.now(pe, i, 3 * h + 3)
                o = begin(i, f"t{h}")
                for t in range(NT):
                    last = pe.transpose(o[:, t * P:(t + 1) * P], nmax[:, h % 2, t, :], C["ident"][:])
                unit.done(last)

            def scores(i, h):
                g = h // REP
                row_done.now(pe, i, h + 1)
                for j in range(NT):
                    o = begin(i, f"s{h}_{j}")
                    pe.matmul(o[:, 0:SELF_N[j]], kop[:, g, j * P:(j + 1) * P], qop[:, h % 4, j * P:T],
                              start=True, stop=False)
                    unit.done(pe.matmul(o[:, 0:P], C["ident_b"][:], C["maskT"][:], start=False, stop=True))

            def weigh(g, o, weight):
                for j in range(NT):
                    for r in range(REP):
                        p = probs[:, REP * g + r, SELF_AT[j]:SELF_AT[j] + SELF_N[j]]
                        last = pe.matmul(o[DL * r:DL * r + DL, j * P:T], weight(j), p, start=(j == 0), stop=(j == NT - 1))
                return last

            def denominators(i, g):
                probs_done.now(pe, i, NT * REP * (g + 1))
                oT_done.now(pe, i, g) if g else oT_done.before(pe, i, KVS)
                sum_done.done(weigh(g, den_ps, lambda j: C["ones"][:, 0:DL]))

            def values(i, g):
                vlat_done.now(pe, i, 1)
                o_done.done(weigh(g, o_ps, lambda j: vlat[:, j, g * DL:(g + 1) * DL]))

            def output_rows(j):
                oT_done.now(pe, j, KVS)
                o = begin_tail(j, "y")
                for t in range(NT):
                    for g in range(KVS):
                        last = pe.matmul(o[:, t * P:(t + 1) * P], oT[:, g, t * P:(t + 1) * P], C["bo"][:, g, :],
                                         start=(g == 0), stop=(g == KVS - 1))
                tail_unit.done(last)

            def turn_inputs(j):
                lat_done.now(pe, j, NT)
                o = begin_tail(j, "lT")
                for t in range(NT):
                    last = pe.transpose(o[:, t * P:(t + 1) * P], lat[:, t, :], C["ident"][:])
                tail_unit.done(last)
                cn_done.now(pe, j, 2)
                o = begin_tail(j, "cT")
                pe.transpose(o[:, 0:P], cn[:, 0, :], C["ident"][:])
                tail_unit.done(pe.transpose(o[:, P:CTX], cn[0:CTX_TAIL, 1, :], C["ident"][0:CTX_TAIL, 0:CTX_TAIL]))

            def project_values(j, c):
                if c == 0:
                    kv_high.now(pe, j, 2)
                    kv_low.now(pe, j, 2)
                for k in range(2):
                    cols = slice(k * T, (k + 1) * T)
                    tail_unit.done(three(begin_tail(j, f"V{c}_{k}")[:], kvT_hi[:, c * P:(c + 1) * P], kvT_lo[:, c * P:(c + 1) * P],
                                         C["wv_hi"][:, cols], C["wv_lo"][:, cols]))

            def body(i, first=False):
                j = i - 1
                pe.wait_ge(x_in, 16 * i + 16)
                o = begin(i, "xT")
                for t in range(NT):
                    last = pe.transpose(o[:, t * P:(t + 1) * P], xs[:, t, :], C["ident"][:])
                unit.done(last)
                if not first:
                    denominators(j, 1)
                low.now(pe, i, 1)
                for g in range(KVS):
                    unit.done(three(begin(i, f"k{g}")[:], C["wk_hi"][:, g, :], C["wk_lo"][:, g, :], xT_hi[:], xT_lo[:]))
                query(i, 0)
                query(i, 1)
                if not first:
                    values(j, 1)
                max_scores(i, 0)
                o = begin(i, "v")
                xT_done.now(pe, i, 1)
                for t in range(NT):
                    last = pe.matmul(o[:, t * KVS * DL:(t + 1) * KVS * DL], xT[:, t * P:(t + 1) * P], C["wvd"][:],
                                     start=True, stop=True)
                unit.done(last)
                for h in range(HS):
                    max_row(i, h)
                    if h + 2 < HS:
                        query(i, h + 2)
                    if h + 1 < HS:
                        max_scores(i, h + 1)
                    scores(i, h)
                    if h == REP - 1:
                        denominators(i, 0)
                        values(i, 0)
                    if first:
                        continue
                    if h == 0:
                        output_rows(j)
                    elif h == INPUTS_AT:
                        turn_inputs(j)
                    for c in VALUES_AT.get(h, ()):
                        project_values(j, c)

            def tail(j):
                denominators(j, 1)
                values(j, 1)
                output_rows(j)
                turn_inputs(j)
                for c in range(KC):
                    project_values(j, c)

            turns(pe, body, tail)

        @block.scalar
        def _(act):
            for c in (high, row_done, probs_done, kv_high, v_act):
                c.credit(act)

            def high_part(i, name, out, rows):
                at_unit(act, i, name)
                high.done(act.activation(out, ps(name)[0:rows, :], ACT.Copy))

            def row(i, h):
                at_unit(act, i, f"t{h}")
                row_done.done(act.activation(qop[SHIFT_ROW:P, h % 4, :], ps(f"t{h}")[SHIFT_ROW:P, :], ACT.Copy))

            def exponentials(i, h):
                for j in range(NT):
                    at_unit(act, i, f"s{h}_{j}")
                    probs_done.done(act.activation(probs[:, h, SELF_AT[j]:SELF_AT[j] + SELF_N[j]],
                                                   ps(f"s{h}_{j}")[:, 0:SELF_N[j]], ACT.Exp, scale=SELF_SCALE))

            def inputs_high(j):
                for k, (a, b) in enumerate(((0, T), (T, KEYS_E))):
                    kv_full.now(act, j, k + 1)
                    if k == 0:
                        kv_kept.before(act, j, 32)
                    kv_high.done(act.activation(kvT_hi[:, a:b], kvf[:, a:b], ACT.Copy))

            def values_out(j, c):
                n = P if c < KC - 1 else TAIL
                at_tail(act, j, f"V{c}_0")
                vout_free(act, j, c)
                v_act.done(act.activation(vout[0:n, c % VOUTS, 0:T], tail_ps(f"V{c}_0")[0:n, :], ACT.Copy))

            def body(i, first=False):
                j = i - 1
                high_part(i, "xT", xT_hi[:], P)
                for g in range(KVS):
                    high_part(i, f"k{g}", kop[0:SHIFT_ROW, g, :], SHIFT_ROW)
                high_part(i, "q0", qop[0:SHIFT_ROW, 0, :], SHIFT_ROW)
                high_part(i, "q1", qop[0:SHIFT_ROW, 1, :], SHIFT_ROW)
                for h in range(HS):
                    row(i, h)
                    if h + 2 < HS:
                        high_part(i, f"q{h + 2}", qop[0:SHIFT_ROW, (h + 2) % 4, :], SHIFT_ROW)
                    exponentials(i, h)
                    if first:
                        continue
                    if h == INPUTS_AT:
                        inputs_high(j)
                    for c in VALUES_AT.get(h, ()):
                        values_out(j, c)

            def tail(j):
                inputs_high(j)
                for c in range(KC):
                    values_out(j, c)

            turns(act, body, tail)

        @block.vector
        def _(dve):
            for c in (low, xT_done, vlat_done, max_done, rden_done, oT_done, y_done, step, tail_step, x1_done, lat_done,
                      cn_done, kv_full, kv_low, v_dve):
                c.credit(dve)
            dve.wait_ge(zeroed, 6)
            rows = [y[:, t, :] for t in range(NT)]
            contexts = [cs[:, 0, :], cs[0:CTX_TAIL, 1, :]]
            normed = [x1[:, t, :] for t in range(NT)]
            latents = [lat[:, t, :] for t in range(NT)]

            def low_of(i, name):
                if name[0] == "k":
                    n, o, r = 2 + int(name[1:]), kop[:, int(name[1:]), :], slice(2 * DL, 3 * DL)
                else:
                    n, o, r = 4 + int(name[1:]), qop[:, int(name[1:]) % 4, :], slice(DL, 2 * DL)
                high.now(dve, i, n)
                low.done(dve.tensor_tensor(o[r, :], ps(name)[r, :], f(o[r, :]), ALU.subtract))

            def maxima(i, h):
                for name, tiles in (("ma", (0, 1)), ("mb", (2,)), ("mc", (3,))):
                    at_unit(dve, i, f"{name}{h}")
                    for t in tiles:
                        o0 = 256 * t if t < 2 else 0
                        last = dve.tensor_reduce(nmax[:, h % 2, t, SHIFT_ROW:SHIFT_ROW + 1],
                                                 ps(f"{name}{h}")[:, o0:o0 + P * (t + 1)], AX_X, ALU.max, negate=True)
                        if t == 0:
                            step.done(last)
                    max_done.done(last)

            def reciprocals(i, g):
                sum_done.now(dve, i, g + 1)
                oT_done.now(dve, i, g) if g else oT_done.before(dve, i, KVS)
                rden_done.done(dve.reciprocal(rden[:], den_ps[:]))

            def outputs(i, g):
                o_done.now(dve, i, g + 1)
                rden_done.now(dve, i, g + 1)
                oT_done.done(dve.tensor_tensor(oT[:, g, :], o_ps[:], rden[:], ALU.mult))

            def sum_rows(j):
                at_tail(dve, j, "y")
                y_done.done(dve.tensor_tensor(y[:].rearrange("p n d -> p (n d)"), tail_ps("y")[:],
                                              C["xall"][:, bass.ds(j * NT, NT), :].rearrange("p n d -> p (n d)"), ALU.add))
                dve.wait_ge(c_in, 32 * j + 32)
                y_done.now(dve, j, 1)
                norm1.moments(dve, j, tail_step, held, rows + contexts)

            def norm_rows(j):
                norm1.roots(dve, j, tail_step)
                norm1.apply(dve, rows, latents, lat_done, again=True)
                norm1.apply(dve, contexts, [cn[:, 0, :], cn[0:CTX_TAIL, 1, :]], cn_done, NT)

            def norm_kept_rows(j):
                x1_kept.before(dve, j, 16)
                norm1.apply(dve, rows, normed, x1_done)

            def inputs(j):
                for k, (name, a, b, g) in enumerate((("lT", 0, T, 0), ("cT", T, KEYS, 2))):
                    at_tail(dve, j, name)
                    gain, bias = C["gb"][:, g:g + 1], C["gb"][:, g + 1:g + 2]
                    if k:
                        tail_step.done(dve.tensor_scalar(kvf[:, KEYS:KEYS_E], tail_ps(name)[:, CTX - 2:CTX], gain, bias,
                                                         ALU.mult, ALU.add))
                    kv_full.done(dve.tensor_scalar(kvf[:, a:b], tail_ps(name)[:, 0:b - a], gain, bias, ALU.mult, ALU.add))
                for k, (a, b) in enumerate(((0, T), (T, KEYS_E))):
                    kv_high.now(dve, j, k + 1)
                    kv_full.now(dve, j, k + 1)
                    kv_low.done(dve.tensor_tensor(kvT_lo[:, a:b], kvf[:, a:b], f(kvT_hi[:, a:b]), ALU.subtract))

            def values_out(j, c):
                n = P if c < KC - 1 else TAIL
                at_tail(dve, j, f"V{c}_1")
                vout_free(dve, j, c)
                v_dve.done(dve.tensor_copy(vout[0:n, c % VOUTS, T:], tail_ps(f"V{c}_1")[0:n, :]))

            def body(i, first=False):
                j = i - 1
                high.now(dve, i, 1)
                low.done(dve.tensor_tensor(xT_lo[:], ps("xT")[:], f(xT_hi[:]), ALU.subtract))
                xT_done.done(dve.tensor_copy(xT[:], ps("xT")[:]))
                if not first:
                    reciprocals(j, 1)
                low_of(i, "k0")
                low_of(i, "k1")
                low_of(i, "q0")
                low_of(i, "q1")
                if not first:
                    outputs(j, 1)
                maxima(i, 0)
                at_unit(dve, i, "v")
                vlat_done.done(dve.tensor_copy(vlat[:], ps("v")[:, 0:NT * KVS * DL].rearrange("p (t l) -> p t l", t=NT)))
                for h in range(HS):
                    if h + 2 < HS:
                        low_of(i, f"q{h + 2}")
                    if h + 1 < HS:
                        maxima(i, h + 1)
                    if not first:
                        if h == 1:
                            sum_rows(j)
                        elif h == 2:
                            norm_rows(j)
                        elif h == INPUTS_AT:
                            inputs(j)
                        elif h == INPUTS_AT + 1:
                            norm_kept_rows(j)
                        for c in VALUES_AT.get(h, ()):
                            values_out(j, c)
                    if h == 6:
                        reciprocals(i, 0)
                        outputs(i, 0)
                assert step.n % step.per == 0

            def tail(j):
                reciprocals(j, 1)
                outputs(j, 1)
                sum_rows(j)
                norm_rows(j)
                inputs(j)
                norm_kept_rows(j)
                for c in range(KC):
                    values_out(j, c)

            turns(dve, body, tail)


FRONT = ["q", "k", "m0_0", "m0_1", "m0_2", "m0_3", "m1_0", "m1_1", "t0", "m1_2", "m1_3", "t1"]


def cross_stage(nc, I, C):
    F_AT = {n: k for k, n in enumerate(FRONT)}
    NF = len(FRONT)
    with ExitStack() as ctx:
        m = Mem(nc, ctx)
        w = [m.sb(f"w{s}", [P, 2, 2, P], F32R) for s in range(2)]
        v = [m.sb(f"v{s}", [P, KC, P]) for s in range(2)]
        qa = [m.sb(f"qa{s}", [P, 2, T], F32R) for s in range(2)]
        qb = [m.sb(f"qb{s}", [P, 2, T], F32R) for s in range(2)]
        ka = [m.sb(f"ka{s}", [P, 2, KPAD], F32R) for s in range(2)]
        kb = [m.sb(f"kb{s}", [P, 2, KPAD], F32R) for s in range(2)]
        nmax = m.sb("nmaxx", [P, 2, NT, P])
        probs = m.sb("probsx", [P, 2, KC, T])
        psum = [m.sb(f"psum{s}", [P, 2, T]) for s in range(2)]
        oraw = [m.sb(f"oraw{s}", [P, T]) for s in range(2)]
        rden = m.sb("rdenx", [P, T])
        front = [m.pb(f"front{k}", [P, 2, T]) for k in range(2)]
        sc = [m.pb(f"sc{k}", [P, T]) for k in range(2)]
        o_ps = m.pb("o_psx", [P, T])
        den_ps = m.pb("den_psx", [P, T])

        w_in = [m.sem(f"w_in{s}") for s in range(2)]
        v_in = [m.sem(f"v_in{s}") for s in range(2)]
        zeroed = m.sem("zeroedx")
        unit = Count(m.sem("unitx"), NF, 2)
        score = Count(m.sem("score"), 2 * KC, 2)
        qa_high = Count(m.sem("qa_high"), 2, 2)
        qb_high = Count(m.sem("qb_high"), 2, 2)
        ka_high = Count(m.sem("ka_high"), 2, 2)
        ka_again = Count(m.sem("ka_again"), 2, 2)
        qa_low = Count(m.sem("qa_low"), 2, 2)
        kb_low = Count(m.sem("kb_low"), 2, 2)
        maxed = Count(m.sem("maxed"), 2 * NT, 2)
        row_in = Count(m.sem("row_in"), 2, 2)
        expd = Count(m.sem("expd"), 2 * KC, 2)
        summed = Count(m.sem("summed"), 2 * (KC - 1), 2)
        o_done = Count(m.sem("o_donex"), 1, 2)
        den_done = Count(m.sem("den_done"), 1, 2)
        o_out = Count(m.sem("o_out"), 1, 2)
        recip = Count(m.sem("recip"), 1, 2)
        norm = Count(m.sem("norm"), 1, 2)
        block = ctx.enter_context(nc.Block())

        readers = {"q": (qa_low, 2), "k": (kb_low, 2), "t0": (row_in, 1), "t1": (row_in, 2)}
        for h in range(2):
            for t in range(NT):
                readers[f"m{h}_{t}"] = (maxed, NT * h + t + 1)

        own = [slice(0, DH), slice(DH, P)]
        other = [slice(DH, P), slice(0, DH)]

        def front_of(s, name):
            return front[(s * NF + F_AT[name]) % 2]

        def turns(eng, body):
            body(0, 0, 0, first=True)
            body(1, 1, 0)
            with eng.Fori(1, STEPS // 2 - 1) as i:
                body(2 * i, 0, i)
                body(2 * i + 1, 1, i)
            body(STEPS - 2, 0, STEPS // 2 - 1)
            body(STEPS - 1, 1, STEPS // 2 - 1, last=True)

        def after(s, u):
            return 1 - s, u + s

        @block.sync
        def _(sp):
            def load(j, s, u, first=False, last=False):
                unit.before(sp, j, F_AT["k"] + 1, 2)
                sp.dma_start(f(w[s][:]).rearrange("p a b c -> p (a b c)"),
                             f(C["wpair"][bass.ds(j % PAIRS, 1)]).rearrange("s p a b c -> p (s a b c)")).then_inc(w_in[s], 16)
                o_done.before(sp, j, 1, 2)
                sp.dma_start(v[s][:].rearrange("p k c -> p (k c)"),
                             C["vals"].rearrange("b s p k c -> (b s) p (k c)")[bass.ds(j, 1)].rearrange("s p c -> p (s c)")
                             ).then_inc(v_in[s], 16)

            turns(sp, load)
            sp.dma_start(C["wout"][:], I["Wout"].rearrange("(s p) n -> p s n", p=P)).then_inc(C["wout_in"], 16)

        @block.gpsimd
        def _(pool):
            summed.credit(pool)
            pool.memset(nmax[:], 0.0).then_inc(zeroed, 1)
            pool.memset(probs[:, :, KC - 1, :], 0.0).then_inc(zeroed, 1)
            pool.wait_ge(zeroed, 6)
            for s in range(2):
                for h in range(2):
                    one = other[h].start
                    pool.memset(f(kb[s][one:one + 1, h, :]), 1.0).then_inc(zeroed, 1)

            def sums(j, s, u, first=False, last=False):
                den_done.before(pool, j, 1, 2)
                for c in range(1, KC):
                    expd.now(pool, j, 2 * c + 2)
                    for h in range(2):
                        n = P if c < KC - 1 else TAIL
                        if c > 1:
                            summed.now(pool, j, 2 * (c - 2) + h + 1)
                        summed.done(pool.tensor_tensor(psum[s][0:n, h, :], probs[0:n, h, 0, :] if c == 1 else psum[s][0:n, h, :],
                                                       probs[0:n, h, c, :], ALU.add))

            turns(pool, sums)

        @block.tensor
        def _(pe):
            for c in (unit, score, o_done, den_done):
                c.credit(pe)

            def begin(j, s, name):
                k = F_AT[name]
                count, n = readers[FRONT[(k - 2) % NF]]
                count.now(pe, j, n) if k >= 2 else count.before(pe, j, n)
                return front_of(s, name)

            def project(j, s, kind, out, cols):
                hi, lo = w[s][:, 0, kind, :], w[s][:, 1, kind, :]
                khi = C["kv_hi"][:, bass.ds(j // PAIRS, 1), cols].rearrange("p b n -> p (b n)")
                klo = C["kv_lo"][:, bass.ds(j // PAIRS, 1), cols].rearrange("p b n -> p (b n)")
                pe.matmul(out, hi, khi, start=True, stop=False)
                pe.matmul(out, hi, klo, start=False, stop=False)
                return pe.matmul(out, lo, khi, start=False, stop=True)

            def queries(j, s, u):
                pe.wait_ge(w_in[s], 16 * (u + 1))
                unit.done(project(j, s, 0, begin(j, s, "q")[:, 0, :], slice(0, T)))

            def keys(j, s):
                o = begin(j, s, "k")
                for k in range(2):
                    last = project(j, s, 1, o[:, k, 0:HALF], slice(k * HALF, (k + 1) * HALF))
                unit.done(last)

            def max_scores(j, s, h, t):
                if t == 0:
                    qa_low.now(pe, j, h + 1)
                    ka_again.now(pe, j, h + 1)
                o = begin(j, s, f"m{h}_{t}")
                for k in range(2):
                    last = pe.matmul(o[:, k, 0:HALF], qa[s][:, h, t * P:(t + 1) * P],
                                     ka[s][:, h, k * HALF:(k + 1) * HALF], start=True, stop=True)
                unit.done(last)

            def max_row(j, s, h):
                maxed.now(pe, j, NT * (h + 1))
                o = begin(j, s, f"t{h}")
                for t in range(NT):
                    last = pe.transpose(o[:, 0, t * P:(t + 1) * P], nmax[:, h, t, :], C["ident"][:])
                unit.done(last)

            def score_tile(j, s, c, h):
                k = 2 * c + h
                expd.now(pe, j, k - 1) if k >= 2 else expd.before(pe, j, 2 * KC - 1 + k)
                if c == 0:
                    row_in.now(pe, j, h + 1)
                    kb_low.now(pe, j, h + 1)
                pe.matmul(sc[h][:], ka[s][:, h, c * P:(c + 1) * P], qa[s][:, h, :], start=True, stop=False)
                score.done(pe.matmul(sc[h][:], kb[s][:, h, c * P:(c + 1) * P], qb[s][:, h, :], start=False, stop=True))

            def scores(j, s, c):
                score_tile(j, s, c, 0)
                score_tile(j, s, c, 1)

            def values(j, s, u, c):
                if c == 0:
                    pe.wait_ge(v_in[s], 16 * (u + 1))
                    o_out.before(pe, j, 1)
                expd.now(pe, j, 2 * c + 2)
                for h in range(2):
                    last = pe.matmul(o_ps[h * DH:(h + 1) * DH, :], v[s][:, c, h * DH:(h + 1) * DH], probs[:, h, c, :],
                                     start=(c == 0), stop=(c == KC - 1))
                if c == KC - 1:
                    o_done.done(last)

            def denominators(j, s):
                summed.now(pe, j, 2 * (KC - 1))
                recip.before(pe, j, 1)
                for h in range(2):
                    last = pe.matmul(den_ps[h * DH:(h + 1) * DH, :], C["ones"][:, 0:DH], psum[s][:, h, :], start=True, stop=True)
                den_done.done(last)

            def maxima(j, s, k, last):
                if not last:
                    max_scores(j, s, k // NT, k % NT)

            def step(j, s, u, first=False, last=False):
                n, (ns, nu) = j + 1, after(s, u)
                scores(j, s, 0)
                if not last:
                    queries(n, ns, nu)
                scores(j, s, 1)
                if not last:
                    keys(n, ns)
                values(j, s, u, 0)
                scores(j, s, 2)
                if not first:
                    denominators(j - 1, 1 - s)
                values(j, s, u, 1)
                maxima(n, ns, 0, last)
                maxima(n, ns, 1, last)
                scores(j, s, 3)
                maxima(n, ns, 2, last)
                values(j, s, u, 2)
                maxima(n, ns, 3, last)
                scores(j, s, 4)
                maxima(n, ns, 4, last)
                values(j, s, u, 3)
                maxima(n, ns, 5, last)
                score_tile(j, s, 5, 0)
                if not last:
                    max_row(n, ns, 0)
                maxima(n, ns, 6, last)
                score_tile(j, s, 5, 1)
                maxima(n, ns, 7, last)
                values(j, s, u, 4)
                if not last:
                    max_row(n, ns, 1)
                values(j, s, u, 5)

            queries(0, 0, 0)
            keys(0, 0)
            pe.wait_ge(zeroed, 10)
            for k in range(2 * NT):
                maxima(0, 0, k, False)
                if k == 5:
                    max_row(0, 0, 0)
            max_row(0, 0, 1)
            turns(pe, step)
            denominators(STEPS - 1, 1)

        @block.scalar
        def _(act):
            for c in (qa_high, qb_high, ka_high, ka_again, row_in, expd):
                c.credit(act)

            def q_high(j, s):
                unit.now(act, j, F_AT["q"] + 1)
                for h in range(2):
                    qa_high.done(act.activation(qa[s][own[h], h, :], front_of(s, "q")[own[h], 0, :], ACT.Copy))

            def q_again(j, s):
                for h in range(2):
                    qa_high.now(act, j, h + 1)
                    qb_high.done(act.activation(qb[s][own[h], h, :], f(qa[s][own[h], h, :]), ACT.Copy))

            def k_high(j, s):
                unit.now(act, j, F_AT["k"] + 1)
                for h in range(2):
                    ka_high.done(act.activation(ka[s][own[h], h, 0:KEYS_E].rearrange("p (a n) -> p a n", a=2),
                                                front_of(s, "k")[own[h], :, 0:HALF], ACT.Copy))
                for h in range(2):
                    ka_high.now(act, j, h + 1)
                    ka_again.done(act.activation(ka[s][other[h], h, 0:KEYS_E], f(ka[s][own[h], h, 0:KEYS_E]), ACT.Copy))

            def row(j, s, h):
                unit.now(act, j, F_AT[f"t{h}"] + 1)
                row_in.done(act.activation(qb[s][other[h], h, :], front_of(s, f"t{h}")[other[h], 0, :], ACT.Copy))

            def exponential(j, c, h):
                score.now(act, j, 2 * c + h + 1)
                summed.before(act, j, 2 * (max(c, 1) - 1) + h + 1)
                rows = P if c < KC - 1 else TAIL
                expd.done(act.activation(probs[0:rows, h, c, :], sc[h][0:rows, :], ACT.Exp, scale=CROSS_SCALE))

            def step(j, s, u, first=False, last=False):
                n, (ns, nu) = j + 1, after(s, u)
                for c in range(KC):
                    exponential(j, c, 0)
                    if c == KC - 1 and not last:
                        row(n, ns, 0)
                    exponential(j, c, 1)
                    if last:
                        continue
                    if c == 0:
                        q_high(n, ns)
                    elif c == 1:
                        k_high(n, ns)
                    elif c == 2:
                        q_again(n, ns)
                if not last:
                    row(n, ns, 1)

            q_high(0, 0)
            q_again(0, 0)
            k_high(0, 0)
            row(0, 0, 0)
            row(0, 0, 1)
            turns(act, step)

        @block.vector
        def _(dve):
            for c in (qa_low, kb_low, maxed, o_out, recip, norm):
                c.credit(dve)

            def q_low(j, s):
                for h in range(2):
                    qa_high.now(dve, j, h + 1)
                    qa_low.done(dve.tensor_tensor(qa[s][other[h], h, :], front_of(s, "q")[own[h], 0, :],
                                                  f(qa[s][own[h], h, :]), ALU.subtract))

            def k_low(j, s):
                view = lambda x, h: x[s][own[h], h, 0:KEYS_E].rearrange("p (a n) -> p a n", a=2)
                for h in range(2):
                    ka_high.now(dve, j, h + 1)
                    kb_low.done(dve.tensor_tensor(view(kb, h), front_of(s, "k")[own[h], :, 0:HALF], f(view(ka, h)),
                                                  ALU.subtract))

            def maxima(j, s, h):
                for t in range(NT):
                    unit.now(dve, j, F_AT[f"m{h}_{t}"] + 1)
                    maxed.done(dve.tensor_reduce(nmax[:, h, t, other[h].start:other[h].start + 1], front_of(s, f"m{h}_{t}")[:, :, 0:HALF],
                                                 mybir.AxisListType.XY, ALU.max, negate=True))

            def reciprocals(j):
                den_done.now(dve, j, 1)
                norm.before(dve, j, 1)
                recip.done(dve.reciprocal(rden[:], den_ps[:]))

            def outputs(j, s):
                o_done.now(dve, j, 1)
                norm.before(dve, j, 1, 2)
                o_out.done(dve.tensor_copy(oraw[s][:], o_ps[:]))

            def normalise(j, s):
                recip.now(dve, j, 1)
                o_out.now(dve, j, 1)
                out = C["oall"][:, bass.ds(j, 1), :].rearrange("p a n -> p (a n)")
                norm.done(dve.tensor_tensor(out, oraw[s][:], rden[:], ALU.mult))

            def step(j, s, u, first=False, last=False):
                n, (ns, nu) = j + 1, after(s, u)
                if not last:
                    q_low(n, ns)
                    k_low(n, ns)
                    maxima(n, ns, 0)
                    maxima(n, ns, 1)
                if not first:
                    reciprocals(j - 1)
                outputs(j, s)
                if not first:
                    normalise(j - 1, 1 - s)

            for s in range(2):
                dve.memset(f(kb[s][:]), 0.0).then_inc(zeroed, 1)
                dve.memset(f(ka[s][:, :, KEYS_E:KPAD]), 0.0).then_inc(zeroed, 1)
            dve.wait_ge(zeroed, 6)
            q_low(0, 0)
            k_low(0, 0)
            maxima(0, 0, 0)
            maxima(0, 0, 1)
            turns(dve, step)
            reciprocals(STEPS - 1)
            normalise(STEPS - 1, 1)


def close_stage(nc, I, C):
    with ExitStack() as ctx:
        m = Mem(nc, ctx)
        t1 = m.sb("t1", [P, T])
        y = m.sb("yc", [P, NT, D])
        x2 = m.sb("x2", [P, NT, D])
        x2T = m.sb("x2T", [P, T])
        norm = Norm(m, "x2", NT)
        lg = m.sb("lg", [P, NT, E])
        top = m.sb("top", [P, NT, E])
        idx = m.sb("idx", [P, NT, E], U32)
        topf = m.sb("topf", [P, NT, 2])
        choice = m.sb("choice", [P, NT, 2, E])
        sums = m.sb("sums", [P, NT + 1, 2, E])
        placed = m.sb("placed", [P, NT, 2, E])
        rank = m.sb("rankc", [P, NT, 2])
        over = m.sb("overc", [P, NT])
        slotf = m.sb("slotfc", [P, NT])
        ahead = m.sb("ahead", [P, E])
        behind = m.sb("behind", [P, TILES, E])
        base = m.sb("base", [P, TILES])
        over2 = m.sb("over2", [P, TILES])
        slotf2 = m.sb("slotf2", [P, TILES])
        number = m.sb("number", [P, 2, TILES], U32)
        e2 = m.sb("e2", [P, NT])
        den = m.sb("denr", [P, NT])
        first_weight = m.sb("first_weight", [P, NT])
        out_ps, back_ps, turn_ps, logit_ps = [m.pb(f"cps{k}", [P, T]) for k in range(4)]
        place_ps = m.pb("place_ps", [P, NT, 2, E])
        ahead_ps = m.pb("ahead_ps", [P, E])
        out_done = Count(m.sem("out_done"), 1)
        t1_done = Count(m.sem("t1_done"), 1)
        back_done = Count(m.sem("back_done"), 1)
        y_done = Count(m.sem("y_donec"), 1)
        step = Count(m.sem("stepc"), norm_steps(NT) + 2 * NT + 2)
        place_step = Count(m.sem("place_step"), 8)
        held = m.sem("heldc")
        x2_done = Count(m.sem("x2_done"), NT)
        x2_kept = Count(m.sem("x2_kept"), 2 * NT)
        turned = Count(m.sem("turnedc"), 1)
        x2T_done = Count(m.sem("x2T_done"), 1)
        logit_done = Count(m.sem("logit_done"), 1)
        lg_done = Count(m.sem("lg_done"), 1)
        topf_done = Count(m.sem("topf_done"), 1)
        choice_done = Count(m.sem("choice_done"), 1)
        summed = Count(m.sem("summedc"), NT + 1)
        places = Count(m.sem("places"), 1)
        placed_done = Count(m.sem("placed_done"), 1)
        slot_done = Count(m.sem("slot_donec"), 1)
        scattered = m.sem("scattered")
        counted = m.sem("counted")
        diff_done = Count(m.sem("diff_done"), 1)
        exp_done = Count(m.sem("exp_done"), 1)
        second_step = m.sem("second_step")
        slot2_done = m.sem("slot2_done")
        cleared = m.sem("cleared")
        block = ctx.enter_context(nc.Block())

        @block.tensor
        def _(pe):
            for c in (out_done, back_done, turned, logit_done, places):
                c.credit(pe)
            pe.wait_ge(C["wout_in"], 16)

            def project(i):
                t1_done.before(pe, i, 1)
                for s in range(PAIRS):
                    last = pe.matmul(out_ps[:], C["wout"][:, s, :],
                                     C["oall"][:, bass.ds(i * PAIRS + s, 1), :].rearrange("p a n -> p (a n)"),
                                     start=(s == 0), stop=(s == PAIRS - 1))
                out_done.done(last)

            def place(i):
                choice_done.now(pe, i, 1)
                placed_done.before(pe, i, 1)
                summed.now(pe, i, NT)
                flat = lambda x: x.rearrange("p n k e -> p (n k e)")
                pe.matmul(flat(place_ps[:]), C["upper"][:], flat(choice[:]), start=True, stop=False)
                places.done(pe.matmul(flat(place_ps[:]), C["ones"][:], flat(sums[:, 0:NT, :, :]), start=False, stop=True))

            def body(i, first=False, last=False):
                t1_done.now(pe, i, 1)
                y_done.before(pe, i, 1)
                for t in range(NT):
                    ins = pe.transpose(back_ps[:, t * P:(t + 1) * P], t1[:, t * P:(t + 1) * P], C["ident"][:])
                back_done.done(ins)
                if not last:
                    project(i + 1)
                if not first:
                    place(i - 1)
                x2_done.now(pe, i, NT)
                x2T_done.before(pe, i, 1)
                for t in range(NT):
                    ins = pe.transpose(turn_ps[:, t * P:(t + 1) * P], x2[:, t, :], C["ident"][:])
                turned.done(ins)
                x2T_done.now(pe, i, 1)
                lg_done.before(pe, i, 1)
                for t in range(NT):
                    ins = pe.matmul(logit_ps[:, t * E:(t + 1) * E], x2T[:, t * P:(t + 1) * P], C["wg"][:], start=True, stop=True)
                logit_done.done(ins)

            project(0)
            body(0, first=True)
            with pe.Fori(1, B - 1) as i:
                body(i)
            body(B - 1, last=True)
            place(B - 1)
            summed.now(pe, B - 1, NT + 1)
            pe.matmul(ahead_ps[:], C["ones"][:], sums[:, NT, 0, :], start=True, stop=True).then_inc(counted, 1)

        @block.scalar
        def _(act):
            for c in (t1_done, x2_kept, x2T_done, lg_done, exp_done):
                c.credit(act)

            def projected(i):
                out_done.now(act, i, 1)
                back_done.before(act, i, 1)
                t1_done.done(act.activation(t1[:], out_ps[:], ACT.Copy))

            def keep(i, k):
                for t in range(NT):
                    x2_kept.done(act.activation(C["rows"][:, k, bass.ds(i * NT + t, 1), 0:D].rearrange("p a d -> p (a d)"),
                                                x2[:, t, :], ACT.Copy))

            def body(i, last=False):
                if not last:
                    projected(i + 1)
                turned.now(act, i, 1)
                logit_done.before(act, i, 1)
                x2T_done.done(act.activation(x2T[:], turn_ps[:], ACT.Copy))
                keep(i, 0)
                logit_done.now(act, i, 1)
                topf_done.before(act, i, 1)
                lg_done.done(act.activation(lg[:], logit_ps[:, 0:NT * E].rearrange("p (n e) -> p n e", n=NT), ACT.Copy))
                keep(i, 1)
                diff_done.now(act, i, 1)
                exp_done.done(act.activation(e2[:], e2[:], ACT.Exp))

            projected(0)
            with act.Fori(0, B - 1) as i:
                body(i)
            body(B - 1, last=True)

        @block.vector
        def _(dve):
            for c in (y_done, step, place_step, x2_done, topf_done, choice_done, placed_done, slot_done, diff_done):
                c.credit(dve)

            def place(i):
                places.now(dve, i, 1)
                placed_done.done(dve.tensor_tensor(placed[:], place_ps[:], choice[:], ALU.mult))
                placed_done.now(dve, i, 1)
                place_step.done(dve.tensor_reduce(rank[:], placed[:], AX_X, ALU.add))
                place_step.own(dve, i)
                place_step.done(dve.tensor_scalar(over[:], rank[:, :, 0], float(CAP), None, ALU.is_ge))
                place_step.done(dve.scalar_tensor_tensor(out=slotf[:], in0=topf[:, :, 0], scalar=float(CAP), in1=rank[:, :, 0],
                                                         op0=ALU.mult, op1=ALU.add))
                place_step.done(dve.tensor_copy(C["rank"][:, bass.ds(i * NT, NT), :], rank[:]))
                exp_done.now(dve, i, 1)
                place_step.done(dve.tensor_scalar(den[:], e2[:], 1.0, None, ALU.add))
                place_step.own(dve, i)
                place_step.done(dve.reciprocal(first_weight[:], den[:]))
                place_step.own(dve, i)
                weight = lambda k: C["rows"][:, k, bass.ds(i * NT, NT), D:D + 1].rearrange("p n a -> p (n a)")
                place_step.done(dve.tensor_copy(weight(0), first_weight[:]))
                place_step.done(dve.tensor_tensor(weight(1), first_weight[:], e2[:], ALU.mult))
                place_step.own(dve, i)
                slot_done.done(dve.scalar_tensor_tensor(out=C["slot"][:, 0, bass.ds(i * NT, NT)], in0=over[:], scalar=DROPPED,
                                                        in1=slotf[:], op0=ALU.mult, op1=ALU.add))
                slot_done.now(dve, i, 1)

            def body(i, first=False):
                back_done.now(dve, i, 1)
                y_done.done(dve.tensor_tensor(y[:], back_ps[:].rearrange("p (n d) -> p n d", n=NT),
                                              C["x1all"][:, bass.ds(i, 1), :, :].rearrange("p b n d -> p (b n) d"), ALU.add))
                y_done.now(dve, i, 1)
                rows = [y[:, t, :] for t in range(NT)]
                norm.moments(dve, i, step, held, rows)
                norm.roots(dve, i, step)
                x2_kept.before(dve, i, 2 * NT)
                norm.apply(dve, rows, [x2[:, t, :] for t in range(NT)], x2_done)
                if not first:
                    place(i - 1)
                lg_done.now(dve, i, 1)
                dve.sem_inc(held, 1)
                for t in range(NT):
                    step.done(dve.max(top[:, t, :], lg[:, t, :]))
                step.own(dve, i, held)
                diff_done.done(dve.tensor_tensor(e2[:], top[:, :, 1], top[:, :, 0], ALU.subtract))
                for t in range(NT):
                    step.done(dve.max_index(idx[:, t, :], top[:, t, :], lg[:, t, :]))
                step.own(dve, i)
                topf_done.done(dve.tensor_copy(topf[:], idx[:, :, 0:2]))
                topf_done.now(dve, i, 1)
                summed.before(dve, i, NT + 1)
                choice_done.done(dve.tensor_tensor(choice[:], topf[:].unsqueeze(3).broadcast_to([P, NT, 2, E]),
                                                   C["expert"][:].unsqueeze(1).unsqueeze(1).broadcast_to([P, NT, 2, E]),
                                                   ALU.is_equal))
                step.done(dve.tensor_copy(C["topi"][:, bass.ds(i * NT, NT), :], topf[:]))
                choice_done.now(dve, i, 1)
                step.done(dve.tensor_copy(C["second"][:, bass.ds(i * NT, NT), :], choice[:, :, 1, :]))

            body(0, first=True)
            with dve.Fori(1, B) as i:
                body(i)
            place(B - 1)
            step.own(dve, B - 1)
            place_step.own(dve, B - 1)
            dve.wait_ge(counted, 1)
            n = [0]

            def then(ins):
                n[0] += 1
                ins.then_inc(second_step, 1)
                dve.wait_ge(second_step, n[0])

            then(dve.tensor_copy(ahead[:], ahead_ps[:]))
            then(dve.tensor_tensor(behind[:], C["second"][:], ahead[:].unsqueeze(1).broadcast_to([P, TILES, E]), ALU.mult))
            then(dve.tensor_reduce(base[:], behind[:], AX_X, ALU.add))
            then(dve.tensor_tensor(C["rank"][:, :, 1], C["rank"][:, :, 1], base[:], ALU.add))
            then(dve.tensor_scalar(over2[:], C["rank"][:, :, 1], float(CAP), None, ALU.is_ge))
            then(dve.scalar_tensor_tensor(out=slotf2[:], in0=C["topi"][:, :, 1], scalar=float(CAP), in1=C["rank"][:, :, 1],
                                          op0=ALU.mult, op1=ALU.add))
            dve.scalar_tensor_tensor(out=C["slot"][:, 1, :], in0=over2[:], scalar=DROPPED, in1=slotf2[:],
                                     op0=ALU.mult, op1=ALU.add).then_inc(slot2_done, 1)

        @block.sync
        def _(sp):
            for e in range(2):
                load_weights(sp, I, C, e, e)
            sp.wait_ge(scattered, 16 * 2 * TILES)
            for e in range(2):
                load_rows(sp, C, e, e)

        @block.gpsimd
        def _(pool):
            summed.credit(pool)
            pool.memset(sums[:, NT, :, :], 0.0).then_inc(cleared, 1)
            for k in range(2):
                pool.iota(number[:, k, :], pattern=[[P, TILES]], base=k * B * T, channel_multiplier=1).then_inc(cleared, 1)
            pool.wait_ge(cleared, 3)
            pool.tensor_copy(C["rows"][:, :, :, D + 1:ROW].bitcast(U32).rearrange("p k n a -> p k (n a)"), number[:]).then_inc(cleared, 1)
            pool.wait_ge(cleared, 4)

            def add_up(i):
                places.before(pool, i, 1)
                summed.done(pool.tensor_copy(sums[:, 0, :, :], sums[:, NT, :, :]))
                choice_done.now(pool, i, 1)
                for t in range(NT):
                    summed.now(pool, i, t + 1)
                    summed.done(pool.tensor_tensor(sums[:, t + 1, :, :], sums[:, t, :, :], choice[:, t, :, :], ALU.add))
                summed.now(pool, i, NT + 1)

            def scatter(k, t):
                pool.indirect_dma_start(C["xslots"], bass.IndirectOffsetOnAxis(ap=C["slot"][:, k, t:t + 1], axis=0),
                                        C["rows"][:, k, t, :], None, bounds_check=SLOTS - 1,
                                        oob_is_err=False).then_inc(scattered, 16)

            add_up(0)
            for i in range(B):
                if i + 1 < B:
                    add_up(i + 1)
                slot_done.now(pool, i, 1)
                x2_kept.now(pool, i, 2 * NT)
                for t in range(i * NT, (i + 1) * NT):
                    scatter(0, t)
            pool.wait_ge(slot2_done, 1)
            for t in range(TILES):
                scatter(1, t)


def load_rows(eng, C, e, s):
    eng.dma_start(C["xe"][s][:], C["xslots"].rearrange("(e n p) d -> e p n d", p=P, n=ST)[bass.ds(e, 1)]
                  .rearrange("e p n d -> p (e n) d")).then_inc(C["xe_in"][s], 16)


def load_weights(eng, I, C, e, s):
    eng.dma_start(C["wf"][s][:], I["c_fc"][bass.ds(e, 1)].rearrange("e p n -> p (e n)")).then_inc(C["we_in"][s], 16)
    eng.dma_start(C["wp"][s][:], I["c_proj"][bass.ds(e, 1)].rearrange("e (c p) d -> p (e c) d", p=P)).then_inc(C["we_in"][s], 16)


def expert_stage(nc, I, C):
    N2 = CAP // 2
    with ExitStack() as ctx:
        m = Mem(nc, ctx)
        xe, wf, wp, x_in, w_in = (C[k] for k in ("xe", "wf", "wp", "xe_in", "we_in"))
        xeT = [m.sb(f"xeT{s}", [P, CAP]) for s in range(2)]
        hT = m.sb("hT", [P, FC, CAP])
        ye = [m.sb(f"ye{s}", [P, ST, D]) for s in range(2)]
        to = [m.sb(f"to{s}", [P, ST], U32) for s in range(2)]
        ps_x = m.pb("ps_x", [P, 2, T])
        ps_h = [m.pb(f"ps_h{k}", [P, 2, T]) for k in range(2)]
        ps_y = m.pb("ps_y", [P, 2, T])
        turned = Count(m.sem("turned_e"), 1, 2)
        xeT_done = Count(m.sem("xeT_done"), 2, 2)
        h_done = Count(m.sem("h_done"), FC, 2)
        act_done = Count(m.sem("act_done"), FC, 2)
        y_done = Count(m.sem("y_done_e"), 1, 2)
        y_out = Count(m.sem("y_out"), ST + 1, 2)
        sent = m.sem("sent")
        y_kept = Count(m.sem("y_kept"), 1, 2)
        held = m.sem("helde")
        block = ctx.enter_context(nc.Block())

        def turns(eng, body):
            with eng.Fori(0, E // 2 - 1) as i:
                body(2 * i, 0, i)
                body(2 * i + 1, 1, i)
            body(E - 2, 0, E // 2 - 1)
            body(E - 1, 1, E // 2 - 1, last=True)

        @block.sync
        def _(sp):
            with sp.Fori(1, E // 2) as i:
                for s in range(2):
                    e = 2 * i + s
                    y_out.before(sp, e, ST + 1, 2)
                    load_rows(sp, C, e, s)
                    y_done.before(sp, e, 1, 2)
                    load_weights(sp, I, C, e, s)

        @block.gpsimd
        def _(pool):
            y_kept.credit(pool)

            def expert(e, s, i, last=False):
                y_out.now(pool, e, ST + 1)
                pool.sem_inc(held, 1)
                for t in range(ST):
                    pool.indirect_dma_start(C["yrows"], bass.IndirectOffsetOnAxis(ap=to[s][:, t:t + 1], axis=0),
                                            ye[s][:, t, :], None, bounds_check=2 * B * T - 1,
                                            oob_is_err=False).then_inc(sent, 16)
                pool.wait_ge(sent, 16 * ST * (e + 1))
                pool.sem_inc(y_kept.sem, 1)

            turns(pool, expert)

        @block.tensor
        def _(pe):
            for c in (turned, h_done, y_done):
                c.credit(pe)

            def turn_rows(e, s, i):
                pe.wait_ge(x_in[s], 16 * (i + 1))
                xeT_done.before(pe, e, 2)
                for t in range(ST):
                    last = pe.transpose(ps_x[:, t // NT, (t % NT) * P:(t % NT) * P + P], xe[s][:, t, 0:D], C["ident"][:])
                turned.done(last)

            def expert(e, s, i, last=False):
                pe.wait_ge(w_in[s], 32 * (i + 1))
                xeT_done.now(pe, e, 2)
                for c in range(FC):
                    act_done.now(pe, e, c - 1) if c >= 2 else act_done.before(pe, e, FC - 1 + c)
                    for k in range(2):
                        ins = pe.matmul(ps_h[c % 2][:, k, 0:N2], wf[s][:, c * P:(c + 1) * P], xeT[s][:, k * N2:(k + 1) * N2],
                                        start=True, stop=True)
                    h_done.done(ins)
                if not last:
                    turn_rows(e + 1, 1 - s, i + s)
                y_out.before(pe, e, ST + 1)
                for t in range(ST):
                    for c in range(FC):
                        if t == 0:
                            act_done.now(pe, e, c + 1)
                        ins = pe.matmul(ps_y[:, t // NT, (t % NT) * P:(t % NT) * P + P], hT[:, c, t * P:(t + 1) * P],
                                        wp[s][:, c, :], start=(c == 0), stop=(c == FC - 1))
                y_done.done(ins)

            turn_rows(0, 0, 0)
            turns(pe, expert)

        @block.scalar
        def _(act):
            for c in (act_done,):
                c.credit(act)

            def expert(e, s, i, last=False):
                for c in range(FC):
                    h_done.now(act, e, c + 1)
                    if c == 0:
                        y_done.before(act, e, 1)
                    act_done.done(act.activation(hT[:, c, :].rearrange("p (k n) -> p k n", k=2), ps_h[c % 2][:, :, 0:N2], ACT.Gelu))

            turns(act, expert)

        @block.vector
        def _(dve):
            for c in (xeT_done, y_out):
                c.credit(dve)

            def rows(e, s):
                turned.now(dve, e, 1)
                xeT_done.done(dve.tensor_copy(xeT[s][:, 0:T], ps_x[:, 0, :]))
                xeT_done.done(dve.tensor_copy(xeT[s][:, T:CAP], ps_x[:, 1, 0:CAP - T]))

            def expert(e, s, i, last=False):
                if not last:
                    rows(e + 1, 1 - s)
                y_done.now(dve, e, 1)
                y_kept.before(dve, e, 1, 2)
                y_out.done(dve.tensor_copy(to[s][:], xe[s][:, :, D + 1:ROW].bitcast(U32).rearrange("p n a -> p (n a)")))
                for t in range(ST):
                    y_out.done(dve.tensor_scalar(ye[s][:, t, :], ps_y[:, t // NT, (t % NT) * P:(t % NT) * P + P],
                                                 xe[s][:, t, D:D + 1], None, ALU.mult))

            rows(0, 0)
            turns(dve, expert)


def combine_stage(nc, C, out):
    GROUPS = 2
    BG, TG = B // GROUPS, TILES // GROUPS
    with ExitStack() as ctx:
        m = Mem(nc, ctx)
        got = m.sb("got", [P, 2, TILES, D])
        both = m.sb("both", [P, TILES, D])
        y = m.sb("yf", [P, TILES, D])
        z = m.sb("zf", [P, TILES, D])
        norm = Norm(m, "x3", TG)
        loaded = [m.sem(f"got{b}") for b in range(B)]
        both_done = m.sem("both_done")
        y_done = Count(m.sem("yf_done"), BG)
        step = Count(m.sem("stepf"), norm_steps(TG))
        held = m.sem("heldf")
        z_done = Count(m.sem("z_done"), TG)
        stored = m.sem("storedf")
        block = ctx.enter_context(nc.Block())

        def load(eng, k):
            for b in range(B):
                eng.dma_start(got[:, k, b * NT:(b + 1) * NT, :],
                              C["yrows"][(k * B + b) * T:(k * B + b + 1) * T, :].rearrange("(n p) d -> p n d", p=P)
                              ).then_inc(loaded[b], 16)

        @block.sync
        def _(sp):
            load(sp, 0)
            for b in range(B):
                z_done.now(sp, b // BG, NT * (b % BG + 1))
                sp.dma_start(out[b].rearrange("(n p) d -> p n d", p=P), z[:, b * NT:(b + 1) * NT, :]).then_inc(stored, 16)
            sp.wait_ge(stored, 16 * B)

        @block.scalar
        def _(act):
            load(act, 1)

        @block.gpsimd
        def _(pool):
            for b in range(B):
                pool.wait_ge(loaded[b], 32)
                tiles = slice(b * NT, (b + 1) * NT)
                pool.tensor_tensor(both[:, tiles, :], got[:, 0, tiles, :], got[:, 1, tiles, :], ALU.add).then_inc(both_done, 1)

        @block.vector
        def _(dve):
            for c in (y_done, step, z_done):
                c.credit(dve)
            for g in range(GROUPS):
                for b in range(g * BG, (g + 1) * BG):
                    tiles = slice(b * NT, (b + 1) * NT)
                    dve.wait_ge(both_done, b + 1)
                    y_done.done(dve.tensor_tensor(y[:, tiles, :], both[:, tiles, :], C["rows"][:, 0, tiles, 0:D], ALU.add))
                y_done.now(dve, g, BG)
                if g:
                    z_done.before(dve, g, TG)
                rows = [y[:, t, :] for t in range(g * TG, (g + 1) * TG)]
                norm.moments(dve, g, step, held, rows)
                norm.roots(dve, g, step)
                norm.apply(dve, rows, [z[:, t, :] for t in range(g * TG, (g + 1) * TG)], z_done)


def common(m):
    C = {}
    C["ident"] = m.sb("ident", [P, P])
    C["ident_b"] = m.sb("ident_b", [P, P], BF16)
    C["mask"] = m.sb("mask", [P, P], BF16)
    C["maskT"] = m.sb("maskT", [P, P], BF16)
    C["ones"] = m.sb("ones", [P, P])
    C["upper"] = m.sb("upper", [P, P])
    C["gb"] = m.sb("gb", [P, 4])
    C["wg"] = m.sb("wg", [P, E])
    C["expert_u"] = m.sb("expert_u", [P, E], U32)
    C["expert"] = m.sb("expert", [P, E])
    C["x1all"] = m.sb("x1all", [P, B, NT, D])
    C["kv_hi"], C["kv_lo"] = m.split("kvall", [P, B, KEYS_E])
    return C


def self_common(m, C):
    C["aq_hi"], C["aq_lo"] = m.split("aq", [P, HS, P])
    C["wk_hi"], C["wk_lo"] = m.split("wk", [P, KVS, P])
    C["wv_hi"], C["wv_lo"] = m.split("wv", [P, HX * DH])
    C["wvd"] = m.sb("wvd", [P, KVS * DL])
    C["bo"] = m.sb("bo", [P, KVS, D])
    C["xall"] = m.sb("xall", [P, TILES, D])
    C["stage_hi"], C["stage_lo"] = m.split("stage", [P, 2, HX, DH])
    C["zero"] = m.sb("zero", [P, 8, P])
    C["empty"] = m.sb("empty", [P, ST, ROW])
    C["stored"] = m.sem("stored")
    C["xs"] = m.sb("xs", [P, NT, D])
    C["kop"] = m.sb("kop", [P, KVS, T], F32R)
    C["nmax"] = m.sb("nmax", [P, 2, NT, P])
    C["norm1"] = Norm(m, "x1", NT + 2, NT)
    C["kvT_hi"], C["kvT_lo"] = m.split("kvT", [P, KPAD])
    C["x_in"] = m.sem("x_in")
    C["zeroed"] = m.sem("zeroed")


def decoder(nc, I, out):
    with ExitStack() as ctx:
        m = Mem(nc, ctx)
        C = common(m)
        late_common(m, C)
        dram = lambda name, shape, dt=F32: nc.dram_tensor(name, shape, dt, kind="Internal").ap()
        C["xslots"] = dram("xslots", (SLOTS, ROW))
        C["yrows"] = dram("yrows", (2 * B * T, D))
        C["wpair"] = dram("wpair", (PAIRS, P, 2, 2, P), F32R)
        C["vals"] = dram("vals", (B, PAIRS, P, KC, P))
        with ExitStack() as early:
            self_common(Mem(nc, early), C)
            setup_stage(nc, I, C)
            self_stage(nc, I, C)
        with ExitStack() as late:
            m = Mem(nc, late)
            C["oall"] = m.sb("oall", [P, STEPS, T])
            C["wout"] = m.sb("wout", [P, PAIRS, D])
            C["wout_in"] = m.sem("wout_in")
            cross_stage(nc, I, C)
            C["rows"] = m.sb("rows", [P, 2, TILES, ROW])
            for name, shape in (("xe", [P, ST, ROW]), ("wf", [P, FF]), ("wp", [P, FC, D])):
                C[name] = [m.sb(f"{name}{s}", shape) for s in range(2)]
            C["xe_in"] = [m.sem(f"xe_in{s}") for s in range(2)]
            C["we_in"] = [m.sem(f"we_in{s}") for s in range(2)]
            close_stage(nc, I, C)
            expert_stage(nc, I, C)
            combine_stage(nc, C, out)


def late_common(m, C):
    C["topi"] = m.sb("topi", [P, TILES, 2])
    C["second"] = m.sb("second", [P, TILES, E])
    C["rank"] = m.sb("rank", [P, TILES, 2])
    C["slot"] = m.sb("slot", [P, 2, TILES], U32)


INPUTS = {"x": "x", "ctx_1024": "ctx", "L0_attn_wq": "wq", "L0_attn_wk_down": "wk_down", "L0_attn_wv_down": "wv_down",
          "L0_attn_wk_up": "wk_up", "L0_attn_wv_up": "wv_up", "L0_attn_wo": "wo", "L0_xattn_ln_m_g": "ln_m_g",
          "L0_xattn_ln_m_b": "ln_m_b", "L0_xattn_ln_l_g": "ln_l_g", "L0_xattn_ln_l_b": "ln_l_b", "L0_xattn_Wq": "Wq",
          "L0_xattn_Wkv": "Wkv", "L0_xattn_Wout": "Wout", "L0_ffn_w_g": "w_g", "L0_ffn_c_fc": "c_fc",
          "L0_ffn_c_proj": "c_proj"}


def kernel(**inputs):
    import numpy as np
    import concourse.bacc as bacc
    from concourse import mybir as mb
    from concourse.bass_utils import run_bass_kernel_spmd

    nc = bacc.Bacc("TRN2", target_bir_lowering=False, num_devices=1)
    arrays, I = {}, {}
    for name, short in INPUTS.items():
        a = np.ascontiguousarray(inputs[name])
        arrays[f"in_{name}"] = a
        I[short] = nc.dram_tensor(f"in_{name}", a.shape, mb.dt.from_np(a.dtype), kind="ExternalInput").ap()
    out = nc.dram_tensor("out_0", (B, T, D), F32, kind="ExternalOutput").ap()
    decoder(nc, I, out)
    return run_bass_kernel_spmd(nc, [arrays], core_ids=[0]).results[0]["out_0"]
```
